# Optimizing a Trainium2 kernel written in Bass

```python
import numpy as np
import jax
import jax.numpy as jnp

def _softmax(x, axis=-1):
    return jax.nn.softmax(x, axis=axis)

def _gelu(x):
    return jax.nn.gelu(x, approximate=True)

def _silu(x):
    return jax.nn.silu(x)

def _sigmoid(x):
    return jax.nn.sigmoid(x)

def _layernorm(x, axis=-1, eps=1e-05):
    m = jnp.mean(x, axis=axis, keepdims=True)
    v = jnp.var(x, axis=axis, keepdims=True)
    return (x - m) / jnp.sqrt(v + eps)

def _scatter_add(tgt, idx, src, axis=0):
    return tgt.at[idx].add(src)

def _segment_sum(src, seg, n):
    return jax.ops.segment_sum(src, seg, n)
kernel_name = 'mk_gnn_preln_d4_gnn_r64_ec57a3'

def setup_inputs(seed: int=0):
    np.random.seed(seed)
    _w = jnp.asarray

    def _rec_inputs():
        import jax
        import jax.numpy as jnp
        _gk = jax.random.key(seed)
        x = -0.0003713 + 1 * jax.random.normal(jax.random.fold_in(_gk, 1), (100000, 128), jnp.float32)
        src = jax.random.randint(jax.random.fold_in(_gk, 2), (25000,), 0, 100000, jnp.int32)
        dst = jnp.minimum((100000 * jax.random.uniform(jax.random.fold_in(_gk, 3), (25000,)) ** 2.0).astype(jnp.int32), 99999)
        _o = jnp.argsort(dst, stable=True)
        src = src[_o]
        dst = dst[_o]
        node_vec = jax.random.uniform(jax.random.fold_in(_gk, 13), (100000,), jnp.float32, 0.0, 36)
        return (x, src, dst, node_vec)
    x, src, dst, node_vec = _rec_inputs()

    def _L0_gnn_setup():
        import jax, jax.numpy as jnp
        import numpy as np
        N = 100000
        E = 25000
        D_IN = 128
        D_OUT = 128
        LN_EPS = 1e-05

        def mean_agg(x, src, dst, deg):
            summed = jax.ops.segment_sum(x[src], dst, num_segments=N)
            return summed / deg[:, None]
        key = jax.random.key(seed)
        ks = jax.random.split(key, 8)
        h = jax.random.normal(ks[0], (N, D_IN), dtype=jnp.float32)
        edge_index_mp = jax.random.randint(ks[1], (2, E), 0, N, dtype=jnp.int64)
        deg_mp = jax.ops.segment_sum(jnp.ones((E,), jnp.float32), edge_index_mp[1], num_segments=N)
        deg_mp = jnp.maximum(deg_mp, 1.0)
        scale = 1.0 / np.sqrt(D_IN)
        W_self = jax.random.uniform(ks[2], (D_OUT, D_IN), jnp.float32, -scale, scale)
        W_nb1 = jax.random.uniform(ks[3], (D_OUT, D_IN), jnp.float32, -scale, scale)
        W_hp = jax.random.uniform(ks[4], (D_OUT, D_IN), jnp.float32, -scale, scale)
        W_nb2 = jax.random.uniform(ks[5], (D_OUT, D_IN), jnp.float32, -scale, scale)
        bias = jnp.zeros((D_OUT,), jnp.float32)
        branch_logits = jnp.zeros((4,), jnp.float32)
        ln_gamma = jnp.ones((D_OUT,), jnp.float32)
        ln_beta = jnp.zeros((D_OUT,), jnp.float32)
        return {'h': h, 'edge_index_mp': edge_index_mp, 'deg_mp': deg_mp, 'W_self': W_self, 'W_nb1': W_nb1, 'W_hp': W_hp, 'W_nb2': W_nb2, 'bias': bias, 'branch_logits': branch_logits, 'ln_gamma': ln_gamma, 'ln_beta': ln_beta}
    _L0_gnn_all = _L0_gnn_setup()
    _L0_gnn_in = {k: v for k, v in _L0_gnn_all.items() if k in ('W_self', 'W_nb1', 'W_hp', 'W_nb2', 'bias', 'branch_logits', 'ln_gamma', 'ln_beta')}
    del _L0_gnn_all

    def _L1_gnn_setup():
        import jax, jax.numpy as jnp
        import numpy as np
        N_NODES = 50000
        N_EDGES = 9375
        FEAT = 128
        N_LAYERS = 4

        def _edgeconv(x, src, dst, tw, tb, pw, pb):
            phi = x @ pw.T + pb
            diff = x[src] - x[dst]
            msg = diff @ tw.T + tb + phi[dst]
            agg = jax.ops.segment_max(msg, dst, num_segments=x.shape[0])
            return jnp.where(jnp.isneginf(agg), jnp.zeros_like(agg), agg)
        key = jax.random.key(seed)
        ks = jax.random.split(key, 7)
        feats = jax.random.normal(ks[0], (N_NODES, FEAT), dtype=jnp.float32)
        src = jax.random.randint(ks[1], (N_EDGES,), 0, N_NODES)
        dst = jax.random.randint(ks[2], (N_EDGES,), 0, N_NODES)
        s = 1.0 / np.sqrt(FEAT)
        theta_w = jax.random.uniform(ks[3], (N_LAYERS, FEAT, FEAT), jnp.float32, -s, s)
        theta_b = jax.random.uniform(ks[4], (N_LAYERS, FEAT), jnp.float32, -s, s)
        phi_w = jax.random.uniform(ks[5], (N_LAYERS, FEAT, FEAT), jnp.float32, -s, s)
        phi_b = jax.random.uniform(ks[6], (N_LAYERS, FEAT), jnp.float32, -s, s)
        return {'feats': feats, 'src': src, 'dst': dst, 'theta_w': theta_w, 'theta_b': theta_b, 'phi_w': phi_w, 'phi_b': phi_b}
    _L1_gnn_all = _L1_gnn_setup()
    _L1_gnn_in = {k: v for k, v in _L1_gnn_all.items() if k in ('theta_w', 'theta_b', 'phi_w', 'phi_b')}
    del _L1_gnn_all

    def _L2_gnn_setup():
        import jax, jax.numpy as jnp
        import numpy as np
        N_NODES = 100000
        N_EDGES = 25000
        D_IN = 128
        D_OUT = 128
        key = jax.random.key(seed)
        k1, k2, k3, k4, k5 = jax.random.split(key, 5)
        x = jax.random.normal(k1, (N_NODES, D_IN), dtype=jnp.float32)
        edge_index = jax.random.randint(k2, (2, N_EDGES), 0, N_NODES, dtype=jnp.int64)
        W = jax.random.normal(k3, (D_IN, D_OUT), dtype=jnp.float32) * (1.0 / np.sqrt(D_IN))
        b = jax.random.normal(k4, (D_OUT,), dtype=jnp.float32) * 0.01
        return {'x': x, 'edge_index': edge_index, 'W': W, 'b': b}
    _L2_gnn_all = _L2_gnn_setup()
    _L2_gnn_in = {k: v for k, v in _L2_gnn_all.items() if k in ('W', 'b')}
    del _L2_gnn_all

    def _L3_gnn_setup():
        import jax, jax.numpy as jnp
        import numpy as np
        N_NODES = 100000
        N_EDGES = 25000
        DIM = 128
        HEADS = 8
        PHC = DIM // HEADS
        key = jax.random.key(seed)
        k1, k2, k3, k4, k5 = jax.random.split(key, 5)
        nodes = jax.random.normal(k1, (N_NODES, DIM), dtype=jnp.float32)
        senders = jax.random.randint(k2, (N_EDGES,), 0, N_NODES, dtype=jnp.int32)
        receivers = jax.random.randint(k3, (N_EDGES,), 0, N_NODES, dtype=jnp.int32)
        lim_w = np.sqrt(3.0 / DIM)
        W = jax.random.uniform(k4, (DIM, DIM), minval=-lim_w, maxval=lim_w, dtype=jnp.float32)
        b = jnp.zeros((DIM,), dtype=jnp.float32)
        lim_a = np.sqrt(3.0 * 2.0 / (2 * PHC + 1))
        attn_w = jax.random.uniform(k5, (2 * PHC, 1), minval=-lim_a, maxval=lim_a, dtype=jnp.float32)
        attn_b = jnp.zeros((1,), dtype=jnp.float32)
        return {'nodes': nodes, 'senders': senders, 'receivers': receivers, 'W': W, 'b': b, 'attn_w': attn_w, 'attn_b': attn_b}
    _L3_gnn_all = _L3_gnn_setup()
    _L3_gnn_in = {k: v for k, v in _L3_gnn_all.items() if k in ('W', 'b', 'attn_w', 'attn_b')}
    del _L3_gnn_all
    return {'x': x, 'src': src, 'dst': dst, 'node_vec': node_vec, 'L0_gnn_W_self': _L0_gnn_in['W_self'], 'L0_gnn_W_nb1': _L0_gnn_in['W_nb1'], 'L0_gnn_W_hp': _L0_gnn_in['W_hp'], 'L0_gnn_W_nb2': _L0_gnn_in['W_nb2'], 'L0_gnn_bias': _L0_gnn_in['bias'], 'L0_gnn_branch_logits': _L0_gnn_in['branch_logits'], 'L0_gnn_ln_gamma': _L0_gnn_in['ln_gamma'], 'L0_gnn_ln_beta': _L0_gnn_in['ln_beta'], 'L1_gnn_theta_w': _L1_gnn_in['theta_w'], 'L1_gnn_theta_b': _L1_gnn_in['theta_b'], 'L1_gnn_phi_w': _L1_gnn_in['phi_w'], 'L1_gnn_phi_b': _L1_gnn_in['phi_b'], 'L2_gnn_W': _L2_gnn_in['W'], 'L2_gnn_b': _L2_gnn_in['b'], 'L3_gnn_W': _L3_gnn_in['W'], 'L3_gnn_b': _L3_gnn_in['b'], 'L3_gnn_attn_w': _L3_gnn_in['attn_w'], 'L3_gnn_attn_b': _L3_gnn_in['attn_b']}

def reference(x, src, dst, node_vec, L0_gnn_W_self, L0_gnn_W_nb1, L0_gnn_W_hp, L0_gnn_W_nb2, L0_gnn_bias, L0_gnn_branch_logits, L0_gnn_ln_gamma, L0_gnn_ln_beta, L1_gnn_theta_w, L1_gnn_theta_b, L1_gnn_phi_w, L1_gnn_phi_b, L2_gnn_W, L2_gnn_b, L3_gnn_W, L3_gnn_b, L3_gnn_attn_w, L3_gnn_attn_b):
    import jax
    import jax.numpy as jnp

    def _L0_gnn_ref(h, edge_index_mp, deg_mp, W_self, W_nb1, W_hp, W_nb2, bias, branch_logits, ln_gamma, ln_beta):
        import jax, jax.numpy as jnp
        import numpy as np
        N = 100000
        E = 25000
        D_IN = 128
        D_OUT = 128
        LN_EPS = 1e-05

        def mean_agg(x, src, dst, deg):
            summed = jax.ops.segment_sum(x[src], dst, num_segments=N)
            return summed / deg[:, None]
        src, dst = (edge_index_mp[0], edge_index_mp[1])
        nb1 = mean_agg(h, src, dst, deg_mp)
        nb2 = mean_agg(nb1, src, dst, deg_mp)
        hp = h - nb1
        scales = 2.0 * jax.nn.sigmoid(branch_logits)
        z = scales[0] * (h @ W_self.T) + scales[1] * (nb1 @ W_nb1.T) + scales[2] * (hp @ W_hp.T) + scales[3] * (nb2 @ W_nb2.T) + bias
        mu = jnp.mean(z, axis=-1, keepdims=True)
        var = jnp.var(z, axis=-1, keepdims=True)
        return (z - mu) * jax.lax.rsqrt(var + LN_EPS) * ln_gamma + ln_beta

    def _L1_gnn_ref(feats, src, dst, theta_w, theta_b, phi_w, phi_b):
        import jax, jax.numpy as jnp
        import numpy as np
        N_NODES = 50000
        N_EDGES = 9375
        FEAT = 128
        N_LAYERS = 4

        def _edgeconv(x, src, dst, tw, tb, pw, pb):
            phi = x @ pw.T + pb
            diff = x[src] - x[dst]
            msg = diff @ tw.T + tb + phi[dst]
            agg = jax.ops.segment_max(msg, dst, num_segments=x.shape[0])
            return jnp.where(jnp.isneginf(agg), jnp.zeros_like(agg), agg)
        x = feats
        for l in range(N_LAYERS):
            x = _edgeconv(x, src, dst, theta_w[l], theta_b[l], phi_w[l], phi_b[l])
            x = jax.nn.relu(x)
        return x

    def _L2_gnn_ref(x, edge_index, W, b):
        import jax, jax.numpy as jnp
        import numpy as np
        N_NODES = 100000
        N_EDGES = 25000
        D_IN = 128
        D_OUT = 128
        'GCNConv forward: add self loops, symmetric deg normalization,\n            linear transform, scatter-add aggregation at target nodes, add bias.'
        n = x.shape[0]
        loop = jnp.arange(n, dtype=edge_index.dtype)
        row = jnp.concatenate([edge_index[0], loop])
        col = jnp.concatenate([edge_index[1], loop])
        ew = jnp.ones(row.shape[0], dtype=x.dtype)
        deg = jax.ops.segment_sum(ew, col, num_segments=n)
        dinv = jnp.where(deg > 0, jax.lax.rsqrt(deg), 0.0).astype(x.dtype)
        norm = dinv[row] * dinv[col]
        h = x @ W
        msgs = norm[:, None] * h[row]
        out = jax.ops.segment_sum(msgs, col, num_segments=n)
        return out + b

    def _L3_gnn_ref(nodes, senders, receivers, W, b, attn_w, attn_b):
        import jax, jax.numpy as jnp
        import numpy as np
        N_NODES = 100000
        N_EDGES = 25000
        DIM = 128
        HEADS = 8
        PHC = DIM // HEADS
        n = nodes.shape[0]
        nt = (nodes @ W + b).reshape(n, HEADS, PHC)
        sent = nt[senders]
        recv = nt[receivers]
        qk = jax.nn.leaky_relu(jnp.concatenate([sent, recv], axis=-1), negative_slope=0.2)
        logits = qk @ attn_w + attn_b
        seg_max = jax.ops.segment_max(logits, receivers, num_segments=n)
        exp = jnp.exp(logits - seg_max[receivers])
        denom = jax.ops.segment_sum(exp, receivers, num_segments=n)
        alpha = exp / denom[receivers]
        out = jax.ops.segment_sum(sent * alpha, receivers, num_segments=n)
        return out.reshape(n, -1)
    edge_index = jnp.stack([src, dst])
    h = jnp.maximum(_layernorm(x, axis=-1), 0.0)
    x = x + _L0_gnn_ref(h, edge_index, node_vec, L0_gnn_W_self, L0_gnn_W_nb1, L0_gnn_W_hp, L0_gnn_W_nb2, L0_gnn_bias, L0_gnn_branch_logits, L0_gnn_ln_gamma, L0_gnn_ln_beta)
    h = jnp.maximum(_layernorm(x, axis=-1), 0.0)
    x = x + _L1_gnn_ref(h, src, dst, L1_gnn_theta_w, L1_gnn_theta_b, L1_gnn_phi_w, L1_gnn_phi_b)
    h = jnp.maximum(_layernorm(x, axis=-1), 0.0)
    x = x + _L2_gnn_ref(h, edge_index, L2_gnn_W, L2_gnn_b)
    h = jnp.maximum(_layernorm(x, axis=-1), 0.0)
    x = x + _L3_gnn_ref(h, src, dst, L3_gnn_W, L3_gnn_b, L3_gnn_attn_w, L3_gnn_attn_b)
    return x

_drawn_inputs = setup_inputs


def setup_inputs(seed=0):
    import zlib

    import numpy as np

    out = dict(_drawn_inputs(seed))
    spreads = {'L0_gnn_bias': (0.0, 0.1),
     'L0_gnn_branch_logits': (0.0, 0.751),
     'L0_gnn_ln_gamma': (1.0, 0.2),
     'L0_gnn_ln_beta': (0.0, 0.1),
     'L3_gnn_b': (0.0, 0.318)}
    factors = {'L0_gnn_W_nb2': 6.397,
     'L1_gnn_theta_b': 4.957,
     'L1_gnn_phi_w': 2.871,
     'L1_gnn_phi_b': 5.267,
     'L2_gnn_b': 8.0,
     'L3_gnn_attn_w': 4.974}
    for name, (base, spread) in spreads.items():
        noise = np.random.default_rng([zlib.crc32(name.encode()), seed]).standard_normal(out[name].shape)
        drawn = base * np.exp(spread * noise) if base else spread * noise
        out[name] = jnp.asarray(drawn.astype(out[name].dtype))
    for name, factor in factors.items():
        out[name] = (out[name] * factor).astype(out[name].dtype)
    return out
```

```python
from contextlib import ExitStack

import numpy as np
import concourse.bass as bass
from concourse import mybir

F32 = mybir.dt.float32
BF16 = mybir.dt.bfloat16
I32 = mybir.dt.int32
ALU = mybir.AluOpType
ACT = mybir.ActivationFunctionType
AX = mybir.AxisListType

NODES, EDGES, F = 100000, 25000, 128
LAYERS, HEADS = 4, 8
HC = F // HEADS
TPG = 4
GW = TPG * 128
U = 5
GROUPS = -(-EDGES // GW)
GROUPS += -GROUPS % U
SLOTS = GROUPS * GW
TILES = SLOTS // 128
RW = 2 * 128
RR = SLOTS // RW
NOWHERE = 1 << 20
NP = 125
NG = NP * TPG
NODE_GROUPS = NODES // NG
EARLY = 40
PT = 40
EPS = 1e-5
SLOPE = 0.2
NEG = 3.0e38
ds = bass.ds


def pipelined(eng, count, phases):
    deepest = max(lag for lag, _ in phases)
    head = U + -(-deepest // U) * U
    turns = (count - head) // U

    def static(n):
        for lag, phase in phases:
            if 0 <= n - lag < count:
                phase(n - lag, (n - lag) % U, (n - lag) // U)

    for n in range(head):
        static(n)
    if turns > 0:
        with eng.Fori(0, turns) as i:
            for k in range(U):
                for lag, phase in phases:
                    g = head + k - lag
                    phase(i * U + g, g % U, i + g // U)
    for n in range(head + turns * U, count + deepest):
        static(n)


class Signal:

    def __init__(self, semaphore, base):
        self.sem, self.base = semaphore, base


def reached(eng, signal, value):
    eng.wait_ge(signal.sem, value + signal.base)


def done(eng, signal, n):
    reached(eng, signal, n + 1)


def freed(eng, signal, n, depth):
    if isinstance(n, int) and n < depth:
        return
    reached(eng, signal, n - depth + 1)


def build(nc, x, src, dst, node_vec, w_self, w_nb1, w_hp, w_nb2, l0_bias, logits, gamma, beta,
          theta_w, theta_b, phi_w, phi_b, gcn_w, gcn_b, gat_w, gat_b, attn_w, attn_b, out):
    with ExitStack() as ctx:
        def sb(name, shape, dt=F32):
            return ctx.enter_context(nc.sbuf_tensor(name, shape, dt))

        def sem(name):
            return ctx.enter_context(nc.semaphore(name))

        def sems(name):
            return [sem(f"{name}{k}") for k in range(U)]

        def dram(name, shape, dt=F32):
            return nc.dram_tensor(name, shape, dt, kind="Internal").ap()

        dst_padded = dram("dst_padded", (1, SLOTS + 2), I32)
        flags_d = [dram(f"flags_{n}", (1, SLOTS), BF16) for n in range(4)]
        same_prev_d, neg_prev_d, same_next_d, neg_next_d = flags_d
        slot_of_node = dram("slot_of_node", (NODES, 1), I32)
        nb1_tab = dram("nb1_tab", (SLOTS + 1, F))
        sum1T_tab = dram("sum1T_tab", (F, SLOTS))
        h1_local = dram("h1_local", (SLOTS, F))
        x3_local = dram("x3_local", (SLOTS, F))
        x1_tab = dram("x1_tab", (SLOTS, F))
        y_tab = [dram(f"y_tab{n}", (SLOTS + (n > 0), F)) for n in range(LAYERS)]
        yT_tab = [dram(f"yT_tab{n}", (F, SLOTS)) for n in range(LAYERS)]
        x2_tab = dram("x2_tab", (SLOTS, F))
        g_tab = dram("g_tab", (SLOTS, F))
        x3_tab = dram("x3_tab", (SLOTS, F))
        x3_last_tab = dram("x3_last_tab", (SLOTS, F))

        def rows_of(tab, g):
            return tab[ds(g * GW, GW), :].rearrange("(j p) f -> p j f", p=128)

        def cols_of(tab, g):
            return tab[:, ds(g * GW, GW)]

        def flags_of(tab, g):
            return tab[0:1, ds(g * GW, GW)].partition_broadcast(128)

        ident = sb("ident", [128, 128])
        head_mask = sb("head_mask", [128, 128])
        ones = sb("ones", [128, GW])
        zeros = sb("zeros", [128, F])
        eps = sb("eps", [128, 1])
        gamma_b = sb("gamma_b", [128, F])
        beta_b = sb("beta_b", [128, F])
        gcn_b_b = sb("gcn_b_b", [128, F])
        l0_bias_r = sb("l0_bias_r", [1, 2 * F])
        wn = sb("wn", [128, 12, F])
        wc = sb("wc", [128, 3, F])
        wT = sb("wT", [128, 3, F])
        wz = sb("wz", [128, 2 * F])
        pt = sb("pt", [128, LAYERS, F])
        thetaT = sb("thetaT", [128, LAYERS, F])
        ptT = sb("ptT", [128, LAYERS, F])
        gcn_w_s = sb("gcn_w_s", [128, F])
        gat_w_s = sb("gat_w_s", [128, F])
        gat_b_c = sb("gat_b_c", [128, 1])
        attn_c = sb("attn_c", [128, 2])
        attn_b_c = sb("attn_b_c", [128, 1])
        attn_m = sb("attn_m", [128, 4, F])
        conv_b = sb("conv_b", [128, 2, LAYERS])
        conv_bias = sb("conv_bias", [128, LAYERS])
        scale_l = sb("scale_l", [128, 4])
        scale_s = sb("scale_s", [128, 4])
        scale_2 = sb("scale_2", [128, 6])
        small = sb("small", [128, 4])

        near_i = sb("near_i", [RR, 3, RW], I32)
        pad_i = sb("pad_i", [1, SLOTS - EDGES + 2], I32)
        far_i = sb("far_i", [NP, NODES // NP], I32)
        src_i = sb("src_i", [RR, RW], I32)
        last_i = sb("last_i", [128, TILES], I32)
        first_i = sb("first_i", [128, TILES], I32)
        dst_i = sb("dst_i", [128, TILES], I32)
        src_c = sb("src_c", [128, TILES], I32)
        slot_i = sb("slot_i", [128, TILES], I32)
        from_i = sb("from_i", [128, TILES], I32)
        is_last = sb("is_last", [128, TILES])
        deg = sb("deg", [128, TILES])
        rdeg = sb("rdeg", [128, TILES])
        count = sb("count", [128, TILES])
        dinv = sb("dinv", [128, TILES])
        now_i = sb("now_i", [128, PT], I32)
        now_v = sb("now_v", [128, PT], I32)
        got_v = sb("got_v", [128, PT])
        gi = sb("gi", [128, U, 2 * TPG], I32)

        units = sb("units", [128, 66, GW])
        near = units[0:RR, 0:2, :].rearrange("p a (b w) -> p (a b) w", w=RW)
        rowf = units[0:RR, 2:6, :].rearrange("p a (b w) -> p (a b) w", w=RW)
        flag_row = [units[0:RR, 6 + n, 0:RW // 2].bitcast(BF16) for n in range(4)]

        def ring(n):
            return [units[:, n * U + k, :] for k in range(U)]

        mask_a = sb("mask_a", [128, U, GW], BF16)
        mask_b = sb("mask_b", [128, U, GW], BF16)
        mx = sb("mx", [128, U, GW + 1])
        junk = sb("junk", [128, GW])
        st0 = sb("st0", [128, U, TPG, 6])
        st1 = sb("st1", [128, U, TPG, 6])
        mv0 = sb("mv0", [128, U, TPG, 2])
        mv1 = sb("mv1", [128, U, TPG, 2])
        sd0 = sb("sd0", [128, U, TPG])
        sd1 = sb("sd1", [128, U, TPG])
        sdz = sb("sdz", [128, U, TPG])
        rs0 = sb("rs0", [128, U, TPG])
        rs1 = sb("rs1", [128, U, TPG])
        rsz = sb("rsz", [128, U, TPG])
        ssq = sb("ssq", [128, U, TPG])
        rdg = sb("rdg", [128, U, TPG])

        bank = [ctx.enter_context(nc.psum_tensor(f"bank{n}", [128, GW], F32)) for n in range(6)]
        wide = ctx.enter_context(nc.psum_tensor("wide", [128, 2 * GW], F32))

        def by_tile(t):
            return t.rearrange("p (j f) -> p j f", j=TPG)

        s_const, s_w, s_pad, s_padded = sem("s_const"), sem("s_w"), sem("s_pad"), sem("s_padded")
        s_near, s_setup, s_rows, s_rowsT = sem("s_near"), sem("s_setup"), sem("s_rows"), sem("s_rowsT")
        s_flags, s_cols, s_act, s_step = sem("s_flags"), sem("s_cols"), sem("s_act"), sem("s_step")
        s_wc, s_wcT, s_wt = sem("s_wc"), sem("s_wcT"), sem("s_wt")
        s_far, s_init, s_placed, s_tails = sem("s_far"), sem("s_init"), sem("s_placed"), sem("s_tails")
        s_idx, s_deg, s_got, s_slot, s_from = sem("s_idx"), sem("s_deg"), sem("s_got"), sem("s_slot"), sem("s_from")
        s_degd, s_rdeg, s_stage, s_sd, s_dinv = sem("s_degd"), sem("s_rdeg"), sem("s_stage"), sem("s_sd"), sem("s_dinv")
        s_gate = {e: sem(f"s_gate_{e}") for e in ("dve", "pool", "sp")}

        def hold(eng, name):
            eng.sem_inc(s_gate[name], 1)

        raised = {}

        def signal(name, total=GROUPS):
            handle, base = raised.get(name) or (sem(name), 0)
            raised[name] = (handle, base + total)
            return Signal(handle, base)

        def signals(names, total=GROUPS):
            return [signal(name, total) for name in names.split()]

        def by_slot(name, per_group, groups=GROUPS):
            return [signal(f"{name}{k}", per_group * groups // U) for k in range(U)]

        RUN_A, RUN_S, RUN_B = (0, EARLY), (EARLY, GROUPS), (EARLY + GROUPS, NODE_GROUPS - EARLY)
        NODE_STEPS = GROUPS + NODE_GROUPS

        class Node:
            bn0, mv0, sd0, rs0, xn0, xb = signals("stats0 moments0 root0 scale0 normed0 x_beta", NODE_STEPS)
            t0, h0, z, ssq, sdz, rsz = signals("turned0 relu0 z z_squares z_root z_scale", NODE_STEPS)
            x1, bn1, mv1, sd1, rs1, xn1 = signals("x1 stats1 moments1 root1 scale1 normed1", NODE_STEPS)
            t1, h1, x3, xo = signals("turned1 relu1 gcn_product x_out", NODE_STEPS)
            idx, sum1, cnt, ts, nb = signals("indices source_sums edge_counts sums_turned means")
            load, store = by_slot("load", 16, NODE_GROUPS), by_slot("store", 16, NODE_STEPS)
            gather, mask = by_slot("gathered", 64), by_slot("flags", 16)
            h1_store, sum_store, nb_store = by_slot("h1_stored", 16), by_slot("sums_stored", 16), by_slot("means_stored", 16)

        X, XB, XN0, H0T, X1, XN1, H1T, XO = [ring(n) for n in range(8)]
        SUM1T, CNT, NBR = [ring(n) for n in range(8, 11)]

        def node_rows(tab, n):
            return tab[ds(n * NG, NG), :].rearrange("(p j) f -> p j f", j=TPG)

        class Dest:
            load, gather, store, idx = by_slot("load", 32), by_slot("gathered", 128), by_slot("store", 48), signal("indices", 2 * GROUPS)
            bn0, mv0, sd0, rs0, xn0, xb = signals("stats0 moments0 root0 scale0 normed0 x_beta")
            tn, sum2, t0, h0, z, zs, zm = signals("means_turned second_sums turned0 relu0 z z_mean z_whole")
            ssq, sdz, rsz, w = signals("z_squares z_root z_scale z_normed")
            x1, bn1, mv1, sd1, rs1, xn1, t1, h1 = signals("x1 stats1 moments1 root1 scale1 normed1 turned1 relu1")

        NBG, XD, S1L, XBD, XN0D, H0D, S2T, ZS, ZM, X1D, XN1D, H1D = [ring(n) for n in range(12)]

        class Conv:
            fill, load, x1_load = by_slot("flags", 16), by_slot("load", 32, LAYERS * GROUPS), by_slot("h1_stored", 16)
            gather, store, idx = by_slot("gathered", 64, LAYERS * GROUPS), by_slot("store", 32, LAYERS * GROUPS), signal("indices", LAYERS * GROUPS)
            ty, yt, m1, m2, scan, add, yn, tb = signals("turned0 relu0 messages own_term scanned agg y y_turned", LAYERS * GROUPS)
            ye = signal("y_rows", (LAYERS - 1) * GROUPS)
            x2, bn, mv, sd, rs, xn, g = signals("x2 stats0 moments0 root0 scale0 normed0 g_rows")

        YG, YL, YT, SC, AD, YN, YE, X1L, X2, XN2, G2 = [ring(n) for n in range(11)]

        class Gcn:
            fill, load, gather, store = by_slot("flags", 16), by_slot("load", 48), by_slot("gathered", 64), by_slot("store", 32)
            idx, tg, gt, scan, u, w, xb, x3, x3m, td = signals("indices turned0 relu0 scanned with_own gcn_product x_beta x3 x3_last own_turned")

        GG, GD, X2L, GTs, SG, UG, XB2, X3, X3M = [ring(n) for n in range(9)]

        class Gat:
            fill, load, neg_load = by_slot("flags", 16), by_slot("load", 32), by_slot("h1_stored", 16)
            gather, scatter, idx = by_slot("gathered", 64), by_slot("scattered", 64), signal("indices")
            bns, mvs, sds, rss, xns, ts, hs = signals("stats0 moments0 root0 scale0 normed0 turned0 relu0")
            bnd, mvd, sdd, rsd, xnd, td, hd = signals("stats1 moments1 root1 scale1 normed1 turned1 relu1")
            ws, nt, lks, wd, lkd, lg, lgs = signals("nt_source nt_kept leaky_source nt_dest leaky_dest logits_sum logits")
            tx, xscan, txb = signals("last_turned x3_spread x3_rows")
            mscan, diff, drop, sub, ec, ep = signals("max_scanned max_diff max_drop exponent decay weight")
            den, pn, num, rden, ratio = signals("denominator weighted numerator denominator_inverse attended")
            ot, tf, oe, out_idx = signals("out_cols out_turned out_rows out_indices")

        XS, XM, NTS, LKS, X3T, LGS, CE, PE_, DEN, NUM, OE = [ring(n) for n in range(11)]
        XNS, HST, XND, HDT, NTD, LKD, PN, OT = [units[:, 55 + n, :] for n in range(8)]
        MX = [mx[:, k, :] for k in range(U)]

        def stats(dve, source, st, mv, s_bn, s_mv, n, P):
            for j in range(TPG):
                last = dve.bn_stats(st[:P, j, :], source[:P, j * F:(j + 1) * F])
            last.then_inc(s_bn.sem, 1)
            done(dve, s_bn, n)
            hold(dve, "dve")
            for j in range(TPG):
                last = dve.bn_aggr(mv[:P, j, :], st[:P, j, :])
            last.then_inc(s_mv.sem, 1)

        def normalise(dve, result, source, mv, sd, rs, s_sd_, s_rs, s_xn, n, P):
            done(dve, s_sd_, n)
            dve.reciprocal(rs[:P, :], sd[:P, :]).then_inc(s_rs.sem, 1)
            done(dve, s_rs, n)
            for j in range(TPG):
                last = dve.tensor_scalar(result[:P, j * F:(j + 1) * F], source[:P, j * F:(j + 1) * F],
                                         mv[:P, j, 0:1], rs[:P, j:j + 1], ALU.subtract, ALU.mult)
            last.then_inc(s_xn.sem, 1)

        def turn(pe, result, source, P=128):
            for j in range(TPG):
                last = pe.transpose(result[:, j * 128:j * 128 + P], source[:P, j * 128:(j + 1) * 128], ident[:P, :P])
            return last

        block = ctx.enter_context(nc.Block())

        @block.sync
        def _(sp):
            sp.wait_ge(s_pad, 2)
            sp.dma_start(dst_padded[0:1, 0:1], pad_i[0:1, 0:1]).then_inc(s_padded, 16)
            sp.dma_start(dst_padded[0:1, 1 + EDGES:], pad_i[0:1, 1:]).then_inc(s_padded, 16)
            sp.dma_start(dst_padded[0:1, 1:1 + EDGES], dst.unsqueeze(0)).then_inc(s_padded, 16)
            full = EDGES // RW
            sp.dma_start(src_i[0:full, :], src[0:full * RW].rearrange("(p w) -> p w", w=RW)).then_inc(s_near, 16)
            sp.dma_start(src_i[full:full + 1, 0:EDGES - full * RW], src[full * RW:EDGES].unsqueeze(0)).then_inc(s_near, 16)
            sp.wait_ge(s_padded, 48)
            for n in range(3):
                sp.dma_start(near_i[:, n, :], dst_padded[0, n:n + SLOTS].rearrange("(p w) -> p w", w=RW)).then_inc(s_near, 16)
            for n, w in enumerate((w_self, w_nb1, w_hp, w_nb2)):
                sp.dma_start(wn[:, n, :], w).then_inc(s_w, 16)
            sp.dma_start(wn[:, 4:8, :], theta_w.rearrange("l o i -> o l i")).then_inc(s_w, 16)
            sp.dma_start(wn[:, 8:12, :], phi_w.rearrange("l o i -> o l i")).then_inc(s_w, 16)
            sp.dma_start(gcn_w_s[:, :], gcn_w).then_inc(s_w, 16)
            sp.dma_start(gat_w_s[:, :], gat_w).then_inc(s_w, 16)
            sp.dma_start(gamma_b[:, :], gamma.unsqueeze(0).partition_broadcast(128)).then_inc(s_w, 16)
            sp.dma_start(beta_b[:, :], beta.unsqueeze(0).partition_broadcast(128)).then_inc(s_w, 16)
            sp.dma_start(gcn_b_b[:, :], gcn_b.unsqueeze(0).partition_broadcast(128)).then_inc(s_w, 16)
            sp.dma_start(l0_bias_r[0:1, 0:F], l0_bias.unsqueeze(0)).then_inc(s_w, 16)
            sp.dma_start(scale_l[:, :], logits.unsqueeze(0).partition_broadcast(128)).then_inc(s_w, 16)
            sp.dma_start(attn_b_c[:, :], attn_b.unsqueeze(0).partition_broadcast(128)).then_inc(s_w, 16)
            sp.dma_start(gat_b_c[:, :], gat_b.unsqueeze(1)).then_inc(s_w, 16)
            for l in range(LAYERS):
                sp.dma_start(conv_b[:, 0, l:l + 1], theta_b[l, :].unsqueeze(1)).then_inc(s_w, 16)
                sp.dma_start(conv_b[:, 1, l:l + 1], phi_b[l, :].unsqueeze(1)).then_inc(s_w, 16)
            for h in range(HEADS):
                for n in range(2):
                    sp.dma_start(attn_c[h * HC:(h + 1) * HC, n:n + 1], attn_w[n * HC:(n + 1) * HC, :]).then_inc(s_w, 16)
            sp.wait_ge(s_const, 5)
            for tab in (nb1_tab, y_tab[1], y_tab[2], y_tab[3]):
                sp.dma_start(tab[SLOTS:SLOTS + 1, :], zeros[0:1, :]).then_inc(s_tails, 16)
            sp.wait_ge(s_far, 1)
            sp.dma_start(slot_of_node.rearrange("(p a) o -> p (a o)", p=NP), far_i[:, :]).then_inc(s_init, 16)
            sp.wait_ge(s_rows, 1)
            for tab, row in zip(flags_d, flag_row):
                sp.dma_start(tab[0, :].rearrange("(p w) -> p w", w=RW), row).then_inc(s_flags, 16)
            sp.wait_ge(s_flags, 64)
            sp.wait_ge(s_cols, 1)

            def node_load(base, first):
                def phase(g, s, q):
                    n = base + g
                    freed(sp, Node.x1, n, U)
                    hold(sp, "sp")
                    sp.dma_start(by_tile(X[s])[:NP], node_rows(x, first + g)).then_inc(Node.load[s].sem, 16)
                return phase

            def node_store(base, first):
                def phase(g, s, q):
                    done(sp, Node.xo, base + g)
                    hold(sp, "sp")
                    sp.dma_start(node_rows(out, first + g), by_tile(XO[s])[:NP]).then_inc(Node.store[s].sem, 16)
                return phase

            def source_flags(g, s, q):
                freed(sp, Node.cnt, g, U)
                hold(sp, "sp")
                sp.dma_start(mask_a[:, s, :], flags_of(same_prev_d, g)).then_inc(Node.mask[s].sem, 16)

            def source_store(g, s, q):
                n = RUN_S[0] + g
                done(sp, Node.sum1, g)
                hold(sp, "sp")
                sp.dma_start(cols_of(sum1T_tab, g), SUM1T[s]).then_inc(Node.sum_store[s].sem, 16)
                done(sp, Node.nb, g)
                hold(sp, "sp")
                sp.dma_start(rows_of(nb1_tab, g), by_tile(NBR[s])).then_inc(Node.nb_store[s].sem, 16)
                done(sp, Node.xn1, n)
                hold(sp, "sp")
                sp.dma_start(rows_of(h1_local, g), by_tile(XN1[s])).then_inc(Node.h1_store[s].sem, 16)
                done(sp, Node.xo, n)
                hold(sp, "sp")
                sp.dma_start(rows_of(x3_local, g), by_tile(XO[s])).then_inc(Node.store[s].sem, 16)

            pipelined(sp, RUN_A[1], [(0, node_load(RUN_A[0], 0)), (6, node_store(RUN_A[0], 0))])
            pipelined(sp, GROUPS, [(0, source_flags), (4, source_store)])
            pipelined(sp, RUN_B[1], [(0, node_load(RUN_B[0], EARLY)), (6, node_store(RUN_B[0], EARLY))])
            for k in range(U):
                reached(sp, Node.store[k], 16 * (NODE_STEPS // U))
                reached(sp, Node.sum_store[k], 16 * (GROUPS // U))
                reached(sp, Node.nb_store[k], 16 * (GROUPS // U))
                reached(sp, Node.h1_store[k], 16 * (GROUPS // U))
            sp.wait_ge(s_tails, 64)
            sp.wait_ge(s_dinv, 1)
            sp.sem_inc(s_stage, 1)

            def dest_load(g, s, q):
                freed(sp, Dest.sum2, g, U)
                hold(sp, "sp")
                sp.dma_start(mask_a[:, s, :], flags_of(same_prev_d, g)).then_inc(Dest.load[s].sem, 16)
                freed(sp, Dest.z, g, U)
                hold(sp, "sp")
                sp.dma_start(S1L[s], cols_of(sum1T_tab, g)).then_inc(Dest.load[s].sem, 16)

            def dest_store(g, s, q):
                done(sp, Dest.x1, g)
                hold(sp, "sp")
                sp.dma_start(rows_of(x1_tab, g), by_tile(X1D[s])).then_inc(Dest.store[s].sem, 16)
                done(sp, Dest.xn1, g)
                hold(sp, "sp")
                sp.dma_start(rows_of(y_tab[0], g), by_tile(XN1D[s])).then_inc(Dest.store[s].sem, 16)
                done(sp, Dest.h1, g)
                hold(sp, "sp")
                sp.dma_start(cols_of(yT_tab[0], g), H1D[s]).then_inc(Dest.store[s].sem, 16)

            pipelined(sp, GROUPS, [(0, dest_load), (5, dest_store)])
            for k in range(U):
                reached(sp, Dest.store[k], 48 * (GROUPS // U))
            sp.sem_inc(s_stage, 1)

            for l in range(LAYERS):
                def conv_load(g, s, q, l=l):
                    n = l * GROUPS + g
                    if l == 0:
                        freed(sp, Conv.ty, n, U)
                        hold(sp, "sp")
                        sp.dma_start(by_tile(YG[s]), rows_of(h1_local, g)).then_inc(Conv.fill[s].sem, 16)
                    freed(sp, Conv.scan, n, U)
                    hold(sp, "sp")
                    sp.dma_start(mask_a[:, s, :], flags_of(neg_prev_d, g)).then_inc(Conv.load[s].sem, 16)
                    freed(sp, Conv.m2, n, U)
                    hold(sp, "sp")
                    sp.dma_start(YL[s], cols_of(yT_tab[l], g)).then_inc(Conv.load[s].sem, 16)
                    if l == LAYERS - 1:
                        if not isinstance(g, int) or g >= U:
                            freed(sp, Conv.x2, g, U)
                        hold(sp, "sp")
                        sp.dma_start(by_tile(X1L[s]), rows_of(x1_tab, g)).then_inc(Conv.x1_load[s].sem, 16)

                def conv_store(g, s, q, l=l):
                    n = l * GROUPS + g
                    if l < LAYERS - 1:
                        done(sp, Conv.yn, n)
                        hold(sp, "sp")
                        sp.dma_start(cols_of(yT_tab[l + 1], g), YN[s]).then_inc(Conv.store[s].sem, 16)
                        done(sp, Conv.ye, n)
                        hold(sp, "sp")
                        sp.dma_start(rows_of(y_tab[l + 1], g), by_tile(YE[s])).then_inc(Conv.store[s].sem, 16)
                    else:
                        done(sp, Conv.x2, g)
                        hold(sp, "sp")
                        sp.dma_start(rows_of(x2_tab, g), by_tile(X2[s])).then_inc(Conv.store[s].sem, 16)
                        done(sp, Conv.g, g)
                        hold(sp, "sp")
                        sp.dma_start(rows_of(g_tab, g), by_tile(G2[s])).then_inc(Conv.store[s].sem, 16)

                pipelined(sp, GROUPS, [(0, conv_load), (4, conv_store)])
                for k in range(U):
                    reached(sp, Conv.store[k], 32 * (l + 1) * (GROUPS // U))
                sp.sem_inc(s_stage, 1)

            def gcn_load(g, s, q):
                freed(sp, Gcn.tg, g, U)
                hold(sp, "sp")
                sp.dma_start(by_tile(GG[s]), rows_of(h1_local, g)).then_inc(Gcn.fill[s].sem, 16)
                sp.dma_start(by_tile(GD[s]), rows_of(g_tab, g)).then_inc(Gcn.load[s].sem, 16)
                freed(sp, Gcn.scan, g, U)
                hold(sp, "sp")
                sp.dma_start(mask_a[:, s, :], flags_of(same_prev_d, g)).then_inc(Gcn.load[s].sem, 16)
                freed(sp, Gcn.xb, g, U)
                hold(sp, "sp")
                sp.dma_start(by_tile(X2L[s]), rows_of(x2_tab, g)).then_inc(Gcn.load[s].sem, 16)

            def gcn_store(g, s, q):
                done(sp, Gcn.x3, g)
                hold(sp, "sp")
                sp.dma_start(rows_of(x3_tab, g), by_tile(X3[s])).then_inc(Gcn.store[s].sem, 16)
                done(sp, Gcn.x3m, g)
                hold(sp, "sp")
                sp.dma_start(rows_of(x3_last_tab, g), by_tile(X3M[s])).then_inc(Gcn.store[s].sem, 16)

            pipelined(sp, GROUPS, [(0, gcn_load), (4, gcn_store)])
            for k in range(U):
                reached(sp, Gcn.store[k], 32 * (GROUPS // U))
            sp.sem_inc(s_stage, 1)

            def gat_load(g, s, q):
                G = GROUPS - 1 - g
                freed(sp, Gat.xns, g, U)
                hold(sp, "sp")
                sp.dma_start(by_tile(XS[s]), rows_of(x3_local, G)).then_inc(Gat.fill[s].sem, 16)
                freed(sp, Gat.tx, g, U)
                hold(sp, "sp")
                sp.dma_start(by_tile(XM[s]), rows_of(x3_last_tab, G)).then_inc(Gat.load[s].sem, 16)
                freed(sp, Gat.xscan, g, U)
                hold(sp, "sp")
                sp.dma_start(mask_a[:, s, :], flags_of(same_next_d, G)).then_inc(Gat.load[s].sem, 16)
                freed(sp, Gat.drop, g, U)
                hold(sp, "sp")
                sp.dma_start(mask_b[:, s, :], flags_of(neg_next_d, G)).then_inc(Gat.neg_load[s].sem, 16)

            pipelined(sp, GROUPS, [(0, gat_load)])

        @block.gpsimd
        def _(pool):
            pool.memset(ident[:, :], 0.0).then_inc(s_const, 1)
            pool.memset(head_mask[:, :], 1.0).then_inc(s_const, 1)
            pool.memset(zeros[:, :], 0.0).then_inc(s_const, 1)
            pool.memset(ones[:, :], 1.0).then_inc(s_const, 1)
            pool.memset(eps[:, :], EPS).then_inc(s_const, 1)
            pool.wait_ge(s_const, 5)
            pool.affine_select(out=ident[:, :], in_=ident[:, :], compare_op=ALU.not_equal, fill=1.0,
                               base=0, pattern=[[-1, 128]], channel_multiplier=1).then_inc(s_const, 1)
            pool.affine_select(out=head_mask[:, :], in_=head_mask[:, :], compare_op=ALU.is_ge, fill=0.0,
                               base=0, pattern=[[-HC, HEADS], [0, HC]], channel_multiplier=1).then_inc(s_const, 1)
            pool.wait_ge(s_const, 7)
            pool.affine_select(out=head_mask[:, :], in_=head_mask[:, :], compare_op=ALU.is_ge, fill=0.0,
                               base=HC - 1, pattern=[[HC, HEADS], [0, HC]], channel_multiplier=-1).then_inc(s_const, 1)
            pool.iota(slot_i[:, :], pattern=[[128, TILES]], base=0, channel_multiplier=1).then_inc(s_const, 1)
            pool.wait_ge(s_cols, 1)

            with pool.Fori(0, TILES // PT) as i:
                pool.tensor_copy(now_i[:, :], dst_i[:, ds(i * PT, PT)]).then_inc(s_idx, 1)
                pool.wait_ge(s_idx, i + 1)
                hold(pool, "pool")
                for k in range(PT):
                    pool.indirect_dma_start(out=got_v[:, k:k + 1], out_offset=None, in_=node_vec.unsqueeze(1),
                                            in_offset=bass.IndirectOffsetOnAxis(ap=now_i[:, k:k + 1], axis=0)
                                            ).then_inc(s_got, 16)
                pool.wait_ge(s_got, (i + 1) * (16 * PT))
                hold(pool, "pool")
                pool.tensor_copy(deg[:, ds(i * PT, PT)], got_v[:, :]).then_inc(s_deg, 1)
                pool.wait_ge(s_deg, i + 1)
                hold(pool, "pool")

            def gather4(s, rows, table, gathered, limit=None, at=0):
                for j in range(TPG):
                    kw = {} if limit is None else {"bounds_check": limit, "oob_is_err": False}
                    pool.indirect_dma_start(out=rows[s][:, j * F:(j + 1) * F], out_offset=None, in_=table,
                                            in_offset=bass.IndirectOffsetOnAxis(ap=gi[:, s, at + j:at + j + 1], axis=0),
                                            **kw).then_inc(gathered[s].sem, 16)

            def source_gather(g, s, q):
                freed(pool, Node.x1, RUN_S[0] + g, U)
                hold(pool, "pool")
                pool.tensor_copy(gi[:, s, 0:TPG], src_c[:, ds(g * TPG, TPG)]).then_inc(Node.idx.sem, 1)
                done(pool, Node.idx, g)
                hold(pool, "pool")
                gather4(s, X, x, Node.gather)

            pipelined(pool, GROUPS, [(0, source_gather)])

            pool.wait_ge(s_init, 16)
            with pool.Fori(0, TILES // PT) as i:
                pool.tensor_copy(now_i[:, :], last_i[:, ds(i * PT, PT)]).then_inc(s_slot, 1)
                pool.tensor_copy(now_v[:, :], slot_i[:, ds(i * PT, PT)]).then_inc(s_slot, 1)
                pool.wait_ge(s_slot, i * 2 + 2)
                hold(pool, "pool")
                for k in range(PT):
                    pool.indirect_dma_start(out=slot_of_node, out_offset=bass.IndirectOffsetOnAxis(ap=now_i[:, k:k + 1], axis=0),
                                            in_=now_v[:, k:k + 1], in_offset=None,
                                            bounds_check=NODES - 1, oob_is_err=False).then_inc(s_placed, 16)
                pool.wait_ge(s_placed, (i + 1) * (16 * PT))
                hold(pool, "pool")
            with pool.Fori(0, TILES // PT) as i:
                pool.tensor_copy(now_i[:, :], src_c[:, ds(i * PT, PT)]).then_inc(s_from, 1)
                pool.wait_ge(s_from, i * 2 + 1)
                hold(pool, "pool")
                for k in range(PT):
                    pool.indirect_dma_start(out=now_v[:, k:k + 1], out_offset=None, in_=slot_of_node,
                                            in_offset=bass.IndirectOffsetOnAxis(ap=now_i[:, k:k + 1], axis=0)
                                            ).then_inc(s_got, 16)
                pool.wait_ge(s_got, (i + 1 + TILES // PT) * (16 * PT))
                hold(pool, "pool")
                pool.tensor_copy(from_i[:, ds(i * PT, PT)], now_v[:, :]).then_inc(s_from, 1)
                pool.wait_ge(s_from, i * 2 + 2)
                hold(pool, "pool")

            pool.wait_ge(s_stage, 1)

            def dest_gather(g, s, q):
                freed(pool, Dest.tn, g, U)
                freed(pool, Dest.xn0, g, U)
                freed(pool, Dest.xb, g, U)
                hold(pool, "pool")
                pool.tensor_copy(gi[:, s, 0:TPG], from_i[:, ds(g * TPG, TPG)]).then_inc(Dest.idx.sem, 1)
                pool.tensor_copy(gi[:, s, TPG:], dst_i[:, ds(g * TPG, TPG)]).then_inc(Dest.idx.sem, 1)
                reached(pool, Dest.idx, g * 2 + 2)
                hold(pool, "pool")
                gather4(s, NBG, nb1_tab, Dest.gather)
                gather4(s, XD, x, Dest.gather, at=TPG)

            pipelined(pool, GROUPS, [(0, dest_gather)])

            for l in range(LAYERS):
                pool.wait_ge(s_stage, 2 + l)

                def conv_gather(g, s, q, l=l):
                    n = l * GROUPS + g
                    freed(pool, Conv.ty, n, U)
                    if l == 0:
                        reached(pool, Conv.fill[s], q * 16 + 16)
                    hold(pool, "pool")
                    pool.tensor_copy(gi[:, s, 0:TPG], from_i[:, ds(g * TPG, TPG)]).then_inc(Conv.idx.sem, 1)
                    done(pool, Conv.idx, n)
                    hold(pool, "pool")
                    gather4(s, YG, y_tab[l], Conv.gather, limit=SLOTS - 1 if l == 0 else None)

                pipelined(pool, GROUPS, [(0, conv_gather)])

            pool.wait_ge(s_stage, 2 + LAYERS)

            def gcn_gather(g, s, q):
                reached(pool, Gcn.fill[s], q * 16 + 16)
                hold(pool, "pool")
                pool.tensor_copy(gi[:, s, 0:TPG], from_i[:, ds(g * TPG, TPG)]).then_inc(Gcn.idx.sem, 1)
                done(pool, Gcn.idx, g)
                hold(pool, "pool")
                gather4(s, GG, g_tab, Gcn.gather, limit=SLOTS - 1)

            pipelined(pool, GROUPS, [(0, gcn_gather)])

            pool.wait_ge(s_stage, 3 + LAYERS)

            def gat_gather(g, s, q):
                reached(pool, Gat.fill[s], q * 16 + 16)
                hold(pool, "pool")
                pool.tensor_copy(gi[:, s, 0:TPG], from_i[:, ds((GROUPS - 1 - g) * TPG, TPG)]).then_inc(Gat.idx.sem, 1)
                done(pool, Gat.idx, g)
                hold(pool, "pool")
                gather4(s, XS, x3_tab, Gat.gather, limit=SLOTS - 1)

            def gat_scatter(g, s, q):
                if not isinstance(g, int) or g >= U:
                    reached(pool, Gat.scatter[s], q * 64)
                    hold(pool, "pool")
                pool.tensor_copy(gi[:, s, TPG:], first_i[:, ds((GROUPS - 1 - g) * TPG, TPG)]).then_inc(Gat.out_idx.sem, 1)
                done(pool, Gat.out_idx, g)
                done(pool, Gat.oe, g)
                hold(pool, "pool")
                for j in range(TPG):
                    pool.indirect_dma_start(out=out, out_offset=bass.IndirectOffsetOnAxis(ap=gi[:, s, TPG + j:TPG + j + 1], axis=0),
                                            in_=OE[s][:, j * F:(j + 1) * F], in_offset=None,
                                            bounds_check=NODES - 1, oob_is_err=False).then_inc(Gat.scatter[s].sem, 16)

            pipelined(pool, GROUPS, [(0, gat_gather), (6, gat_scatter)])
            for k in range(U):
                reached(pool, Gat.scatter[k], 64 * (GROUPS // U))

        @block.vector
        def _(dve):
            link_count = [0]

            def link(ins):
                link_count[0] += 1
                ins.then_inc(s_setup, 1)
                dve.wait_ge(s_setup, link_count[0])

            link(dve.memset(pad_i[0:1, :], NOWHERE))
            link(dve.memset(pad_i[0:1, 0:1], -1))
            dve.memset(src_i[:, :], 0).then_inc(s_pad, 1)
            dve.memset(near_i[:, :, :], 0).then_inc(s_pad, 1)
            dve.memset(far_i[:, :], SLOTS).then_inc(s_far, 1)
            dve.wait_ge(s_near, 80)
            for n in range(3):
                dve.tensor_copy(near[:, n, :], near_i[:, n, :])
            link(dve.tensor_copy(near[:, 3, :], src_i[:, :]))
            before, itself, behind = near[:, 0, :], near[:, 1, :], near[:, 2, :]
            dve.tensor_tensor(rowf[:, 0, :], itself, before, ALU.is_equal)
            link(dve.tensor_tensor(rowf[:, 1, :], itself, behind, ALU.is_equal))
            dve.tensor_scalar(rowf[:, 2, :], rowf[:, 1, :], -1.0, 1.0, ALU.mult, ALU.add)
            dve.tensor_scalar(rowf[:, 3, :], rowf[:, 0, :], -1.0, 1.0, ALU.mult, ALU.add)
            dve.tensor_copy(flag_row[0], rowf[:, 0, :])
            dve.tensor_scalar(flag_row[1], rowf[:, 0, :], -1.0, NEG, ALU.add, ALU.mult)
            dve.tensor_copy(flag_row[2], rowf[:, 1, :])
            link(dve.tensor_scalar(flag_row[3], rowf[:, 1, :], -1.0, NEG, ALU.add, ALU.mult))
            dve.scalar_tensor_tensor(rowf[:, 4, :], itself, -float(NOWHERE), rowf[:, 2, :], ALU.add, ALU.mult)
            dve.scalar_tensor_tensor(rowf[:, 5, :], itself, -float(NOWHERE), rowf[:, 3, :], ALU.add, ALU.mult)
            link(dve.tensor_scalar(rowf[:, 6, :], itself, float(NODES - 1), None, ALU.min))
            dve.tensor_scalar(rowf[:, 4, :], rowf[:, 4, :], float(NOWHERE), None, ALU.add)
            dve.tensor_scalar(rowf[:, 5, :], rowf[:, 5, :], float(NOWHERE), None, ALU.add).then_inc(s_rows, 1)
            for n, dest in enumerate((last_i, first_i, dst_i, src_c, is_last)):
                dve.wait_ge(s_rowsT, n + 1)
                last = dve.tensor_copy(dest[:, :].rearrange("p (a b) -> p b a", b=2),
                                       bank[n][:, 0:2 * RR].rearrange("p (b a) -> p b a", b=2))
            last.then_inc(s_cols, 1)
            dve.wait_ge(s_act, 1)
            dve.wait_ge(s_w, 16 * (15 + 2 * LAYERS + 2 * HEADS))
            link(dve.tensor_scalar(scale_2[:, 0:4], scale_s[:, :], 2.0, None, ALU.mult))
            link(dve.tensor_scalar(scale_2[:, 4:5], scale_2[:, 2:3], -1.0, None, ALU.mult))
            dve.tensor_scalar(wc[:, 0, :], wn[:, 2, :], scale_2[:, 2:3], None, ALU.mult)
            dve.tensor_scalar(wc[:, 1, :], wn[:, 2, :], scale_2[:, 4:5], None, ALU.mult)
            link(dve.tensor_scalar(wc[:, 2, :], wn[:, 3, :], scale_2[:, 3:4], None, ALU.mult))
            dve.scalar_tensor_tensor(wc[:, 0, :], wn[:, 0, :], scale_2[:, 0:1], wc[:, 0, :], ALU.mult, ALU.add)
            dve.scalar_tensor_tensor(wc[:, 1, :], wn[:, 1, :], scale_2[:, 1:2], wc[:, 1, :], ALU.mult, ALU.add)
            dve.tensor_tensor(pt[:, :, :], wn[:, 8:12, :], wn[:, 4:8, :], ALU.subtract).then_inc(s_wc, 1)
            dve.wait_ge(s_wcT, 1)
            for n in range(3):
                last = dve.reduce_sum(small[:, n:n + 1], bank[0][:, n * F:(n + 1) * F], axis=AX.X)
            link(last)
            link(dve.reduce_sum(small[0:1, 3:4], l0_bias_r[0:1, 0:F], axis=AX.X))
            link(dve.tensor_scalar(small[:, 0:3], small[:, 0:3], 1.0 / F, None, ALU.mult))
            link(dve.tensor_scalar(small[0:1, 3:4], small[0:1, 3:4], 1.0 / F, None, ALU.mult))
            for n in range(3):
                dve.tensor_scalar(wT[:, n, :], bank[0][:, n * F:(n + 1) * F], small[:, n:n + 1], None, ALU.subtract)
            dve.tensor_scalar(wz[:, 0:F], bank[0][:, 0:F], small[:, 0:1], None, ALU.subtract)
            link(dve.tensor_scalar(l0_bias_r[0:1, 0:F], l0_bias_r[0:1, 0:F], small[0:1, 3:4], None, ALU.subtract))
            dve.tensor_tensor(wz[:, F:2 * F], wz[:, 0:F], gamma_b[:, :], ALU.mult)
            dve.tensor_tensor(l0_bias_r[0:1, F:2 * F], l0_bias_r[0:1, 0:F], gamma_b[0:1, :], ALU.mult)
            dve.wait_ge(s_const, 8)
            for n in range(2):
                dve.tensor_scalar(attn_m[:, 2 * n, :], head_mask[:, :], attn_c[:, n:n + 1], SLOPE, ALU.mult, ALU.mult)
                dve.tensor_scalar(attn_m[:, 2 * n + 1, :], head_mask[:, :], attn_c[:, n:n + 1], 1.0 - SLOPE, ALU.mult, ALU.mult)
            dve.tensor_tensor(conv_bias[:, :], conv_b[:, 0, :], conv_b[:, 1, :], ALU.add)
            dve.tensor_copy(thetaT[:, :, :], bank[1][:, :].rearrange("p (l f) -> p l f", l=LAYERS))
            dve.tensor_copy(ptT[:, :, :], bank[2][:, :].rearrange("p (l f) -> p l f", l=LAYERS)).then_inc(s_wt, 1)

            def node_phases(base, P, sources):
                def finish(g, s, q):
                    n = base + g
                    done(dve, Node.x3, n)
                    if n if isinstance(n, int) and n < U else True:
                        if not (isinstance(n, int) and n < U):
                            reached(dve, Node.store[s], (q + base // U) * 16)
                    dve.tensor_tensor(XO[s][:P], X1[s][:P], bank[2][:P, :], ALU.add).then_inc(Node.xo.sem, 1)

                def measure_x(g, s, q):
                    n = base + g
                    if sources:
                        reached(dve, Node.gather[s], q * 64 + 64)
                    else:
                        reached(dve, Node.load[s], (q + (EARLY // U if base else 0)) * 16 + 16)
                    stats(dve, X[s], st0[:, s], mv0[:, s], Node.bn0, Node.mv0, n, P)
                    dve.tensor_tensor(by_tile(XB[s])[:P], by_tile(X[s])[:P], beta_b[:P, :].unsqueeze(1).broadcast_to((P, TPG, F)), ALU.add).then_inc(Node.xb.sem, 1)

                def norm_x(g, s, q):
                    normalise(dve, XN0[s], X[s], mv0[:, s], sd0[:, s], rs0[:, s], Node.sd0, Node.rs0, Node.xn0, base + g, P)

                def layer0(g, s, q):
                    n = base + g
                    done(dve, Node.sdz, n)
                    dve.reciprocal(rsz[:P, s, :], sdz[:P, s, :]).then_inc(Node.rsz.sem, 1)
                    done(dve, Node.rsz, n)
                    z = wide[:P, :].rearrange("p (j f) -> p j f", j=TPG)
                    for j in range(TPG):
                        last = dve.scalar_tensor_tensor(X1[s][:P, j * F:(j + 1) * F], z[:, j, F:2 * F], rsz[:P, s, j:j + 1],
                                                        XB[s][:P, j * F:(j + 1) * F], ALU.mult, ALU.add)
                    last.then_inc(Node.x1.sem, 1)
                    done(dve, Node.x1, n)
                    stats(dve, X1[s], st1[:, s], mv1[:, s], Node.bn1, Node.mv1, n, P)

                def norm_x1(g, s, q):
                    if not (isinstance(g, int) and g < U):
                        if sources:
                            reached(dve, Node.h1_store[s], q * 16)
                    elif not sources and base:
                        reached(dve, Node.h1_store[s], 16 * (GROUPS // U))
                    normalise(dve, XN1[s], X1[s], mv1[:, s], sd1[:, s], rs1[:, s], Node.sd1, Node.rs1, Node.xn1, base + g, P)

                def scan_sources(g, s, q):
                    n = base + g
                    done(dve, Node.h0, n)
                    reached(dve, Node.mask[s], q * 16 + 16)
                    first = isinstance(g, int) and g == 0
                    if not first:
                        reached(dve, Node.sum1, g)
                        reached(dve, Node.cnt, g)
                    if not (isinstance(g, int) and g < U):
                        reached(dve, Node.sum_store[s], q * 16)
                    before_ = (s - 1) % U
                    dve.tensor_tensor_scan(SUM1T[s], mask_a[:, s, :], H0T[s], 0.0 if first else SUM1T[before_][:, GW - 1:GW],
                                           ALU.mult, ALU.add).then_inc(Node.sum1.sem, 1)
                    dve.tensor_tensor_scan(CNT[s], mask_a[:, s, :], ones[:, :], 0.0 if first else CNT[before_][:, GW - 1:GW],
                                           ALU.mult, ALU.add).then_inc(Node.cnt.sem, 1)

                def mean_sources(g, s, q):
                    if isinstance(g, int) and g == 0:
                        dve.wait_ge(s_deg, TILES // PT)
                        link(dve.reciprocal(rdeg[:, :], deg[:, :]))
                    done(dve, Node.ts, g)
                    if not (isinstance(g, int) and g < U):
                        reached(dve, Node.nb_store[s], q * 16)
                    hold(dve, "dve")
                    for j in range(TPG):
                        dve.tensor_scalar(NBR[s][:, j * F:(j + 1) * F], bank[3][:, j * F:(j + 1) * F], rdeg[:, ds(g * TPG + j, 1)], None, ALU.mult)
                    dve.tensor_copy(count[:, ds(g * TPG, TPG)], bank[4][:, 0:TPG]).then_inc(Node.nb.sem, 1)

                phases = [(4, finish), (0, measure_x), (1, norm_x), (2, layer0), (3, norm_x1)]
                return phases + ([(2, scan_sources), (3, mean_sources)] if sources else [])

            pipelined(dve, RUN_A[1], node_phases(RUN_A[0], NP, False))
            pipelined(dve, GROUPS, node_phases(RUN_S[0], 128, True))
            pipelined(dve, RUN_B[1], node_phases(RUN_B[0], NP, False))
            done(dve, Node.nb, GROUPS - 1)
            link(dve.tensor_scalar(count[:, :], count[:, :], 1.0, None, ALU.add))
            dve.sem_inc(s_sd, 1)
            dve.wait_ge(s_sd, 2)
            dve.reciprocal(dinv[:, :], dinv[:, :]).then_inc(s_dinv, 1)

            dve.wait_ge(s_stage, 1)

            def dest_measure(g, s, q):
                reached(dve, Dest.gather[s], q * 128 + 128)
                stats(dve, XD[s], st0[:, s], mv0[:, s], Dest.bn0, Dest.mv0, g, 128)
                dve.tensor_copy(rdg[:, s, :], rdeg[:, ds(g * TPG, TPG)])
                dve.tensor_tensor(by_tile(XBD[s]), by_tile(XD[s]), beta_b[:, :].unsqueeze(1).broadcast_to((128, TPG, F)), ALU.add).then_inc(Dest.xb.sem, 1)

            def dest_scan(g, s, q):
                done(dve, Dest.tn, g)
                reached(dve, Dest.load[s], q * 32 + 32)
                first = isinstance(g, int) and g == 0
                if not first:
                    reached(dve, Dest.sum2, g)
                dve.tensor_tensor_scan(S2T[s], mask_a[:, s, :], bank[0][:, :], 0.0 if first else S2T[(s - 1) % U][:, GW - 1:GW],
                                       ALU.mult, ALU.add).then_inc(Dest.sum2.sem, 1)

            def dest_norm(g, s, q):
                normalise(dve, XN0D[s], XD[s], mv0[:, s], sd0[:, s], rs0[:, s], Dest.sd0, Dest.rs0, Dest.xn0, g, 128)

            def dest_z(g, s, q):
                done(dve, Dest.zs, g)
                dve.tensor_tensor(ZM[s], ZS[s], bank[2][:, :], ALU.add).then_inc(Dest.zm.sem, 1)

            def dest_x1(g, s, q):
                done(dve, Dest.sdz, g)
                if not (isinstance(g, int) and g < U):
                    reached(dve, Dest.store[s], q * 48)
                dve.reciprocal(rsz[:, s, :], sdz[:, s, :]).then_inc(Dest.rsz.sem, 1)
                done(dve, Dest.rsz, g)
                for j in range(TPG):
                    last = dve.scalar_tensor_tensor(ZM[s][:, j * F:(j + 1) * F], ZM[s][:, j * F:(j + 1) * F], rsz[:, s, j:j + 1],
                                                    gamma_b[:, :], ALU.mult, ALU.mult)
                last.then_inc(Dest.w.sem, 1)
                done(dve, Dest.w, g)
                dve.tensor_tensor(X1D[s], ZM[s], XBD[s], ALU.add).then_inc(Dest.x1.sem, 1)
                done(dve, Dest.x1, g)
                stats(dve, X1D[s], st1[:, s], mv1[:, s], Dest.bn1, Dest.mv1, g, 128)

            def dest_norm1(g, s, q):
                normalise(dve, XN1D[s], X1D[s], mv1[:, s], sd1[:, s], rs1[:, s], Dest.sd1, Dest.rs1, Dest.xn1, g, 128)

            pipelined(dve, GROUPS, [(0, dest_measure), (1, dest_scan), (1, dest_norm), (2, dest_z), (3, dest_x1), (4, dest_norm1)])

            for l in range(LAYERS):
                dve.wait_ge(s_stage, 2 + l)

                def conv_scan(g, s, q, l=l):
                    n = l * GROUPS + g
                    done(dve, Conv.m1, n)
                    reached(dve, Conv.load[s], (q + l * (GROUPS // U)) * 32 + 32)
                    first = isinstance(g, int) and g == 0
                    if not first:
                        reached(dve, Conv.scan, n)
                    dve.tensor_tensor_scan(SC[s], mask_a[:, s, :], bank[1][:, :], -NEG if first else SC[(s - 1) % U][:, GW - 1:GW],
                                           ALU.add, ALU.max).then_inc(Conv.scan.sem, 1)
                    done(dve, Conv.scan, n)
                    done(dve, Conv.m2, n)
                    dve.tensor_tensor(AD[s], SC[s], bank[2][:, :], ALU.add).then_inc(Conv.add.sem, 1)

                def conv_rows(g, s, q, l=l):
                    n = l * GROUPS + g
                    done(dve, Conv.tb, n)
                    if not (isinstance(g, int) and g < U):
                        reached(dve, Conv.store[s], (q + l * (GROUPS // U)) * 32)
                    dve.tensor_copy(YE[s], bank[3][:, :]).then_inc(Conv.ye.sem, 1)

                def conv_x2(g, s, q, l=l):
                    done(dve, Conv.tb, l * GROUPS + g)
                    reached(dve, Conv.x1_load[s], q * 16 + 16)
                    if not (isinstance(g, int) and g < U):
                        reached(dve, Conv.store[s], (q + l * (GROUPS // U)) * 32)
                    dve.tensor_tensor(X2[s], X1L[s], bank[3][:, :], ALU.add).then_inc(Conv.x2.sem, 1)
                    done(dve, Conv.x2, g)
                    stats(dve, X2[s], st0[:, s], mv0[:, s], Conv.bn, Conv.mv, g, 128)

                def conv_g(g, s, q):
                    normalise(dve, XN2[s], X2[s], mv0[:, s], sd0[:, s], rs0[:, s], Conv.sd, Conv.rs, Conv.xn, g, 128)
                    done(dve, Conv.xn, g)
                    hold(dve, "dve")
                    for j in range(TPG):
                        last = dve.tensor_scalar(G2[s][:, j * F:(j + 1) * F], XN2[s][:, j * F:(j + 1) * F], 0.0,
                                                 dinv[:, ds(g * TPG + j, 1)], ALU.max, ALU.mult)
                    last.then_inc(Conv.g.sem, 1)

                if l < LAYERS - 1:
                    pipelined(dve, GROUPS, [(1, conv_scan), (2, conv_rows)])
                else:
                    pipelined(dve, GROUPS, [(1, conv_scan), (2, conv_x2), (3, conv_g)])

            dve.wait_ge(s_stage, 2 + LAYERS)

            def gcn_scan(g, s, q):
                done(dve, Gcn.gt, g)
                reached(dve, Gcn.load[s], q * 48 + 48)
                first = isinstance(g, int) and g == 0
                if not first:
                    reached(dve, Gcn.scan, g)
                dve.tensor_tensor_scan(SG[s], mask_a[:, s, :], GTs[s], 0.0 if first else SG[(s - 1) % U][:, GW - 1:GW],
                                       ALU.mult, ALU.add).then_inc(Gcn.scan.sem, 1)
                done(dve, Gcn.scan, g)
                done(dve, Gcn.td, g)
                dve.tensor_tensor(UG[s], SG[s], bank[1][:, :], ALU.add).then_inc(Gcn.u.sem, 1)
                dve.tensor_tensor(by_tile(XB2[s]), by_tile(X2L[s]), gcn_b_b[:, :].unsqueeze(1).broadcast_to((128, TPG, F)), ALU.add).then_inc(Gcn.xb.sem, 1)

            def gcn_x3(g, s, q):
                done(dve, Gcn.w, g)
                done(dve, Gcn.xb, g)
                if not (isinstance(g, int) and g < U):
                    reached(dve, Gcn.store[s], q * 32)
                hold(dve, "dve")
                for j in range(TPG):
                    last = dve.scalar_tensor_tensor(X3[s][:, j * F:(j + 1) * F], bank[2][:, j * F:(j + 1) * F], dinv[:, ds(g * TPG + j, 1)],
                                                    XB2[s][:, j * F:(j + 1) * F], ALU.mult, ALU.add)
                last.then_inc(Gcn.x3.sem, 1)
                done(dve, Gcn.x3, g)
                hold(dve, "dve")
                for j in range(TPG):
                    last = dve.tensor_scalar(X3M[s][:, j * F:(j + 1) * F], X3[s][:, j * F:(j + 1) * F], is_last[:, ds(g * TPG + j, 1)], None, ALU.mult)
                last.then_inc(Gcn.x3m.sem, 1)

            pipelined(dve, GROUPS, [(1, gcn_scan), (2, gcn_x3)])

            dve.wait_ge(s_stage, 3 + LAYERS)

            def back(t):
                return t[:, ::-1]

            def gat_measure(g, s, q):
                reached(dve, Gat.gather[s], q * 64 + 64)
                stats(dve, XS[s], st0[:, s], mv0[:, s], Gat.bns, Gat.mvs, g, 128)

            def gat_spread(g, s, q):
                done(dve, Gat.tx, g)
                reached(dve, Gat.load[s], q * 32 + 32)
                first = isinstance(g, int) and g == 0
                if not first:
                    reached(dve, Gat.xscan, g)
                dve.tensor_tensor_scan(back(X3T[s]), back(mask_a[:, s, :]), back(bank[2][:, :]),
                                       0.0 if first else X3T[(s - 1) % U][:, 0:1], ALU.mult, ALU.add).then_inc(Gat.xscan.sem, 1)

            def gat_norm(g, s, q):
                freed(dve, Gat.ts, g, 1)
                normalise(dve, XNS, XS[s], mv0[:, s], sd0[:, s], rs0[:, s], Gat.sds, Gat.rss, Gat.xns, g, 128)

            def gat_measure_d(g, s, q):
                done(dve, Gat.txb, g)
                stats(dve, bank[3], st1[:, s], mv1[:, s], Gat.bnd, Gat.mvd, g, 128)

            def gat_norm_d(g, s, q):
                freed(dve, Gat.td, g, 1)
                normalise(dve, XND, bank[3], mv1[:, s], sd1[:, s], rs1[:, s], Gat.sdd, Gat.rsd, Gat.xnd, g, 128)

            def gat_max(g, s, q):
                done(dve, Gat.lgs, g)
                reached(dve, Gat.neg_load[s], q * 16 + 16)
                first = isinstance(g, int) and g == 0
                if not first:
                    reached(dve, Gat.mscan, g)
                    dve.tensor_copy(MX[s][:, GW:GW + 1], MX[(s - 1) % U][:, 0:1])
                else:
                    dve.memset(MX[s][:, GW:GW + 1], 0.0)
                dve.tensor_tensor_scan(back(MX[s][:, 0:GW]), back(mask_b[:, s, :]), back(LGS[s]),
                                       -NEG if first else MX[(s - 1) % U][:, 0:1], ALU.add, ALU.max).then_inc(Gat.mscan.sem, 1)
                done(dve, Gat.mscan, g)
                dve.tensor_tensor(CE[s], MX[s][:, 1:GW + 1], MX[s][:, 0:GW], ALU.subtract).then_inc(Gat.diff.sem, 1)
                dve.tensor_tensor(PE_[s], LGS[s], MX[s][:, 0:GW], ALU.subtract).then_inc(Gat.sub.sem, 1)
                done(dve, Gat.diff, g)
                dve.scalar_tensor_tensor(CE[s], CE[s], 0.0, mask_b[:, s, :], ALU.min, ALU.add).then_inc(Gat.drop.sem, 1)

            def gat_sum(g, s, q):
                done(dve, Gat.ec, g)
                done(dve, Gat.ep, g)
                first = isinstance(g, int) and g == 0
                if not first:
                    reached(dve, Gat.den, g)
                dve.tensor_tensor_scan(back(DEN[s]), back(CE[s]), back(PE_[s]), 0.0 if first else DEN[(s - 1) % U][:, 0:1],
                                       ALU.mult, ALU.add).then_inc(Gat.den.sem, 1)
                if not first:
                    reached(dve, Gat.num, g)
                freed(dve, Gat.ot, g, 1)
                dve.tensor_tensor(PN, PE_[s], NTS[s], ALU.mult).then_inc(Gat.pn.sem, 1)
                done(dve, Gat.pn, g)
                dve.tensor_tensor_scan(back(NUM[s]), back(CE[s]), back(PN), 0.0 if first else NUM[(s - 1) % U][:, 0:1],
                                       ALU.mult, ALU.add).then_inc(Gat.num.sem, 1)
                done(dve, Gat.den, g)
                dve.reciprocal(PE_[s], DEN[s]).then_inc(Gat.rden.sem, 1)
                done(dve, Gat.rden, g)
                done(dve, Gat.num, g)
                freed(dve, Gat.tf, g, 1)
                dve.tensor_tensor(PN, PE_[s], NUM[s], ALU.mult).then_inc(Gat.ratio.sem, 1)
                done(dve, Gat.ratio, g)
                dve.tensor_tensor(OT, PN, X3T[s], ALU.add).then_inc(Gat.ot.sem, 1)

            pipelined(dve, GROUPS, [(0, gat_measure), (0, gat_spread), (2, gat_norm_d), (1, gat_norm), (1, gat_measure_d),
                                    (3, gat_max), (4, gat_sum)])

        @block.scalar
        def _(act):
            act.wait_ge(s_w, 16 * (15 + 2 * LAYERS + 2 * HEADS))
            act.activation(scale_s[:, :], scale_l[:, :], ACT.Sigmoid).then_inc(s_act, 1)

            def root(sd, mv, s_sd_, s_mv, n, P=128):
                done(act, s_mv, n)
                act.activation(sd[:P, :], mv[:P, :, 1], ACT.Sqrt, bias=eps[:P, :]).then_inc(s_sd_.sem, 1)

            def node_phases(base, P):
                def root_x(g, s, q):
                    root(sd0[:, s], mv0[:, s], Node.sd0, Node.mv0, base + g, P)

                def turned_x(g, s, q):
                    done(act, Node.t0, base + g)
                    if base == RUN_S[0] and not (isinstance(g, int) and g < U):
                        reached(act, Node.sum1, g - U + 1)
                    act.activation(by_tile(H0T[s])[:, :, 0:P], by_tile(bank[0][:, :])[:, :, 0:P], ACT.Relu).then_inc(Node.h0.sem, 1)

                def square_z(g, s, q):
                    n = base + g
                    done(act, Node.z, n)
                    z = wide[:P, :].rearrange("p (j f) -> p j f", j=TPG)
                    for j in range(TPG):
                        last = act.activation(junk[:P, j * F:(j + 1) * F], z[:, j, 0:F], ACT.Square, accum_out=ssq[:P, s, j:j + 1])
                    last.then_inc(Node.ssq.sem, 1)
                    done(act, Node.ssq, n)
                    act.activation(sdz[:P, s, :], ssq[:P, s, :], ACT.Sqrt, bias=eps[:P, :], scale=1.0 / F).then_inc(Node.sdz.sem, 1)

                def root_x1(g, s, q):
                    root(sd1[:, s], mv1[:, s], Node.sd1, Node.mv1, base + g, P)

                def turned_x1(g, s, q):
                    done(act, Node.t1, base + g)
                    act.activation(by_tile(H1T[s])[:, :, 0:P], by_tile(bank[1][:, :])[:, :, 0:P], ACT.Relu).then_inc(Node.h1.sem, 1)

                return [(0, root_x), (1, turned_x), (1, square_z), (2, root_x1), (3, turned_x1)]

            pipelined(act, RUN_A[1], node_phases(RUN_A[0], NP))
            pipelined(act, GROUPS, node_phases(RUN_S[0], 128))
            pipelined(act, RUN_B[1], node_phases(RUN_B[0], NP))
            act.wait_ge(s_sd, 1)
            act.activation(dinv[:, :], count[:, :], ACT.Sqrt).then_inc(s_sd, 1)

            act.wait_ge(s_stage, 1)

            def dest_root(g, s, q):
                root(sd0[:, s], mv0[:, s], Dest.sd0, Dest.mv0, g)

            def dest_turned(g, s, q):
                done(act, Dest.t0, g)
                act.activation(H0D[s], bank[1][:, :], ACT.Relu).then_inc(Dest.h0.sem, 1)

            def dest_mean(g, s, q):
                done(act, Dest.z, g)
                done(act, Dest.xb, g)
                for j in range(TPG):
                    last = act.activation(ZS[s][:, j * F:(j + 1) * F], bank[3][:, j * F:(j + 1) * F], ACT.Identity, scale=rdg[:, s, j:j + 1])
                last.then_inc(Dest.zs.sem, 1)

            def dest_square(g, s, q):
                done(act, Dest.zm, g)
                for j in range(TPG):
                    last = act.activation(junk[:, j * F:(j + 1) * F], ZM[s][:, j * F:(j + 1) * F], ACT.Square, accum_out=ssq[:, s, j:j + 1])
                last.then_inc(Dest.ssq.sem, 1)
                done(act, Dest.ssq, g)
                act.activation(sdz[:, s, :], ssq[:, s, :], ACT.Sqrt, bias=eps[:, :], scale=1.0 / F).then_inc(Dest.sdz.sem, 1)

            def dest_root1(g, s, q):
                root(sd1[:, s], mv1[:, s], Dest.sd1, Dest.mv1, g)

            def dest_turned1(g, s, q):
                done(act, Dest.t1, g)
                if not (isinstance(g, int) and g < U):
                    reached(act, Dest.store[s], q * 48)
                act.activation(H1D[s], bank[4][:, :], ACT.Relu).then_inc(Dest.h1.sem, 1)

            pipelined(act, GROUPS, [(0, dest_root), (1, dest_turned), (1, dest_mean), (2, dest_square), (3, dest_root1), (4, dest_turned1)])

            for l in range(LAYERS):
                act.wait_ge(s_stage, 2 + l)

                def conv_turned(g, s, q, l=l):
                    done(act, Conv.ty, l * GROUPS + g)
                    act.activation(YT[s], bank[0][:, :], ACT.Relu).then_inc(Conv.yt.sem, 1)

                def conv_relu(g, s, q, l=l):
                    n = l * GROUPS + g
                    done(act, Conv.add, n)
                    if l < LAYERS - 1 and not (isinstance(g, int) and g < U):
                        reached(act, Conv.store[s], (q + l * (GROUPS // U)) * 32)
                    act.activation(YN[s], AD[s], ACT.Relu, bias=conv_bias[:, l:l + 1]).then_inc(Conv.yn.sem, 1)

                def conv_root(g, s, q):
                    root(sd0[:, s], mv0[:, s], Conv.sd, Conv.mv, g)

                pipelined(act, GROUPS, [(0, conv_turned), (1, conv_relu)] + ([(2, conv_root)] if l == LAYERS - 1 else []))

            act.wait_ge(s_stage, 2 + LAYERS)

            def gcn_turned(g, s, q):
                done(act, Gcn.tg, g)
                act.activation(GTs[s], bank[0][:, :], ACT.Relu).then_inc(Gcn.gt.sem, 1)

            pipelined(act, GROUPS, [(0, gcn_turned)])

            act.wait_ge(s_stage, 3 + LAYERS)

            def gat_root(g, s, q):
                root(sd0[:, s], mv0[:, s], Gat.sds, Gat.mvs, g)

            def gat_root_d(g, s, q):
                root(sd1[:, s], mv1[:, s], Gat.sdd, Gat.mvd, g)

            def gat_source(g, s, q):
                done(act, Gat.ts, g)
                freed(act, Gat.ws, g, 1)
                act.activation(HST, bank[0][:, :], ACT.Relu).then_inc(Gat.hs.sem, 1)
                done(act, Gat.ws, g)
                act.activation(NTS[s], bank[1][:, :], ACT.Identity, bias=gat_b_c[:, :]).then_inc(Gat.nt.sem, 1)
                act.activation(LKS[s], bank[1][:, :], ACT.Relu, bias=gat_b_c[:, :]).then_inc(Gat.lks.sem, 1)

            def gat_dest(g, s, q):
                done(act, Gat.td, g)
                freed(act, Gat.wd, g, 1)
                act.activation(HDT, bank[4][:, :], ACT.Relu).then_inc(Gat.hd.sem, 1)
                done(act, Gat.wd, g)
                freed(act, Gat.lg, g, 1)
                act.activation(NTD, bank[5][:, :], ACT.Identity, bias=gat_b_c[:, :])
                act.activation(LKD, bank[5][:, :], ACT.Relu, bias=gat_b_c[:, :]).then_inc(Gat.lkd.sem, 1)
                done(act, Gat.lg, g)
                act.activation(LGS[s], wide[:, 0:GW], ACT.Identity, bias=attn_b_c[:, :]).then_inc(Gat.lgs.sem, 1)

            def gat_exp(g, s, q):
                done(act, Gat.sub, g)
                act.activation(PE_[s], PE_[s], ACT.Exp).then_inc(Gat.ep.sem, 1)
                done(act, Gat.drop, g)
                act.activation(CE[s], CE[s], ACT.Exp).then_inc(Gat.ec.sem, 1)

            def gat_out(g, s, q):
                done(act, Gat.tf, g)
                if not (isinstance(g, int) and g < U):
                    reached(act, Gat.scatter[s], q * 64)
                act.activation(OE[s], wide[:, GW:], ACT.Copy).then_inc(Gat.oe.sem, 1)

            pipelined(act, GROUPS, [(0, gat_root), (1, gat_source), (2, gat_dest), (1, gat_root_d), (3, gat_exp), (4, gat_out)])

        @block.tensor
        def _(pe):
            pe.wait_ge(s_const, 6)
            pe.wait_ge(s_rows, 1)
            for n, row in enumerate((rowf[:, 4, :], rowf[:, 5, :], rowf[:, 6, :], near[:, 3, :], rowf[:, 2, :])):
                for b in range(2):
                    last = pe.transpose(bank[n][:, b * RR:(b + 1) * RR], row[:, b * 128:(b + 1) * 128], ident[:RR, :RR])
                last.then_inc(s_rowsT, 1)
            pe.wait_ge(s_cols, 1)
            pe.wait_ge(s_wc, 1)
            for n in range(3):
                pe.transpose(bank[0][:, n * F:(n + 1) * F], wc[:, n, :], ident[:, :])
            for l in range(LAYERS):
                pe.transpose(bank[1][:, l * F:(l + 1) * F], wn[:, 4 + l, :], ident[:, :])
                last = pe.transpose(bank[2][:, l * F:(l + 1) * F], pt[:, l, :], ident[:, :])
            last.then_inc(s_wcT, 1)
            pe.wait_ge(s_wt, 1)

            def node_phases(base, P, sources):
                def turn_x(g, s, q):
                    n = base + g
                    done(pe, Node.xn0, n)
                    freed(pe, Node.h0, n, 1)
                    turn(pe, bank[0], XN0[s], P).then_inc(Node.t0.sem, 1)

                def product_z(g, s, q):
                    n = base + g
                    done(pe, Node.h0, n)
                    freed(pe, Node.x1, n, 1)
                    z = wide[:P, :].rearrange("p (j f) -> p j f", j=TPG)
                    for j in range(TPG):
                        pe.matmul(z[:, j, :], H0T[s][:, j * 128:j * 128 + P], wz[:, :], start=True, stop=False)
                        last = pe.matmul(z[:, j, :], ones[0:1, 0:P], l0_bias_r[0:1, :], start=False, stop=True)
                    last.then_inc(Node.z.sem, 1)

                def turn_x1(g, s, q):
                    n = base + g
                    done(pe, Node.xn1, n)
                    freed(pe, Node.h1, n, 1)
                    turn(pe, bank[1], XN1[s], P).then_inc(Node.t1.sem, 1)

                def product_x3(g, s, q):
                    n = base + g
                    done(pe, Node.h1, n)
                    freed(pe, Node.xo, n, 1)
                    for j in range(TPG):
                        pe.matmul(bank[2][:P, j * F:(j + 1) * F], H1T[s][:, j * 128:j * 128 + P], gcn_w_s[:, :], start=True, stop=False)
                        last = pe.matmul(bank[2][:P, j * F:(j + 1) * F], ones[0:1, 0:P], gcn_b_b[0:1, :], start=False, stop=True)
                    last.then_inc(Node.x3.sem, 1)

                def turn_sums(g, s, q):
                    done(pe, Node.cnt, g)
                    freed(pe, Node.nb, g, 1)
                    turn(pe, bank[3], SUM1T[s])
                    for j in range(TPG):
                        last = pe.matmul(bank[4][:, j:j + 1], CNT[s][:, j * 128:(j + 1) * 128], ident[:, 0:1], start=True, stop=True)
                    last.then_inc(Node.ts.sem, 1)

                return ([(2, turn_sums)] if sources else []) + [(1, turn_x), (1, product_z), (3, turn_x1), (3, product_x3)]

            pipelined(pe, RUN_A[1], node_phases(RUN_A[0], NP, False))
            pipelined(pe, GROUPS, node_phases(RUN_S[0], 128, True))
            pipelined(pe, RUN_B[1], node_phases(RUN_B[0], NP, False))

            pe.wait_ge(s_stage, 1)

            def dest_turn_nb(g, s, q):
                reached(pe, Dest.gather[s], q * 128 + 128)
                freed(pe, Dest.sum2, g, 1)
                turn(pe, bank[0], NBG[s]).then_inc(Dest.tn.sem, 1)

            def dest_turn_x(g, s, q):
                done(pe, Dest.xn0, g)
                freed(pe, Dest.h0, g, 1)
                turn(pe, bank[1], XN0D[s]).then_inc(Dest.t0.sem, 1)

            def dest_products(g, s, q):
                done(pe, Dest.h0, g)
                done(pe, Dest.sum2, g)
                reached(pe, Dest.load[s], q * 32 + 32)
                freed(pe, Dest.zm, g, 1)
                freed(pe, Dest.zs, g, 1)
                for j in range(TPG):
                    at = slice(j * F, (j + 1) * F)
                    pe.matmul(bank[2][:, at], H0D[s][:, at], wT[:, 0, :], start=True, stop=False)
                    pe.matmul(bank[2][:, at], ones[0:1, 0:128], l0_bias_r[0:1, 0:F], start=False, stop=True)
                    pe.matmul(bank[3][:, at], S1L[s][:, at], wT[:, 1, :], start=True, stop=False)
                    last = pe.matmul(bank[3][:, at], S2T[s][:, at], wT[:, 2, :], start=False, stop=True)
                last.then_inc(Dest.z.sem, 1)

            def dest_turn_x1(g, s, q):
                done(pe, Dest.xn1, g)
                freed(pe, Dest.h1, g, 1)
                turn(pe, bank[4], XN1D[s]).then_inc(Dest.t1.sem, 1)

            pipelined(pe, GROUPS, [(0, dest_turn_nb), (1, dest_turn_x), (1, dest_products), (4, dest_turn_x1)])

            for l in range(LAYERS):
                pe.wait_ge(s_stage, 2 + l)

                def conv_turn(g, s, q, l=l):
                    n = l * GROUPS + g
                    reached(pe, Conv.gather[s], (q + l * (GROUPS // U)) * 64 + 64)
                    freed(pe, Conv.yt, n, 1)
                    turn(pe, bank[0], YG[s]).then_inc(Conv.ty.sem, 1)

                def conv_products(g, s, q, l=l):
                    n = l * GROUPS + g
                    reached(pe, Conv.load[s], (q + l * (GROUPS // U)) * 32 + 32)
                    freed(pe, Conv.add, n, 1)
                    pe.matmul(bank[2][:, :], ptT[:, l, :], YL[s], start=True, stop=True).then_inc(Conv.m2.sem, 1)
                    done(pe, Conv.yt, n)
                    pe.matmul(bank[1][:, :], thetaT[:, l, :], YT[s], start=True, stop=True).then_inc(Conv.m1.sem, 1)

                def conv_turn_back(g, s, q, l=l):
                    n = l * GROUPS + g
                    done(pe, Conv.yn, n)
                    if l < LAYERS - 1:
                        freed(pe, Conv.ye, n, 1)
                    elif not (isinstance(g, int) and g == 0):
                        freed(pe, Conv.x2, g, 1)
                    turn(pe, bank[3], YN[s]).then_inc(Conv.tb.sem, 1)

                pipelined(pe, GROUPS, [(0, conv_turn), (0, conv_products), (2, conv_turn_back)])

            pe.wait_ge(s_stage, 2 + LAYERS)

            def gcn_turn(g, s, q):
                reached(pe, Gcn.load[s], q * 48 + 48)
                freed(pe, Gcn.u, g, 1)
                turn(pe, bank[1], GD[s]).then_inc(Gcn.td.sem, 1)
                reached(pe, Gcn.gather[s], q * 64 + 64)
                freed(pe, Gcn.gt, g, 1)
                turn(pe, bank[0], GG[s]).then_inc(Gcn.tg.sem, 1)

            def gcn_product(g, s, q):
                done(pe, Gcn.u, g)
                freed(pe, Gcn.x3, g, 1)
                for j in range(TPG):
                    at = slice(j * F, (j + 1) * F)
                    last = pe.matmul(bank[2][:, at], UG[s][:, at], gcn_w_s[:, :], start=True, stop=True)
                last.then_inc(Gcn.w.sem, 1)

            pipelined(pe, GROUPS, [(0, gcn_turn), (2, gcn_product)])

            pe.wait_ge(s_stage, 3 + LAYERS)

            def gat_turn_last(g, s, q):
                reached(pe, Gat.load[s], q * 32 + 32)
                freed(pe, Gat.xscan, g, 1)
                turn(pe, bank[2], XM[s]).then_inc(Gat.tx.sem, 1)

            def gat_turn_back(g, s, q):
                done(pe, Gat.xscan, g)
                freed(pe, Gat.xnd, g, 1)
                turn(pe, bank[3], X3T[s]).then_inc(Gat.txb.sem, 1)

            def gat_source(g, s, q):
                done(pe, Gat.xns, g)
                freed(pe, Gat.hs, g, 1)
                turn(pe, bank[0], XNS).then_inc(Gat.ts.sem, 1)
                done(pe, Gat.hs, g)
                freed(pe, Gat.lks, g, 1)
                pe.matmul(bank[1][:, :], gat_w_s[:, :], HST, start=True, stop=True).then_inc(Gat.ws.sem, 1)

            def gat_dest(g, s, q):
                done(pe, Gat.xnd, g)
                freed(pe, Gat.hd, g, 1)
                turn(pe, bank[4], XND).then_inc(Gat.td.sem, 1)
                done(pe, Gat.hd, g)
                freed(pe, Gat.lkd, g, 1)
                pe.matmul(bank[5][:, :], gat_w_s[:, :], HDT, start=True, stop=True).then_inc(Gat.wd.sem, 1)
                done(pe, Gat.lks, g)
                done(pe, Gat.lkd, g)
                freed(pe, Gat.lgs, g, 1)
                pe.matmul(wide[:, 0:GW], attn_m[:, 0, :], NTS[s], start=True, stop=False)
                pe.matmul(wide[:, 0:GW], attn_m[:, 1, :], LKS[s], start=False, stop=False)
                pe.matmul(wide[:, 0:GW], attn_m[:, 2, :], NTD, start=False, stop=False)
                pe.matmul(wide[:, 0:GW], attn_m[:, 3, :], LKD, start=False, stop=True).then_inc(Gat.lg.sem, 1)

            def gat_turn_out(g, s, q):
                done(pe, Gat.ot, g)
                freed(pe, Gat.oe, g, 1)
                turn(pe, wide[:, GW:], OT).then_inc(Gat.tf.sem, 1)

            pipelined(pe, GROUPS, [(0, gat_turn_last), (1, gat_source), (1, gat_turn_back), (2, gat_dest), (4, gat_turn_out)])


_INS = ["x", "src", "dst", "node_vec", "L0_gnn_W_self", "L0_gnn_W_nb1", "L0_gnn_W_hp", "L0_gnn_W_nb2", "L0_gnn_bias",
        "L0_gnn_branch_logits", "L0_gnn_ln_gamma", "L0_gnn_ln_beta", "L1_gnn_theta_w", "L1_gnn_theta_b",
        "L1_gnn_phi_w", "L1_gnn_phi_b", "L2_gnn_W", "L2_gnn_b", "L3_gnn_W", "L3_gnn_b", "L3_gnn_attn_w", "L3_gnn_attn_b"]


def kernel(**inputs):
    import concourse.bacc as bacc
    from concourse.bass_utils import run_bass_kernel_spmd

    nc = bacc.Bacc("TRN2", target_bir_lowering=False, num_devices=1)
    arrays, args = {}, []
    for name in _INS:
        a = np.ascontiguousarray(inputs[name])
        arrays[f"in_{name}"] = a
        args.append(nc.dram_tensor(f"in_{name}", a.shape, mybir.dt.from_np(a.dtype), kind="ExternalInput").ap())
    out = nc.dram_tensor("out_0", (NODES, F), F32, kind="ExternalOutput").ap()
    build(nc, *args, out)
    return run_bass_kernel_spmd(nc, [arrays], core_ids=[0]).results[0]["out_0"]
```

```python
from contextlib import ExitStack

import numpy as np
import concourse.bass as bass
from concourse import mybir

F32 = mybir.dt.float32
BF16 = mybir.dt.bfloat16
I32 = mybir.dt.int32
ALU = mybir.AluOpType
ACT = mybir.ActivationFunctionType
AX = mybir.AxisListType

NODES, EDGES, F = 100000, 25000, 128
LAYERS, HEADS = 4, 8
HC = F // HEADS
TPG = 4
GW = TPG * 128
U = 5
GROUPS = -(-EDGES // GW)
GROUPS += -GROUPS % U
SLOTS = GROUPS * GW
TILES = SLOTS // 128
RW = 2 * 128
RR = SLOTS // RW
NOWHERE = 1 << 20
NP = 125
NG = NP * TPG
NODE_GROUPS = NODES // NG
EARLY = 40
PT = 40
EPS = 1e-5
SLOPE = 0.2
NEG = 3.0e38
ds = bass.ds


def pipelined(eng, count, phases):
    deepest = max(lag for lag, _ in phases)
    head = U + -(-deepest // U) * U
    turns = (count - head) // U

    def static(n):
        for lag, phase in phases:
            if 0 <= n - lag < count:
                phase(n - lag, (n - lag) % U, (n - lag) // U)

    for n in range(head):
        static(n)
    if turns > 0:
        with eng.Fori(0, turns) as i:
            for k in range(U):
                for lag, phase in phases:
                    g = head + k - lag
                    phase(i * U + g, g % U, i + g // U)
    for n in range(head + turns * U, count + deepest):
        static(n)


class Signal:

    def __init__(self, semaphore, base):
        self.sem, self.base = semaphore, base


def reached(eng, signal, value):
    eng.wait_ge(signal.sem, value + signal.base)


def done(eng, signal, n):
    reached(eng, signal, n + 1)


def freed(eng, signal, n, depth):
    if isinstance(n, int) and n < depth:
        return
    reached(eng, signal, n - depth + 1)


def build(nc, x, src, dst, node_vec, w_self, w_nb1, w_hp, w_nb2, l0_bias, logits, gamma, beta,
          theta_w, theta_b, phi_w, phi_b, gcn_w, gcn_b, gat_w, gat_b, attn_w, attn_b, out):
    with ExitStack() as ctx:
        def sb(name, shape, dt=F32):
            return ctx.enter_context(nc.sbuf_tensor(name, shape, dt))

        def sem(name):
            return ctx.enter_context(nc.semaphore(name))

        def sems(name):
            return [sem(f"{name}{k}") for k in range(U)]

        def dram(name, shape, dt=F32):
            return nc.dram_tensor(name, shape, dt, kind="Internal").ap()

        dst_padded = dram("dst_padded", (1, SLOTS + 2), I32)
        flags_d = [dram(f"flags_{n}", (1, SLOTS), BF16) for n in range(4)]
        same_prev_d, neg_prev_d, same_next_d, neg_next_d = flags_d
        slot_of_node = dram("slot_of_node", (NODES, 1), I32)
        nb1_tab = dram("nb1_tab", (SLOTS + 1, F))
        sum1T_tab = dram("sum1T_tab", (F, SLOTS))
        h1_local = dram("h1_local", (SLOTS, F))
        message_local = dram("message_local", (SLOTS, F))
        nt_local = dram("nt_local", (SLOTS, F))
        x1_tab = dram("x1_tab", (SLOTS, F))
        message_tab = [dram(f"message_tab{n}", (SLOTS + (n > 0), F)) for n in range(LAYERS)]
        ownT_tab = [dram(f"ownT_tab{n}", (F, SLOTS)) for n in range(LAYERS)]
        x2_tab = dram("x2_tab", (SLOTS, F))
        g_tab = dram("g_tab", (SLOTS, F))
        nt_tab = dram("nt_tab", (SLOTS, F))
        x3_last_tab = dram("x3_last_tab", (SLOTS, F))
        nt_last_tab = dram("nt_last_tab", (SLOTS, F))

        def rows_of(tab, g):
            return tab[ds(g * GW, GW), :].rearrange("(j p) f -> p j f", p=128)

        def cols_of(tab, g):
            return tab[:, ds(g * GW, GW)]

        def flags_of(tab, g):
            return tab[0:1, ds(g * GW, GW)].partition_broadcast(128)

        ident = sb("ident", [128, 128])
        head_mask = sb("head_mask", [128, 128])
        ones = sb("ones", [128, GW])
        zeros = sb("zeros", [128, F])
        eps = sb("eps", [128, 1])
        gamma_b = sb("gamma_b", [128, F])
        beta_b = sb("beta_b", [128, F])
        gcn_b_b = sb("gcn_b_b", [128, F])
        bias3 = sb("bias3", [3, 2, GW], BF16)
        ones3 = sb("ones3", [3, 128], BF16)
        wT = sb("wT", [128, 3, F])
        thetaT = sb("thetaT", [128, LAYERS, F])
        ptT = sb("ptT", [128, LAYERS, F])
        gcn_w_s = sb("gcn_w_s", [128, F])
        gat_w_s = sb("gat_w_s", [128, F])
        gat_b_c = sb("gat_b_c", [128, 1])
        attn_c = sb("attn_c", [128, 2])
        attn_b_c = sb("attn_b_c", [128, 1])
        attn_m = sb("attn_m", [128, 2, F])
        conv_b = sb("conv_b", [128, 2, LAYERS])
        conv_bias = sb("conv_bias", [128, LAYERS])
        scale_l = sb("scale_l", [128, 4])
        scale_s = sb("scale_s", [128, 4])
        scale_2 = sb("scale_2", [128, 6])
        small = sb("small", [128, 4])

        far_i = sb("far_i", [NP, NODES // NP], I32)
        last_i = sb("last_i", [128, TILES], I32)
        first_i = sb("first_i", [128, TILES], I32)
        dst_i = sb("dst_i", [128, TILES], I32)
        src_c = sb("src_c", [128, TILES], I32)
        slot_i = sb("slot_i", [128, TILES], I32)
        from_i = sb("from_i", [128, TILES], I32)
        is_last = sb("is_last", [128, TILES])
        deg = sb("deg", [128, TILES])
        rdeg = sb("rdeg", [128, TILES])
        count = sb("count", [128, TILES])
        dinv = sb("dinv", [128, TILES])
        now_i = sb("now_i", [128, PT], I32)
        now_v = sb("now_v", [128, PT], I32)
        got_v = sb("got_v", [128, PT])
        gi = sb("gi", [128, U, 2 * TPG], I32)

        units = sb("units", [128, 75, GW])
        near = units[0:RR, 0:2, :].rearrange("p a (b w) -> p (a b) w", w=RW)
        rowf = units[0:RR, 2:6, :].rearrange("p a (b w) -> p (a b) w", w=RW)
        def lent(unit, parts, shape, dt=F32):
            size = int(np.prod(shape)) * (2 if dt == BF16 else 4) // 4
            flat = units[0:parts, unit:unit + -(-size // GW), :].rearrange("p a b -> p (a b)")[:, 0:size]
            flat = flat if dt == F32 else flat.bitcast(dt)
            names = "abc"[:len(shape)]
            return flat.rearrange(f"p ({' '.join(names)}) -> p {' '.join(names)}", **dict(zip(names, shape)))

        wn = lent(40, 128, (12, F))
        pt = lent(43, 128, (LAYERS, F))
        wc = lent(44, 128, (3, F))
        near_i = lent(45, RR, (3, RW), I32)
        pad_i = lent(47, 1, (SLOTS - EDGES + 2,), I32)
        src_i = lent(49, RR, (RW,), I32)
        bias_src = lent(50, 3, (2, F))
        bias_part = lent(51, 3, (3, 2, F))
        bias_rest = lent(53, 3, (2, F))
        bias_bf = lent(54, 3, (2, F), BF16)
        flag_row = [units[0:RR, 6 + n, 0:RW // 2].bitcast(BF16) for n in range(4)]

        def ring(n):
            return [units[:, n * U + k, :] for k in range(U)]

        mask_a = sb("mask_a", [128, U, GW], BF16)
        mask_b = sb("mask_b", [128, U, GW], BF16)
        mx = sb("mx", [128, U, GW + 1])
        junk = sb("junk", [128, GW])
        st0 = sb("st0", [128, U, TPG, 6])
        st2 = sb("st2", [128, U, TPG, 6])
        mv2 = sb("mv2", [128, U, TPG, 2])
        sd2 = sb("sd2", [128, U, TPG])
        rs2 = sb("rs2", [128, U, TPG])
        nm2 = sb("nm2", [128, U, TPG])
        st1 = sb("st1", [128, U, TPG, 6])
        mv0 = sb("mv0", [128, U, TPG, 2])
        mv1 = sb("mv1", [128, U, TPG, 2])
        sd0 = sb("sd0", [128, U, TPG])
        sd1 = sb("sd1", [128, U, TPG])
        sdz = sb("sdz", [128, U, TPG])
        nm0 = sb("nm0", [128, U, TPG])
        nm1 = sb("nm1", [128, U, TPG])
        rs0 = sb("rs0", [128, U, TPG])
        rs1 = sb("rs1", [128, U, TPG])
        rsz = sb("rsz", [128, U, TPG])
        ssq = sb("ssq", [128, U, TPG])
        rdg = sb("rdg", [128, U, TPG])
        lastg = sb("lastg", [128, U, TPG])
        rden = sb("rden", [128, U, TPG * HEADS])

        bank = [ctx.enter_context(nc.psum_tensor(f"bank{n}", [128, GW], F32)) for n in range(6)]
        wide = ctx.enter_context(nc.psum_tensor("wide", [128, 2 * GW], F32))

        def by_tile(t):
            return t.rearrange("p (j f) -> p j f", j=TPG)

        s_const, s_w, s_pad, s_padded = sem("s_const"), sem("s_w"), sem("s_pad"), sem("s_padded")
        s_near, s_setup, s_rows, s_rowsT = sem("s_near"), sem("s_setup"), sem("s_rows"), sem("s_rowsT")
        s_flags, s_cols, s_act = sem("s_flags"), sem("s_cols"), sem("s_act")
        s_wc, s_wcT, s_wt = sem("s_wc"), sem("s_wcT"), sem("s_wt")
        s_far, s_init, s_placed, s_tails = sem("s_far"), sem("s_init"), sem("s_placed"), sem("s_tails")
        s_idx, s_deg, s_got, s_slot, s_from = sem("s_idx"), sem("s_deg"), sem("s_got"), sem("s_slot"), sem("s_from")
        s_stage, s_sd, s_dinv = sem("s_stage"), sem("s_sd"), sem("s_dinv")
        s_gate = {e: sem(f"s_gate_{e}") for e in ("dve", "pool", "sp")}

        def hold(eng, name):
            eng.sem_inc(s_gate[name], 1)

        raised = {}

        def signal(name, total=GROUPS):
            handle, base = raised.get(name) or (sem(name), 0)
            raised[name] = (handle, base + total)
            return Signal(handle, base)

        def signals(names, total=GROUPS):
            return [signal(name, total) for name in names.split()]

        def by_slot(name, per_group, groups=GROUPS):
            return [signal(f"{name}{k}", per_group * groups // U) for k in range(U)]

        RUN_A, RUN_S, RUN_B = (0, EARLY), (EARLY, GROUPS), (EARLY + GROUPS, NODE_GROUPS - EARLY)
        NODE_STEPS = GROUPS + NODE_GROUPS

        class Node:
            bn0, mv0, sd0, rs0, nm0, xn0, xb = signals("stats0 moments0 root0 scale0 shift0 normed0 x_beta", NODE_STEPS)
            t0, h0, z, ssq, sdz, rsz, w = signals("turned0 relu0 z z_squares z_root z_scale z_scaled", NODE_STEPS)
            x1, bn1, mv1, sd1, rs1, nm1, xn1 = signals("x1 stats1 moments1 root1 scale1 shift1 normed1", NODE_STEPS)
            t1, h1, x3, xo = signals("turned1 relu1 gcn_product x_out", NODE_STEPS)
            idx, sum1, cnt, ts, nb = signals("indices source_sums edge_counts sums_turned means")
            bn2, mv2, sd2, rs2, nm2, xn2, t2, h2 = signals("stats2 moments2 root2 scale2 shift2 normed2 turned2 relu2")
            msg, mr, nt, ntr = signals("message message_rows nt nt_rows")
            load, store = by_slot("load", 16, NODE_GROUPS), by_slot("store", 16, NODE_GROUPS)
            gather, mask, sum_store = by_slot("gathered", 64), by_slot("flags", 16), by_slot("sums_stored", 32)
            h1_store, msg_store, nt_store = by_slot("h1_stored", 16), by_slot("message_stored", 16), by_slot("nt_stored", 16)

        X, XB, XN0, H0T, X1, XN1, H1T, XO = [ring(n) for n in range(8)]
        SUM1T, CNT, NBR, XN2, H2T, NTR, MR = [ring(n) for n in range(8, 15)]

        def node_rows(tab, n):
            return tab[ds(n * NG, NG), :].rearrange("(p j) f -> p j f", j=TPG)

        class Dest:
            load, gather, store, idx = by_slot("load", 32), by_slot("gathered", 128), by_slot("store", 48), signal("indices", 2 * GROUPS)
            bn0, mv0, sd0, rs0, nm0, xn0, xb = signals("stats0 moments0 root0 scale0 shift0 normed0 x_beta")
            tn, sum2, t0, h0, z, zs, zm = signals("turned2 scanned turned0 relu0 z z_mean z_whole")
            ssq, sdz, rsz, w = signals("z_squares z_root z_scale z_scaled")
            x1, bn1, mv1, sd1, rs1, nm1, xn1, t1, h1 = signals("x1 stats1 moments1 root1 scale1 shift1 normed1 turned1 relu1")
            msg, mr, own, ownr = signals("message message_rows own own_kept")

        NBG, XD, S1L, XBD, XN0D, H0D, S2T, ZS, ZM, X1D, XN1D, H1D, MD, OD = [ring(n) for n in range(14)]

        class Conv:
            fill, load, x1_load = by_slot("flags", 16), by_slot("load", 32, LAYERS * GROUPS), by_slot("flags", 16)
            gather, store, idx = by_slot("gathered", 64, LAYERS * GROUPS), by_slot("store", 32, LAYERS * GROUPS), signal("indices", LAYERS * GROUPS)
            tm, scan, add, yn = signals("turned0 scanned with_own relu1", LAYERS * GROUPS)
            msg, mr, own, ownr = signals("message message_rows own own_kept", (LAYERS - 1) * GROUPS)
            tb, x2, bn, mv, sd, rs, rd, nm, g = signals("turned1 x_out stats0 moments0 root0 scale0 scale1 shift0 normed0")

        MG, OL, SC, AD, YN, MRN, OWN, X1L, X2, G2 = [ring(n) for n in range(10)]

        class Gcn:
            fill, load, gather, store = by_slot("flags", 16), by_slot("load", 48), by_slot("gathered", 64), by_slot("store", 48)
            idx, tg, gt, scan, u, w, xb, x3, td = signals("indices turned0 relu0 scanned with_own gcn_product x_beta x_out own_turned")
            last, bn, mv, sd, rs, nm, xn, t1, h1 = signals("last_kept stats1 moments1 root1 scale1 shift1 normed1 turned1 relu1")
            x3m, nt, ntr, ntm = signals("x3_last nt nt_rows nt_last")

        GG, GD, X2L, GTs, SG, UG, XB2, X3, X3M, XN3, H3T, NT3, NTM = [ring(n) for n in range(13)]

        class Gat:
            fill, load, neg_load = by_slot("flags", 16), by_slot("load", 48), by_slot("sums_stored", 16)
            gather, scatter, idx, out_idx = by_slot("gathered", 64), by_slot("scattered", 64), signal("indices"), signal("out_indices")
            ts, nts, lks, td, spread, ntd, lkd = signals("turned0 nt_rows leaky_source turned1 nt_spread nt_dest leaky_dest")
            lg, lgs, tx, xscan, txb = signals("logits_sum logits turned2 x3_spread x3_rows")
            mscan, diff, drop, sub, ec, ep = signals("scanned max_diff max_drop exponent decay weight")
            den, pn, num, tden, tnum = signals("denominator weighted numerator denominator_turned numerator_turned")
            rden, ratio, oe = signals("scale0 attended x_out")

        NS, NM, XM, NTS, LKS, NDT, NTD, LKD, X3T, LGS, CE, PE_, DEN, NUM, OE = [ring(n) for n in range(15)]
        MX = [mx[:, k, :] for k in range(U)]

        def stats(dve, source, st, mv, s_bn, s_mv, n, P):
            for j in range(TPG):
                last = dve.bn_stats(st[:P, j, :], source[:P, j * F:(j + 1) * F])
            last.then_inc(s_bn.sem, 1)
            done(dve, s_bn, n)
            hold(dve, "dve")
            for j in range(TPG):
                last = dve.bn_aggr(mv[:P, j, :], st[:P, j, :])
            last.then_inc(s_mv.sem, 1)

        def scale(dve, mv, sd, rs, nm, s_sd_, s_rs, s_nm, n, P=128):
            done(dve, s_sd_, n)
            dve.reciprocal(rs[:P, :], sd[:P, :]).then_inc(s_rs.sem, 1)
            done(dve, s_rs, n)
            dve.scalar_tensor_tensor(nm[:P, :], mv[:P, :, 0], -1.0, rs[:P, :], ALU.mult, ALU.mult).then_inc(s_nm.sem, 1)

        def norm_rows(act, result, source, rs, nm, s_nm, s_xn, n, P=128):
            done(act, s_nm, n)
            for j in range(TPG):
                last = act.activation(result[:P, j * F:(j + 1) * F], source[:P, j * F:(j + 1) * F], ACT.Identity,
                                      bias=nm[:P, j:j + 1], scale=rs[:P, j:j + 1])
            last.then_inc(s_xn.sem, 1)

        def z_bank(s, sources):
            return wide[:, 0:GW] if sources or s == 0 else wide[:, GW:] if s == 1 else bank[s + 1][:, :]

        def turn(pe, result, source, P=128):
            for j in range(TPG):
                last = pe.transpose(result[:, j * 128:j * 128 + P], source[:P, j * 128:(j + 1) * 128], ident[:P, :P])
            return last

        block = ctx.enter_context(nc.Block())

        @block.sync
        def _(sp):
            sp.wait_ge(s_pad, 2)
            sp.dma_start(dst_padded[0:1, 0:1], pad_i[0:1, 0:1]).then_inc(s_padded, 16)
            sp.dma_start(dst_padded[0:1, 1 + EDGES:], pad_i[0:1, 1:]).then_inc(s_padded, 16)
            sp.dma_start(dst_padded[0:1, 1:1 + EDGES], dst.unsqueeze(0)).then_inc(s_padded, 16)
            full = EDGES // RW
            sp.dma_start(src_i[0:full, :], src[0:full * RW].rearrange("(p w) -> p w", w=RW)).then_inc(s_near, 16)
            sp.dma_start(src_i[full:full + 1, 0:EDGES - full * RW], src[full * RW:EDGES].unsqueeze(0)).then_inc(s_near, 16)
            sp.wait_ge(s_padded, 48)
            for n in range(3):
                sp.dma_start(near_i[:, n, :], dst_padded[0, n:n + SLOTS].rearrange("(p w) -> p w", w=RW)).then_inc(s_near, 16)
            for n, w in enumerate((w_self, w_nb1, w_hp, w_nb2)):
                sp.dma_start(wn[:, n, :], w).then_inc(s_w, 16)
            sp.dma_start(wn[:, 4:8, :], theta_w.rearrange("l o i -> o l i")).then_inc(s_w, 16)
            sp.dma_start(wn[:, 8:12, :], phi_w.rearrange("l o i -> o l i")).then_inc(s_w, 16)
            sp.dma_start(gcn_w_s[:, :], gcn_w).then_inc(s_w, 16)
            sp.dma_start(gat_w_s[:, :], gat_w).then_inc(s_w, 16)
            sp.dma_start(gamma_b[:, :], gamma.unsqueeze(0).partition_broadcast(128)).then_inc(s_w, 16)
            sp.dma_start(beta_b[:, :], beta.unsqueeze(0).partition_broadcast(128)).then_inc(s_w, 16)
            sp.dma_start(gcn_b_b[:, :], gcn_b.unsqueeze(0).partition_broadcast(128)).then_inc(s_w, 16)
            sp.dma_start(bias_src[:, 0, :], l0_bias.unsqueeze(0).partition_broadcast(3)).then_inc(s_w, 16)
            sp.dma_start(bias_src[:, 1, :], gcn_b.unsqueeze(0).partition_broadcast(3)).then_inc(s_w, 16)
            sp.dma_start(scale_l[:, :], logits.unsqueeze(0).partition_broadcast(128)).then_inc(s_w, 16)
            sp.dma_start(attn_b_c[:, :], attn_b.unsqueeze(0).partition_broadcast(128)).then_inc(s_w, 16)
            sp.dma_start(gat_b_c[:, :], gat_b.unsqueeze(1)).then_inc(s_w, 16)
            for l in range(LAYERS):
                sp.dma_start(conv_b[:, 0, l:l + 1], theta_b[l, :].unsqueeze(1)).then_inc(s_w, 16)
                sp.dma_start(conv_b[:, 1, l:l + 1], phi_b[l, :].unsqueeze(1)).then_inc(s_w, 16)
            for h in range(HEADS):
                for n in range(2):
                    sp.dma_start(attn_c[h * HC:(h + 1) * HC, n:n + 1], attn_w[n * HC:(n + 1) * HC, :]).then_inc(s_w, 16)
            sp.wait_ge(s_const, 6)
            for tab in (nb1_tab, message_tab[1], message_tab[2], message_tab[3]):
                sp.dma_start(tab[SLOTS:SLOTS + 1, :], zeros[0:1, :]).then_inc(s_tails, 16)
            sp.wait_ge(s_far, 1)
            sp.dma_start(slot_of_node.rearrange("(p a) o -> p (a o)", p=NP), far_i[:, :]).then_inc(s_init, 16)
            sp.wait_ge(s_rows, 1)
            for tab, row in zip(flags_d, flag_row):
                sp.dma_start(tab[0, :].rearrange("(p w) -> p w", w=RW), row).then_inc(s_flags, 16)
            sp.wait_ge(s_flags, 64)
            sp.wait_ge(s_cols, 1)

            def node_load(base, first):
                def phase(g, s, q):
                    n = base + g
                    freed(sp, Node.xn0, n, U)
                    freed(sp, Node.xb, n, U)
                    hold(sp, "sp")
                    sp.dma_start(by_tile(X[s])[:NP], node_rows(x, first + g)).then_inc(Node.load[s].sem, 16)
                return phase

            def node_store(base, first):
                def phase(g, s, q):
                    done(sp, Node.xo, base + g)
                    hold(sp, "sp")
                    sp.dma_start(node_rows(out, first + g), by_tile(XO[s])[:NP]).then_inc(Node.store[s].sem, 16)
                return phase

            def source_flags(g, s, q):
                freed(sp, Node.cnt, g, U)
                hold(sp, "sp")
                sp.dma_start(mask_a[:, s, :], flags_of(same_prev_d, g)).then_inc(Node.mask[s].sem, 16)

            def source_store(g, s, q):
                n = RUN_S[0] + g
                done(sp, Node.sum1, g)
                hold(sp, "sp")
                sp.dma_start(cols_of(sum1T_tab, g), SUM1T[s]).then_inc(Node.sum_store[s].sem, 16)
                done(sp, Node.xn1, n)
                hold(sp, "sp")
                sp.dma_start(rows_of(h1_local, g), by_tile(XN1[s])).then_inc(Node.h1_store[s].sem, 16)
                done(sp, Node.nb, g)
                hold(sp, "sp")
                sp.dma_start(rows_of(nb1_tab, g), by_tile(NBR[s])).then_inc(Node.sum_store[s].sem, 16)

            def message_store(g, s, q):
                done(sp, Node.mr, g)
                hold(sp, "sp")
                sp.dma_start(rows_of(message_local, g), by_tile(MR[s])).then_inc(Node.msg_store[s].sem, 16)

            def nt_store(g, s, q):
                done(sp, Node.ntr, g)
                hold(sp, "sp")
                sp.dma_start(rows_of(nt_local, g), by_tile(NTR[s])).then_inc(Node.nt_store[s].sem, 16)

            pipelined(sp, RUN_A[1], [(0, node_load(RUN_A[0], 0)), (11, node_store(RUN_A[0], 0))])
            pipelined(sp, GROUPS, [(0, source_flags), (7, source_store), (9, message_store), (14, nt_store)])
            pipelined(sp, RUN_B[1], [(0, node_load(RUN_B[0], EARLY)), (11, node_store(RUN_B[0], EARLY))])
            for k in range(U):
                reached(sp, Node.store[k], 16 * (NODE_GROUPS // U))
                reached(sp, Node.msg_store[k], 16 * (GROUPS // U))
                reached(sp, Node.nt_store[k], 16 * (GROUPS // U))
                reached(sp, Node.sum_store[k], 32 * (GROUPS // U))
                reached(sp, Node.h1_store[k], 16 * (GROUPS // U))
            sp.wait_ge(s_tails, 64)
            sp.wait_ge(s_dinv, 1)
            sp.sem_inc(s_stage, 1)

            def dest_load(g, s, q):
                freed(sp, Dest.sum2, g, U)
                hold(sp, "sp")
                sp.dma_start(mask_a[:, s, :], flags_of(same_prev_d, g)).then_inc(Dest.load[s].sem, 16)
                freed(sp, Dest.z, g, U)
                hold(sp, "sp")
                sp.dma_start(S1L[s], cols_of(sum1T_tab, g)).then_inc(Dest.load[s].sem, 16)

            def dest_store(g, s, q):
                done(sp, Dest.x1, g)
                hold(sp, "sp")
                sp.dma_start(rows_of(x1_tab, g), by_tile(X1D[s])).then_inc(Dest.store[s].sem, 16)
                done(sp, Dest.mr, g)
                hold(sp, "sp")
                sp.dma_start(rows_of(message_tab[0], g), by_tile(MD[s])).then_inc(Dest.store[s].sem, 16)
                done(sp, Dest.ownr, g)
                hold(sp, "sp")
                sp.dma_start(cols_of(ownT_tab[0], g), OD[s]).then_inc(Dest.store[s].sem, 16)

            pipelined(sp, GROUPS, [(0, dest_load), (8, dest_store)])
            for k in range(U):
                reached(sp, Dest.store[k], 48 * (GROUPS // U))
            sp.sem_inc(s_stage, 1)

            for l in range(LAYERS):
                def conv_load(g, s, q, l=l):
                    n = l * GROUPS + g
                    if l == 0:
                        freed(sp, Conv.tm, n, U)
                        hold(sp, "sp")
                        sp.dma_start(by_tile(MG[s]), rows_of(message_local, g)).then_inc(Conv.fill[s].sem, 16)
                    freed(sp, Conv.scan, n, U)
                    hold(sp, "sp")
                    sp.dma_start(mask_a[:, s, :], flags_of(neg_prev_d, g)).then_inc(Conv.load[s].sem, 16)
                    freed(sp, Conv.add, n, U)
                    hold(sp, "sp")
                    sp.dma_start(OL[s], cols_of(ownT_tab[l], g)).then_inc(Conv.load[s].sem, 16)
                    if l == LAYERS - 1:
                        freed(sp, Conv.x2, g, U)
                        hold(sp, "sp")
                        sp.dma_start(by_tile(X1L[s]), rows_of(x1_tab, g)).then_inc(Conv.x1_load[s].sem, 16)

                def conv_store(g, s, q, l=l):
                    n = l * GROUPS + g
                    if l < LAYERS - 1:
                        done(sp, Conv.mr, n)
                        hold(sp, "sp")
                        sp.dma_start(rows_of(message_tab[l + 1], g), by_tile(MRN[s])).then_inc(Conv.store[s].sem, 16)
                        done(sp, Conv.ownr, n)
                        hold(sp, "sp")
                        sp.dma_start(cols_of(ownT_tab[l + 1], g), OWN[s]).then_inc(Conv.store[s].sem, 16)
                    else:
                        done(sp, Conv.x2, g)
                        hold(sp, "sp")
                        sp.dma_start(rows_of(x2_tab, g), by_tile(X2[s])).then_inc(Conv.store[s].sem, 16)
                        done(sp, Conv.g, g)
                        hold(sp, "sp")
                        sp.dma_start(rows_of(g_tab, g), by_tile(G2[s])).then_inc(Conv.store[s].sem, 16)

                pipelined(sp, GROUPS, [(0, conv_load), (5, conv_store)])
                for k in range(U):
                    reached(sp, Conv.store[k], 32 * (l + 1) * (GROUPS // U))
                sp.sem_inc(s_stage, 1)

            def gcn_load(g, s, q):
                freed(sp, Gcn.tg, g, U)
                hold(sp, "sp")
                sp.dma_start(by_tile(GG[s]), rows_of(h1_local, g)).then_inc(Gcn.fill[s].sem, 16)
                sp.dma_start(by_tile(GD[s]), rows_of(g_tab, g)).then_inc(Gcn.load[s].sem, 16)
                freed(sp, Gcn.scan, g, U)
                hold(sp, "sp")
                sp.dma_start(mask_a[:, s, :], flags_of(same_prev_d, g)).then_inc(Gcn.load[s].sem, 16)
                freed(sp, Gcn.xb, g, U)
                hold(sp, "sp")
                sp.dma_start(by_tile(X2L[s]), rows_of(x2_tab, g)).then_inc(Gcn.load[s].sem, 16)

            def gcn_store(g, s, q):
                done(sp, Gcn.x3m, g)
                hold(sp, "sp")
                sp.dma_start(rows_of(x3_last_tab, g), by_tile(X3M[s])).then_inc(Gcn.store[s].sem, 16)
                done(sp, Gcn.ntr, g)
                hold(sp, "sp")
                sp.dma_start(rows_of(nt_tab, g), by_tile(NT3[s])).then_inc(Gcn.store[s].sem, 16)
                done(sp, Gcn.ntm, g)
                hold(sp, "sp")
                sp.dma_start(rows_of(nt_last_tab, g), by_tile(NTM[s])).then_inc(Gcn.store[s].sem, 16)

            pipelined(sp, GROUPS, [(0, gcn_load), (7, gcn_store)])
            for k in range(U):
                reached(sp, Gcn.store[k], 48 * (GROUPS // U))
            sp.sem_inc(s_stage, 1)

            def gat_load(g, s, q):
                G = GROUPS - 1 - g
                freed(sp, Gat.ts, g, U)
                hold(sp, "sp")
                sp.dma_start(by_tile(NS[s]), rows_of(nt_local, G)).then_inc(Gat.fill[s].sem, 16)
                freed(sp, Gat.td, g, U)
                hold(sp, "sp")
                sp.dma_start(by_tile(NM[s]), rows_of(nt_last_tab, G)).then_inc(Gat.load[s].sem, 16)
                freed(sp, Gat.spread, g, U)
                freed(sp, Gat.xscan, g, U)
                hold(sp, "sp")
                sp.dma_start(mask_a[:, s, :], flags_of(same_next_d, G)).then_inc(Gat.load[s].sem, 16)
                freed(sp, Gat.tx, g, U)
                hold(sp, "sp")
                sp.dma_start(by_tile(XM[s]), rows_of(x3_last_tab, G)).then_inc(Gat.load[s].sem, 16)
                freed(sp, Gat.drop, g, U)
                hold(sp, "sp")
                sp.dma_start(mask_b[:, s, :], flags_of(neg_next_d, G)).then_inc(Gat.neg_load[s].sem, 16)

            pipelined(sp, GROUPS, [(0, gat_load)])

        @block.gpsimd
        def _(pool):
            pool.memset(ident[:, :], 0.0).then_inc(s_const, 1)
            pool.memset(head_mask[:, :], 1.0).then_inc(s_const, 1)
            pool.memset(zeros[:, :], 0.0).then_inc(s_const, 1)
            pool.memset(ones[:, :], 1.0).then_inc(s_const, 1)
            pool.memset(eps[:, :], EPS).then_inc(s_const, 1)
            pool.memset(ones3[:, :], 1.0).then_inc(s_const, 1)
            pool.wait_ge(s_const, 6)
            pool.affine_select(out=ident[:, :], in_=ident[:, :], compare_op=ALU.not_equal, fill=1.0,
                               base=0, pattern=[[-1, 128]], channel_multiplier=1).then_inc(s_const, 1)
            pool.affine_select(out=head_mask[:, :], in_=head_mask[:, :], compare_op=ALU.is_ge, fill=0.0,
                               base=0, pattern=[[-HC, HEADS], [0, HC]], channel_multiplier=1).then_inc(s_const, 1)
            pool.wait_ge(s_const, 8)
            pool.affine_select(out=head_mask[:, :], in_=head_mask[:, :], compare_op=ALU.is_ge, fill=0.0,
                               base=HC - 1, pattern=[[HC, HEADS], [0, HC]], channel_multiplier=-1).then_inc(s_const, 1)
            pool.iota(slot_i[:, :], pattern=[[128, TILES]], base=0, channel_multiplier=1).then_inc(s_const, 1)
            pool.wait_ge(s_cols, 1)

            with pool.Fori(0, TILES // PT) as i:
                pool.tensor_copy(now_i[:, :], dst_i[:, ds(i * PT, PT)]).then_inc(s_idx, 1)
                pool.wait_ge(s_idx, i + 1)
                hold(pool, "pool")
                for k in range(PT):
                    pool.indirect_dma_start(out=got_v[:, k:k + 1], out_offset=None, in_=node_vec.unsqueeze(1),
                                            in_offset=bass.IndirectOffsetOnAxis(ap=now_i[:, k:k + 1], axis=0)
                                            ).then_inc(s_got, 16)
                pool.wait_ge(s_got, (i + 1) * (16 * PT))
                hold(pool, "pool")
                pool.tensor_copy(deg[:, ds(i * PT, PT)], got_v[:, :]).then_inc(s_deg, 1)
                pool.wait_ge(s_deg, i + 1)
                hold(pool, "pool")

            def gather4(s, rows, table, gathered, limit=None, at=0):
                for j in range(TPG):
                    kw = {} if limit is None else {"bounds_check": limit, "oob_is_err": False}
                    pool.indirect_dma_start(out=rows[s][:, j * F:(j + 1) * F], out_offset=None, in_=table,
                                            in_offset=bass.IndirectOffsetOnAxis(ap=gi[:, s, at + j:at + j + 1], axis=0),
                                            **kw).then_inc(gathered[s].sem, 16)

            def source_gather(g, s, q):
                freed(pool, Node.xn0, RUN_S[0] + g, U)
                freed(pool, Node.xb, RUN_S[0] + g, U)
                hold(pool, "pool")
                pool.tensor_copy(gi[:, s, 0:TPG], src_c[:, ds(g * TPG, TPG)]).then_inc(Node.idx.sem, 1)
                done(pool, Node.idx, g)
                hold(pool, "pool")
                gather4(s, X, x, Node.gather)

            pipelined(pool, GROUPS, [(0, source_gather)])

            pool.wait_ge(s_init, 16)
            with pool.Fori(0, TILES // PT) as i:
                pool.tensor_copy(now_i[:, :], last_i[:, ds(i * PT, PT)]).then_inc(s_slot, 1)
                pool.tensor_copy(now_v[:, :], slot_i[:, ds(i * PT, PT)]).then_inc(s_slot, 1)
                pool.wait_ge(s_slot, i * 2 + 2)
                hold(pool, "pool")
                for k in range(PT):
                    pool.indirect_dma_start(out=slot_of_node, out_offset=bass.IndirectOffsetOnAxis(ap=now_i[:, k:k + 1], axis=0),
                                            in_=now_v[:, k:k + 1], in_offset=None,
                                            bounds_check=NODES - 1, oob_is_err=False).then_inc(s_placed, 16)
                pool.wait_ge(s_placed, (i + 1) * (16 * PT))
                hold(pool, "pool")
            with pool.Fori(0, TILES // PT) as i:
                pool.tensor_copy(now_i[:, :], src_c[:, ds(i * PT, PT)]).then_inc(s_from, 1)
                pool.wait_ge(s_from, i * 2 + 1)
                hold(pool, "pool")
                for k in range(PT):
                    pool.indirect_dma_start(out=now_v[:, k:k + 1], out_offset=None, in_=slot_of_node,
                                            in_offset=bass.IndirectOffsetOnAxis(ap=now_i[:, k:k + 1], axis=0)
                                            ).then_inc(s_got, 16)
                pool.wait_ge(s_got, (i + 1 + TILES // PT) * (16 * PT))
                hold(pool, "pool")
                pool.tensor_copy(from_i[:, ds(i * PT, PT)], now_v[:, :]).then_inc(s_from, 1)
                pool.wait_ge(s_from, i * 2 + 2)
                hold(pool, "pool")

            pool.wait_ge(s_stage, 1)

            def dest_gather(g, s, q):
                freed(pool, Dest.tn, g, U)
                freed(pool, Dest.xn0, g, U)
                freed(pool, Dest.xb, g, U)
                hold(pool, "pool")
                pool.tensor_copy(gi[:, s, 0:TPG], from_i[:, ds(g * TPG, TPG)]).then_inc(Dest.idx.sem, 1)
                pool.tensor_copy(gi[:, s, TPG:], dst_i[:, ds(g * TPG, TPG)]).then_inc(Dest.idx.sem, 1)
                reached(pool, Dest.idx, g * 2 + 2)
                hold(pool, "pool")
                gather4(s, NBG, nb1_tab, Dest.gather)
                gather4(s, XD, x, Dest.gather, at=TPG)

            pipelined(pool, GROUPS, [(0, dest_gather)])

            for l in range(LAYERS):
                pool.wait_ge(s_stage, 2 + l)

                def conv_gather(g, s, q, l=l):
                    n = l * GROUPS + g
                    freed(pool, Conv.tm, n, U)
                    if l == 0:
                        reached(pool, Conv.fill[s], q * 16 + 16)
                    hold(pool, "pool")
                    pool.tensor_copy(gi[:, s, 0:TPG], from_i[:, ds(g * TPG, TPG)]).then_inc(Conv.idx.sem, 1)
                    done(pool, Conv.idx, n)
                    hold(pool, "pool")
                    gather4(s, MG, message_tab[l], Conv.gather, limit=SLOTS - 1 if l == 0 else None)

                pipelined(pool, GROUPS, [(0, conv_gather)])

            pool.wait_ge(s_stage, 2 + LAYERS)

            def gcn_gather(g, s, q):
                reached(pool, Gcn.fill[s], q * 16 + 16)
                hold(pool, "pool")
                pool.tensor_copy(gi[:, s, 0:TPG], from_i[:, ds(g * TPG, TPG)]).then_inc(Gcn.idx.sem, 1)
                done(pool, Gcn.idx, g)
                hold(pool, "pool")
                gather4(s, GG, g_tab, Gcn.gather, limit=SLOTS - 1)

            pipelined(pool, GROUPS, [(0, gcn_gather)])

            pool.wait_ge(s_stage, 3 + LAYERS)

            def gat_gather(g, s, q):
                reached(pool, Gat.fill[s], q * 16 + 16)
                hold(pool, "pool")
                pool.tensor_copy(gi[:, s, 0:TPG], from_i[:, ds((GROUPS - 1 - g) * TPG, TPG)]).then_inc(Gat.idx.sem, 1)
                done(pool, Gat.idx, g)
                hold(pool, "pool")
                gather4(s, NS, nt_tab, Gat.gather, limit=SLOTS - 1)

            def gat_scatter(g, s, q):
                if not isinstance(g, int) or g >= U:
                    reached(pool, Gat.scatter[s], q * 64)
                    hold(pool, "pool")
                pool.tensor_copy(gi[:, s, TPG:], first_i[:, ds((GROUPS - 1 - g) * TPG, TPG)]).then_inc(Gat.out_idx.sem, 1)
                done(pool, Gat.out_idx, g)
                done(pool, Gat.oe, g)
                hold(pool, "pool")
                for j in range(TPG):
                    pool.indirect_dma_start(out=out, out_offset=bass.IndirectOffsetOnAxis(ap=gi[:, s, TPG + j:TPG + j + 1], axis=0),
                                            in_=OE[s][:, j * F:(j + 1) * F], in_offset=None,
                                            bounds_check=NODES - 1, oob_is_err=False).then_inc(Gat.scatter[s].sem, 16)

            pipelined(pool, GROUPS, [(0, gat_gather), (8, gat_scatter)])
            for k in range(U):
                reached(pool, Gat.scatter[k], 64 * (GROUPS // U))

        @block.vector
        def _(dve):
            link_count = [0]

            def link(ins):
                link_count[0] += 1
                ins.then_inc(s_setup, 1)
                dve.wait_ge(s_setup, link_count[0])

            link(dve.memset(pad_i[0:1, :], NOWHERE))
            link(dve.memset(pad_i[0:1, 0:1], -1))
            dve.memset(src_i[:, :], 0).then_inc(s_pad, 1)
            dve.memset(near_i[:, :, :], 0).then_inc(s_pad, 1)
            dve.memset(far_i[:, :], SLOTS).then_inc(s_far, 1)
            dve.wait_ge(s_near, 80)
            for n in range(3):
                dve.tensor_copy(near[:, n, :], near_i[:, n, :])
            link(dve.tensor_copy(near[:, 3, :], src_i[:, :]))
            before, itself, behind = near[:, 0, :], near[:, 1, :], near[:, 2, :]
            dve.tensor_tensor(rowf[:, 0, :], itself, before, ALU.is_equal)
            link(dve.tensor_tensor(rowf[:, 1, :], itself, behind, ALU.is_equal))
            dve.tensor_scalar(rowf[:, 2, :], rowf[:, 1, :], -1.0, 1.0, ALU.mult, ALU.add)
            dve.tensor_scalar(rowf[:, 3, :], rowf[:, 0, :], -1.0, 1.0, ALU.mult, ALU.add)
            dve.tensor_copy(flag_row[0], rowf[:, 0, :])
            dve.tensor_scalar(flag_row[1], rowf[:, 0, :], -1.0, NEG, ALU.add, ALU.mult)
            dve.tensor_copy(flag_row[2], rowf[:, 1, :])
            link(dve.tensor_scalar(flag_row[3], rowf[:, 1, :], -1.0, NEG, ALU.add, ALU.mult))
            dve.scalar_tensor_tensor(rowf[:, 4, :], itself, -float(NOWHERE), rowf[:, 2, :], ALU.add, ALU.mult)
            dve.scalar_tensor_tensor(rowf[:, 5, :], itself, -float(NOWHERE), rowf[:, 3, :], ALU.add, ALU.mult)
            link(dve.tensor_scalar(rowf[:, 6, :], itself, float(NODES - 1), None, ALU.min))
            dve.tensor_scalar(rowf[:, 4, :], rowf[:, 4, :], float(NOWHERE), None, ALU.add)
            dve.tensor_scalar(rowf[:, 5, :], rowf[:, 5, :], float(NOWHERE), None, ALU.add).then_inc(s_rows, 1)
            for n, dest in enumerate((last_i, first_i, dst_i, src_c, is_last)):
                dve.wait_ge(s_rowsT, n + 1)
                last = dve.tensor_copy(dest[:, :].rearrange("p (a b) -> p b a", b=2),
                                       bank[n][:, 0:2 * RR].rearrange("p (b a) -> p b a", b=2))
            last.then_inc(s_cols, 1)
            dve.wait_ge(s_act, 1)
            dve.wait_ge(s_w, 16 * (16 + 2 * LAYERS + 2 * HEADS))
            link(dve.tensor_scalar(scale_2[:, 0:4], scale_s[:, :], 2.0, None, ALU.mult))
            link(dve.tensor_scalar(scale_2[:, 4:5], scale_2[:, 2:3], -1.0, None, ALU.mult))
            dve.tensor_scalar(wc[:, 0, :], wn[:, 2, :], scale_2[:, 2:3], None, ALU.mult)
            dve.tensor_scalar(wc[:, 1, :], wn[:, 2, :], scale_2[:, 4:5], None, ALU.mult)
            link(dve.tensor_scalar(wc[:, 2, :], wn[:, 3, :], scale_2[:, 3:4], None, ALU.mult))
            dve.scalar_tensor_tensor(wc[:, 0, :], wn[:, 0, :], scale_2[:, 0:1], wc[:, 0, :], ALU.mult, ALU.add)
            dve.scalar_tensor_tensor(wc[:, 1, :], wn[:, 1, :], scale_2[:, 1:2], wc[:, 1, :], ALU.mult, ALU.add)
            dve.tensor_tensor(pt[:, :, :], wn[:, 8:12, :], wn[:, 4:8, :], ALU.subtract).then_inc(s_wc, 1)
            dve.wait_ge(s_wcT, 1)
            for n in range(3):
                last = dve.reduce_sum(small[:, n:n + 1], bank[0][:, n * F:(n + 1) * F], axis=AX.X)
            link(last)
            link(dve.reduce_sum(small[0:3, 3:4], bias_src[:, 0, :], axis=AX.X))
            link(dve.tensor_scalar(small[:, 0:3], small[:, 0:3], 1.0 / F, None, ALU.mult))
            link(dve.tensor_scalar(small[0:3, 3:4], small[0:3, 3:4], 1.0 / F, None, ALU.mult))
            for n in range(3):
                dve.tensor_scalar(wT[:, n, :], bank[0][:, n * F:(n + 1) * F], small[:, n:n + 1], None, ALU.subtract)
            link(dve.tensor_scalar(bias_src[:, 0, :], bias_src[:, 0, :], small[0:3, 3:4], None, ALU.subtract))
            link(dve.tensor_copy(bias_bf[:, :, :], bias_src[:, :, :]))
            link(dve.tensor_copy(bias_part[:, 0, :, :], bias_bf[:, :, :]))
            link(dve.tensor_tensor(bias_rest[:, :, :], bias_src[:, :, :], bias_part[:, 0, :, :], ALU.subtract))
            link(dve.tensor_copy(bias_bf[:, :, :], bias_rest[:, :, :]))
            link(dve.tensor_copy(bias_part[:, 1, :, :], bias_bf[:, :, :]))
            link(dve.tensor_tensor(bias_part[:, 2, :, :], bias_rest[:, :, :], bias_part[:, 1, :, :], ALU.subtract))
            dve.wait_ge(s_const, 9)
            link(dve.tensor_scalar(bias_rest[:, :, :], bias_part[:, 0, :, :], ident[0:3, 0:1], None, ALU.mult))
            for k in (1, 2):
                link(dve.scalar_tensor_tensor(bias_rest[:, :, :], bias_part[:, k, :, :], ident[0:3, k:k + 1], bias_rest[:, :, :],
                                              ALU.mult, ALU.add))
            for j in range(TPG):
                dve.tensor_copy(bias3[:, :, j * F:(j + 1) * F], bias_rest[:, :, :])
            for n in range(2):
                dve.tensor_scalar(attn_m[:, n, :], head_mask[:, :], attn_c[:, n:n + 1], None, ALU.mult)
            dve.tensor_tensor(conv_bias[:, :], conv_b[:, 0, :], conv_b[:, 1, :], ALU.add)
            dve.tensor_copy(thetaT[:, :, :], bank[1][:, :].rearrange("p (l f) -> p l f", l=LAYERS))
            dve.tensor_copy(ptT[:, :, :], bank[2][:, :].rearrange("p (l f) -> p l f", l=LAYERS)).then_inc(s_wt, 1)

            def node_phases(base, P, sources):
                def finish(g, s, q):
                    n = base + g
                    done(dve, Node.x3, n)
                    if sources or not isinstance(g, int) or g >= U:
                        if sources:
                            reached(dve, Node.store[s], 16 * (EARLY // U))
                        else:
                            reached(dve, Node.store[s], (q + (EARLY // U if base else 0)) * 16)
                    elif base:
                        done(dve, Node.xn2, GROUPS - 1)
                    dve.tensor_tensor(XO[s][:P], X1[s][:P], bank[2][:P, :], ALU.add).then_inc(Node.xo.sem, 1)

                def measure_x(g, s, q):
                    n = base + g
                    if sources:
                        reached(dve, Node.gather[s], q * 64 + 64)
                    else:
                        reached(dve, Node.load[s], (q + (EARLY // U if base else 0)) * 16 + 16)
                    stats(dve, X[s], st0[:, s], mv0[:, s], Node.bn0, Node.mv0, n, P)
                    dve.tensor_tensor(by_tile(XB[s])[:P], by_tile(X[s])[:P], beta_b[:P, :].unsqueeze(1).broadcast_to((P, TPG, F)), ALU.add).then_inc(Node.xb.sem, 1)

                def scale_x(g, s, q):
                    scale(dve, mv0[:, s], sd0[:, s], rs0[:, s], nm0[:, s], Node.sd0, Node.rs0, Node.nm0, base + g, P)

                def layer0(g, s, q):
                    n = base + g
                    done(dve, Node.sdz, n)
                    dve.reciprocal(rsz[:P, s, :], sdz[:P, s, :]).then_inc(Node.rsz.sem, 1)
                    done(dve, Node.rsz, n)
                    for j in range(TPG):
                        last = dve.scalar_tensor_tensor(X1[s][:P, j * F:(j + 1) * F], z_bank(s, sources)[:P, j * F:(j + 1) * F], rsz[:P, s, j:j + 1],
                                                        gamma_b[:P, :], ALU.mult, ALU.mult)
                    last.then_inc(Node.w.sem, 1)
                    done(dve, Node.w, n)
                    dve.tensor_tensor(X1[s][:P], X1[s][:P], XB[s][:P], ALU.add).then_inc(Node.x1.sem, 1)
                    done(dve, Node.x1, n)
                    stats(dve, X1[s], st1[:, s], mv1[:, s], Node.bn1, Node.mv1, n, P)

                def scale_x1(g, s, q):
                    scale(dve, mv1[:, s], sd1[:, s], rs1[:, s], nm1[:, s], Node.sd1, Node.rs1, Node.nm1, base + g, P)

                def scan_sources(g, s, q):
                    n = base + g
                    done(dve, Node.h0, n)
                    reached(dve, Node.mask[s], q * 16 + 16)
                    first = isinstance(g, int) and g == 0
                    if not first:
                        reached(dve, Node.sum1, g)
                        reached(dve, Node.cnt, g)
                    if not (isinstance(g, int) and g < U):
                        reached(dve, Node.sum_store[s], q * 32)
                    before_ = (s - 1) % U
                    dve.tensor_tensor_scan(SUM1T[s], mask_a[:, s, :], H0T[s], 0.0 if first else SUM1T[before_][:, GW - 1:GW],
                                           ALU.mult, ALU.add).then_inc(Node.sum1.sem, 1)
                    dve.tensor_tensor_scan(CNT[s], mask_a[:, s, :], ones[:, :], 0.0 if first else CNT[before_][:, GW - 1:GW],
                                           ALU.mult, ALU.add).then_inc(Node.cnt.sem, 1)

                def mean_sources(g, s, q):
                    if isinstance(g, int) and g == 0:
                        dve.wait_ge(s_deg, TILES // PT)
                        link(dve.reciprocal(rdeg[:, :], deg[:, :]))
                    done(dve, Node.ts, g)
                    if not (isinstance(g, int) and g < U):
                        reached(dve, Node.sum_store[s], q * 32)
                    hold(dve, "dve")
                    for j in range(TPG):
                        dve.tensor_scalar(NBR[s][:, j * F:(j + 1) * F], bank[3][:, j * F:(j + 1) * F], rdeg[:, ds(g * TPG + j, 1)], None, ALU.mult)
                    dve.tensor_copy(count[:, ds(g * TPG, TPG)], bank[4][:, 0:TPG]).then_inc(Node.nb.sem, 1)

                def measure_x3(g, s, q):
                    stats(dve, XO[s], st2[:, s], mv2[:, s], Node.bn2, Node.mv2, g, P)

                def scale_x3(g, s, q):
                    scale(dve, mv2[:, s], sd2[:, s], rs2[:, s], nm2[:, s], Node.sd2, Node.rs2, Node.nm2, g, P)

                first = [(8, finish)] + ([(6, mean_sources)] if sources else [])
                phases = first + [(4, layer0), (0, measure_x), (1, scale_x), (5, scale_x1)]
                return phases + ([(4, scan_sources), (10, scale_x3), (9, measure_x3)] if sources else [])

            pipelined(dve, RUN_A[1], node_phases(RUN_A[0], NP, False))
            pipelined(dve, GROUPS, node_phases(RUN_S[0], 128, True))
            pipelined(dve, RUN_B[1], node_phases(RUN_B[0], NP, False))
            done(dve, Node.nb, GROUPS - 1)
            link(dve.tensor_scalar(count[:, :], count[:, :], 1.0, None, ALU.add))
            dve.sem_inc(s_sd, 1)
            dve.wait_ge(s_sd, 2)
            dve.reciprocal(dinv[:, :], dinv[:, :]).then_inc(s_dinv, 1)

            dve.wait_ge(s_stage, 1)

            def dest_measure(g, s, q):
                reached(dve, Dest.gather[s], q * 128 + 128)
                stats(dve, XD[s], st0[:, s], mv0[:, s], Dest.bn0, Dest.mv0, g, 128)
                dve.tensor_copy(rdg[:, s, :], rdeg[:, ds(g * TPG, TPG)])
                dve.tensor_tensor(by_tile(XBD[s]), by_tile(XD[s]), beta_b[:, :].unsqueeze(1).broadcast_to((128, TPG, F)), ALU.add).then_inc(Dest.xb.sem, 1)

            def dest_scan(g, s, q):
                done(dve, Dest.tn, g)
                reached(dve, Dest.load[s], q * 32 + 32)
                first = isinstance(g, int) and g == 0
                if not first:
                    reached(dve, Dest.sum2, g)
                dve.tensor_tensor_scan(S2T[s], mask_a[:, s, :], bank[0][:, :], 0.0 if first else S2T[(s - 1) % U][:, GW - 1:GW],
                                       ALU.mult, ALU.add).then_inc(Dest.sum2.sem, 1)

            def dest_scale(g, s, q):
                scale(dve, mv0[:, s], sd0[:, s], rs0[:, s], nm0[:, s], Dest.sd0, Dest.rs0, Dest.nm0, g)

            def dest_z(g, s, q):
                done(dve, Dest.zs, g)
                dve.tensor_tensor(ZM[s], ZS[s], bank[2][:, :], ALU.add).then_inc(Dest.zm.sem, 1)

            def dest_x1(g, s, q):
                done(dve, Dest.sdz, g)
                if not (isinstance(g, int) and g < U):
                    reached(dve, Dest.store[s], q * 48)
                dve.reciprocal(rsz[:, s, :], sdz[:, s, :]).then_inc(Dest.rsz.sem, 1)
                done(dve, Dest.rsz, g)
                for j in range(TPG):
                    last = dve.scalar_tensor_tensor(ZM[s][:, j * F:(j + 1) * F], ZM[s][:, j * F:(j + 1) * F], rsz[:, s, j:j + 1],
                                                    gamma_b[:, :], ALU.mult, ALU.mult)
                last.then_inc(Dest.w.sem, 1)
                done(dve, Dest.w, g)
                dve.tensor_tensor(X1D[s], ZM[s], XBD[s], ALU.add).then_inc(Dest.x1.sem, 1)
                done(dve, Dest.x1, g)
                stats(dve, X1D[s], st1[:, s], mv1[:, s], Dest.bn1, Dest.mv1, g, 128)

            def dest_scale1(g, s, q):
                scale(dve, mv1[:, s], sd1[:, s], rs1[:, s], nm1[:, s], Dest.sd1, Dest.rs1, Dest.nm1, g)

            pipelined(dve, GROUPS, [(3, dest_z), (0, dest_measure), (1, dest_scan), (1, dest_scale), (4, dest_x1), (5, dest_scale1)])

            for l in range(LAYERS):
                dve.wait_ge(s_stage, 2 + l)

                def conv_scan(g, s, q, l=l):
                    n = l * GROUPS + g
                    done(dve, Conv.tm, n)
                    reached(dve, Conv.load[s], (q + l * (GROUPS // U)) * 32 + 32)
                    first = isinstance(g, int) and g == 0
                    if not first:
                        reached(dve, Conv.scan, n)
                    dve.tensor_tensor_scan(SC[s], mask_a[:, s, :], bank[0][:, :], -NEG if first else SC[(s - 1) % U][:, GW - 1:GW],
                                           ALU.add, ALU.max).then_inc(Conv.scan.sem, 1)
                    done(dve, Conv.scan, n)
                    freed(dve, Conv.yn, n, U)
                    dve.tensor_tensor(AD[s], SC[s], OL[s], ALU.add).then_inc(Conv.add.sem, 1)

                def conv_x2(g, s, q, l=l):
                    done(dve, Conv.tb, g)
                    reached(dve, Conv.x1_load[s], q * 16 + 16)
                    if not (isinstance(g, int) and g < U):
                        reached(dve, Conv.store[s], (q + l * (GROUPS // U)) * 32)
                    dve.tensor_tensor(X2[s], X1L[s], bank[3][:, :], ALU.add).then_inc(Conv.x2.sem, 1)
                    done(dve, Conv.x2, g)
                    stats(dve, X2[s], st0[:, s], mv0[:, s], Conv.bn, Conv.mv, g, 128)

                def conv_scale(g, s, q):
                    done(dve, Conv.sd, g)
                    dve.reciprocal(rs0[:, s], sd0[:, s]).then_inc(Conv.rs.sem, 1)
                    done(dve, Conv.rs, g)
                    hold(dve, "dve")
                    dve.tensor_tensor(rs1[:, s], rs0[:, s], dinv[:, ds(g * TPG, TPG)], ALU.mult).then_inc(Conv.rd.sem, 1)
                    done(dve, Conv.rd, g)
                    dve.scalar_tensor_tensor(nm0[:, s], mv0[:, s, :, 0], -1.0, rs1[:, s], ALU.mult, ALU.mult).then_inc(Conv.nm.sem, 1)

                pipelined(dve, GROUPS, [(0, conv_scan)] + ([(3, conv_x2), (4, conv_scale)] if l == LAYERS - 1 else []))

            dve.wait_ge(s_stage, 2 + LAYERS)

            def gcn_scan(g, s, q):
                done(dve, Gcn.gt, g)
                reached(dve, Gcn.load[s], q * 48 + 48)
                first = isinstance(g, int) and g == 0
                if not first:
                    reached(dve, Gcn.scan, g)
                dve.tensor_tensor_scan(SG[s], mask_a[:, s, :], GTs[s], 0.0 if first else SG[(s - 1) % U][:, GW - 1:GW],
                                       ALU.mult, ALU.add).then_inc(Gcn.scan.sem, 1)
                done(dve, Gcn.scan, g)
                done(dve, Gcn.td, g)
                dve.tensor_tensor(UG[s], SG[s], bank[1][:, :], ALU.add).then_inc(Gcn.u.sem, 1)
                dve.tensor_tensor(by_tile(XB2[s]), by_tile(X2L[s]), gcn_b_b[:, :].unsqueeze(1).broadcast_to((128, TPG, F)), ALU.add).then_inc(Gcn.xb.sem, 1)

            def gcn_x3(g, s, q):
                done(dve, Gcn.w, g)
                done(dve, Gcn.xb, g)
                if not (isinstance(g, int) and g < U):
                    reached(dve, Gcn.x3m, g - U + 1)
                    reached(dve, Gcn.xn, g - U + 1)
                    reached(dve, Gcn.ntm, g - U + 1)
                hold(dve, "dve")
                for j in range(TPG):
                    last = dve.scalar_tensor_tensor(X3[s][:, j * F:(j + 1) * F], bank[2][:, j * F:(j + 1) * F], dinv[:, ds(g * TPG + j, 1)],
                                                    XB2[s][:, j * F:(j + 1) * F], ALU.mult, ALU.add)
                last.then_inc(Gcn.x3.sem, 1)
                dve.tensor_copy(lastg[:, s], is_last[:, ds(g * TPG, TPG)]).then_inc(Gcn.last.sem, 1)
                done(dve, Gcn.x3, g)
                stats(dve, X3[s], st1[:, s], mv1[:, s], Gcn.bn, Gcn.mv, g, 128)

            def gcn_scale(g, s, q):
                scale(dve, mv1[:, s], sd1[:, s], rs1[:, s], nm1[:, s], Gcn.sd, Gcn.rs, Gcn.nm, g)

            pipelined(dve, GROUPS, [(4, gcn_scale), (3, gcn_x3), (1, gcn_scan)])

            dve.wait_ge(s_stage, 3 + LAYERS)

            def back(t):
                return t[:, ::-1]

            def gat_leaky(g, s, q):
                done(dve, Gat.nts, g)
                freed(dve, Gat.lg, g, U)
                dve.scalar_tensor_tensor(LKS[s], NTS[s], SLOPE, NTS[s], ALU.mult, ALU.max).then_inc(Gat.lks.sem, 1)

            def gat_leaky_d(g, s, q):
                done(dve, Gat.ntd, g)
                freed(dve, Gat.lg, g, U)
                dve.scalar_tensor_tensor(LKD[s], NTD[s], SLOPE, NTD[s], ALU.mult, ALU.max).then_inc(Gat.lkd.sem, 1)

            def spread(signal_, result, rows, g, s):
                first = isinstance(g, int) and g == 0
                if not first:
                    reached(dve, signal_, g)
                dve.tensor_tensor_scan(back(result[s]), back(mask_a[:, s, :]), back(rows),
                                       0.0 if first else result[(s - 1) % U][:, 0:1], ALU.mult, ALU.add).then_inc(signal_.sem, 1)

            def gat_spread(g, s, q):
                done(dve, Gat.td, g)
                reached(dve, Gat.load[s], q * 48 + 48)
                freed(dve, Gat.ntd, g, U)
                spread(Gat.spread, NDT, bank[1][:, :], g, s)

            def gat_spread_x(g, s, q):
                done(dve, Gat.tx, g)
                freed(dve, Gat.txb, g, U)
                spread(Gat.xscan, X3T, bank[2][:, :], g, s)

            def gat_max(g, s, q):
                done(dve, Gat.lgs, g)
                reached(dve, Gat.neg_load[s], q * 16 + 16)
                first = isinstance(g, int) and g == 0
                if not first:
                    reached(dve, Gat.mscan, g)
                    dve.tensor_copy(MX[s][:, GW:GW + 1], MX[(s - 1) % U][:, 0:1])
                else:
                    dve.memset(MX[s][:, GW:GW + 1], 0.0)
                dve.tensor_tensor_scan(back(MX[s][:, 0:GW]), back(mask_b[:, s, :]), back(LGS[s]),
                                       -NEG if first else MX[(s - 1) % U][:, 0:1], ALU.add, ALU.max).then_inc(Gat.mscan.sem, 1)
                done(dve, Gat.mscan, g)
                dve.tensor_tensor(CE[s], MX[s][:, 1:GW + 1], MX[s][:, 0:GW], ALU.subtract).then_inc(Gat.diff.sem, 1)
                dve.tensor_tensor(PE_[s], LGS[s], MX[s][:, 0:GW], ALU.subtract).then_inc(Gat.sub.sem, 1)
                done(dve, Gat.diff, g)
                dve.scalar_tensor_tensor(CE[s], CE[s], 0.0, mask_b[:, s, :], ALU.min, ALU.add).then_inc(Gat.drop.sem, 1)

            def gat_sum(g, s, q):
                done(dve, Gat.ec, g)
                done(dve, Gat.ep, g)
                first = isinstance(g, int) and g == 0
                if not first:
                    reached(dve, Gat.den, g)
                dve.tensor_tensor_scan(back(DEN[s]), back(CE[s]), back(PE_[s]), 0.0 if first else DEN[(s - 1) % U][:, 0:1],
                                       ALU.mult, ALU.add).then_inc(Gat.den.sem, 1)
                if not first:
                    reached(dve, Gat.num, g)
                dve.tensor_tensor(NTS[s], PE_[s], NTS[s], ALU.mult).then_inc(Gat.pn.sem, 1)
                done(dve, Gat.pn, g)
                dve.tensor_tensor_scan(back(NUM[s]), back(CE[s]), back(NTS[s]), 0.0 if first else NUM[(s - 1) % U][:, 0:1],
                                       ALU.mult, ALU.add).then_inc(Gat.num.sem, 1)

            def gat_final(g, s, q):
                done(dve, Gat.tden, g)
                dve.reciprocal(rden[:, s], bank[4][:, 0:TPG * HEADS]).then_inc(Gat.rden.sem, 1)
                done(dve, Gat.rden, g)
                done(dve, Gat.tnum, g)
                if not (isinstance(g, int) and g < U):
                    reached(dve, Gat.scatter[s], q * 64)
                dve.tensor_tensor(OE[s].rearrange("p (h c) -> p h c", c=HC), bank[5][:, :].rearrange("p (h c) -> p h c", c=HC),
                                  rden[:, s].unsqueeze(2).broadcast_to((128, TPG * HEADS, HC)), ALU.mult).then_inc(Gat.ratio.sem, 1)
                done(dve, Gat.ratio, g)
                done(dve, Gat.txb, g)
                dve.tensor_tensor(OE[s], OE[s], bank[3][:, :], ALU.add).then_inc(Gat.oe.sem, 1)

            pipelined(dve, GROUPS, [(1, gat_spread), (1, gat_spread_x), (6, gat_final), (5, gat_sum), (4, gat_max), (1, gat_leaky),
                                    (2, gat_leaky_d)])

        @block.scalar
        def _(act):
            act.wait_ge(s_w, 16 * (16 + 2 * LAYERS + 2 * HEADS))
            act.activation(scale_s[:, :], scale_l[:, :], ACT.Sigmoid).then_inc(s_act, 1)

            def root(sd, mv, s_sd_, s_mv, n, P=128):
                done(act, s_mv, n)
                act.activation(sd[:P, :], mv[:P, :, 1], ACT.Sqrt, bias=eps[:P, :]).then_inc(s_sd_.sem, 1)

            def node_phases(base, P, sources):
                def root_x(g, s, q):
                    root(sd0[:, s], mv0[:, s], Node.sd0, Node.mv0, base + g, P)

                def turned_x(g, s, q):
                    done(act, Node.t0, base + g)
                    if base == RUN_S[0] and not (isinstance(g, int) and g < U):
                        reached(act, Node.sum1, g - U + 1)
                    act.activation(by_tile(H0T[s])[:, :, 0:P], by_tile(bank[0][:, :])[:, :, 0:P], ACT.Relu).then_inc(Node.h0.sem, 1)

                def square_z(g, s, q):
                    n = base + g
                    done(act, Node.z, n)
                    for j in range(TPG):
                        last = act.activation(junk[:P, j * F:(j + 1) * F], z_bank(s, sources)[:P, j * F:(j + 1) * F], ACT.Square, accum_out=ssq[:P, s, j:j + 1])
                    last.then_inc(Node.ssq.sem, 1)
                    done(act, Node.ssq, n)
                    act.activation(sdz[:P, s, :], ssq[:P, s, :], ACT.Sqrt, bias=eps[:P, :], scale=1.0 / F).then_inc(Node.sdz.sem, 1)

                def root_x1(g, s, q):
                    root(sd1[:, s], mv1[:, s], Node.sd1, Node.mv1, base + g, P)

                def turned_x1(g, s, q):
                    done(act, Node.t1, base + g)
                    act.activation(by_tile(H1T[s])[:, :, 0:P], by_tile(bank[1][:, :])[:, :, 0:P], ACT.Relu).then_inc(Node.h1.sem, 1)

                def norm_x(g, s, q):
                    norm_rows(act, XN0[s], X[s], rs0[:, s], nm0[:, s], Node.nm0, Node.xn0, base + g, P)

                def norm_x1(g, s, q):
                    if not (isinstance(g, int) and g < U):
                        if sources:
                            reached(act, Node.h1_store[s], q * 16)
                    elif not sources and base:
                        reached(act, Node.h1_store[s], 16 * (GROUPS // U))
                    norm_rows(act, XN1[s], X1[s], rs1[:, s], nm1[:, s], Node.nm1, Node.xn1, base + g, P)

                def message_rows(g, s, q):
                    done(act, Node.msg, g)
                    if not (isinstance(g, int) and g < U):
                        reached(act, Node.msg_store[s], q * 16)
                    act.activation(MR[s], wide[:, GW:], ACT.Copy).then_inc(Node.mr.sem, 1)

                def root_x3(g, s, q):
                    root(sd2[:, s], mv2[:, s], Node.sd2, Node.mv2, g)

                def norm_x3(g, s, q):
                    norm_rows(act, XN2[s], XO[s], rs2[:, s], nm2[:, s], Node.nm2, Node.xn2, g)

                def turned_x3(g, s, q):
                    done(act, Node.t2, g)
                    act.activation(H2T[s], bank[5][:, :], ACT.Relu).then_inc(Node.h2.sem, 1)

                def nt_rows(g, s, q):
                    done(act, Node.nt, g)
                    if not (isinstance(g, int) and g < U):
                        reached(act, Node.nt_store[s], q * 16)
                    act.activation(NTR[s], bank[5][:, :], ACT.Copy).then_inc(Node.ntr.sem, 1)

                first = [(1, root_x), (5, root_x1)] + ([(10, root_x3), (13, nt_rows), (8, message_rows)] if sources else [])
                norms = [(7, turned_x1), (3, turned_x), (2, norm_x), (6, norm_x1)]
                return first + norms + ([(12, turned_x3), (11, norm_x3)] if sources else []) + [(3, square_z)]

            pipelined(act, RUN_A[1], node_phases(RUN_A[0], NP, False))
            pipelined(act, GROUPS, node_phases(RUN_S[0], 128, True))
            pipelined(act, RUN_B[1], node_phases(RUN_B[0], NP, False))
            act.wait_ge(s_sd, 1)
            act.activation(dinv[:, :], count[:, :], ACT.Sqrt).then_inc(s_sd, 1)

            act.wait_ge(s_stage, 1)

            def dest_root(g, s, q):
                root(sd0[:, s], mv0[:, s], Dest.sd0, Dest.mv0, g)

            def dest_turned(g, s, q):
                done(act, Dest.t0, g)
                act.activation(H0D[s], bank[1][:, :], ACT.Relu).then_inc(Dest.h0.sem, 1)

            def dest_mean(g, s, q):
                done(act, Dest.z, g)
                done(act, Dest.xb, g)
                for j in range(TPG):
                    last = act.activation(ZS[s][:, j * F:(j + 1) * F], bank[3][:, j * F:(j + 1) * F], ACT.Identity, scale=rdg[:, s, j:j + 1])
                last.then_inc(Dest.zs.sem, 1)

            def dest_square(g, s, q):
                done(act, Dest.zm, g)
                for j in range(TPG):
                    last = act.activation(junk[:, j * F:(j + 1) * F], ZM[s][:, j * F:(j + 1) * F], ACT.Square, accum_out=ssq[:, s, j:j + 1])
                last.then_inc(Dest.ssq.sem, 1)
                done(act, Dest.ssq, g)
                act.activation(sdz[:, s, :], ssq[:, s, :], ACT.Sqrt, bias=eps[:, :], scale=1.0 / F).then_inc(Dest.sdz.sem, 1)

            def dest_root1(g, s, q):
                root(sd1[:, s], mv1[:, s], Dest.sd1, Dest.mv1, g)

            def dest_turned1(g, s, q):
                done(act, Dest.t1, g)
                act.activation(H1D[s], bank[4][:, :], ACT.Relu).then_inc(Dest.h1.sem, 1)

            def dest_messages(g, s, q):
                done(act, Dest.msg, g)
                if not (isinstance(g, int) and g < U):
                    reached(act, Dest.store[s], q * 48)
                act.activation(MD[s], wide[:, GW:], ACT.Copy).then_inc(Dest.mr.sem, 1)
                done(act, Dest.own, g)
                act.activation(OD[s], bank[5][:, :], ACT.Identity, bias=conv_bias[:, 0:1]).then_inc(Dest.ownr.sem, 1)

            def dest_norm(g, s, q):
                norm_rows(act, XN0D[s], XD[s], rs0[:, s], nm0[:, s], Dest.nm0, Dest.xn0, g)

            def dest_norm1(g, s, q):
                norm_rows(act, XN1D[s], X1D[s], rs1[:, s], nm1[:, s], Dest.nm1, Dest.xn1, g)

            pipelined(act, GROUPS, [(7, dest_messages), (2, dest_turned), (0, dest_root), (1, dest_norm), (2, dest_mean), (3, dest_square),
                                    (4, dest_root1), (6, dest_turned1), (5, dest_norm1)])

            for l in range(LAYERS):
                act.wait_ge(s_stage, 2 + l)

                def conv_relu(g, s, q, l=l):
                    done(act, Conv.add, l * GROUPS + g)
                    act.activation(YN[s], AD[s], ACT.Relu).then_inc(Conv.yn.sem, 1)

                def conv_tables(g, s, q, l=l):
                    n = l * GROUPS + g
                    done(act, Conv.msg, n)
                    if not (isinstance(g, int) and g < U):
                        reached(act, Conv.store[s], (q + l * (GROUPS // U)) * 32)
                    act.activation(MRN[s], bank[1][:, :], ACT.Copy).then_inc(Conv.mr.sem, 1)
                    done(act, Conv.own, n)
                    act.activation(OWN[s], bank[2][:, :], ACT.Identity, bias=conv_bias[:, l + 1:l + 2]).then_inc(Conv.ownr.sem, 1)

                def conv_root(g, s, q):
                    root(sd0[:, s], mv0[:, s], Conv.sd, Conv.mv, g)

                def conv_g(g, s, q):
                    done(act, Conv.nm, g)
                    if not (isinstance(g, int) and g < U):
                        reached(act, Conv.store[s], (q + (LAYERS - 1) * (GROUPS // U)) * 32)
                    for j in range(TPG):
                        last = act.activation(G2[s][:, j * F:(j + 1) * F], X2[s][:, j * F:(j + 1) * F], ACT.Relu,
                                              bias=nm0[:, s, j:j + 1], scale=rs1[:, s, j:j + 1])
                    last.then_inc(Conv.g.sem, 1)

                if l < LAYERS - 1:
                    pipelined(act, GROUPS, [(3, conv_tables), (1, conv_relu)])
                else:
                    pipelined(act, GROUPS, [(4, conv_g), (3, conv_root), (1, conv_relu)])

            act.wait_ge(s_stage, 2 + LAYERS)

            def gcn_turned(g, s, q):
                done(act, Gcn.tg, g)
                freed(act, Gcn.scan, g, U)
                act.activation(GTs[s], bank[0][:, :], ACT.Relu).then_inc(Gcn.gt.sem, 1)

            def gcn_root(g, s, q):
                root(sd1[:, s], mv1[:, s], Gcn.sd, Gcn.mv, g)
                if not (isinstance(g, int) and g < U):
                    reached(act, Gcn.store[s], q * 48)
                done(act, Gcn.last, g)
                for j in range(TPG):
                    last = act.activation(X3M[s][:, j * F:(j + 1) * F], X3[s][:, j * F:(j + 1) * F], ACT.Identity, scale=lastg[:, s, j:j + 1])
                last.then_inc(Gcn.x3m.sem, 1)

            def gcn_norm(g, s, q):
                norm_rows(act, XN3[s], X3[s], rs1[:, s], nm1[:, s], Gcn.nm, Gcn.xn, g)

            def gcn_turned1(g, s, q):
                done(act, Gcn.t1, g)
                act.activation(H3T[s], bank[3][:, :], ACT.Relu).then_inc(Gcn.h1.sem, 1)

            def gcn_nt(g, s, q):
                done(act, Gcn.nt, g)
                if not (isinstance(g, int) and g < U):
                    reached(act, Gcn.store[s], q * 48)
                act.activation(NT3[s], bank[4][:, :], ACT.Copy).then_inc(Gcn.ntr.sem, 1)
                for j in range(TPG):
                    last = act.activation(NTM[s][:, j * F:(j + 1) * F], bank[4][:, j * F:(j + 1) * F], ACT.Identity, scale=lastg[:, s, j:j + 1])
                last.then_inc(Gcn.ntm.sem, 1)

            pipelined(act, GROUPS, [(6, gcn_nt), (5, gcn_turned1), (4, gcn_norm), (3, gcn_root), (0, gcn_turned)])

            act.wait_ge(s_stage, 3 + LAYERS)

            def gat_source(g, s, q):
                done(act, Gat.ts, g)
                freed(act, Gat.num, g, U)
                act.activation(NTS[s], bank[0][:, :], ACT.Identity, bias=gat_b_c[:, :]).then_inc(Gat.nts.sem, 1)

            def gat_dest(g, s, q):
                done(act, Gat.spread, g)
                freed(act, Gat.lkd, g, U)
                act.activation(NTD[s], NDT[s], ACT.Identity, bias=gat_b_c[:, :]).then_inc(Gat.ntd.sem, 1)

            def gat_logits(g, s, q):
                done(act, Gat.lg, g)
                freed(act, Gat.sub, g, U)
                act.activation(LGS[s], wide[:, 0:GW], ACT.Identity, bias=attn_b_c[:, :]).then_inc(Gat.lgs.sem, 1)

            def gat_exp(g, s, q):
                done(act, Gat.sub, g)
                act.activation(PE_[s], PE_[s], ACT.Exp).then_inc(Gat.ep.sem, 1)
                done(act, Gat.drop, g)
                act.activation(CE[s], CE[s], ACT.Exp).then_inc(Gat.ec.sem, 1)

            pipelined(act, GROUPS, [(1, gat_dest), (3, gat_logits), (0, gat_source), (4, gat_exp)])

        @block.tensor
        def _(pe):
            pe.wait_ge(s_const, 8)
            pe.wait_ge(s_rows, 1)
            for n, row in enumerate((rowf[:, 4, :], rowf[:, 5, :], rowf[:, 6, :], near[:, 3, :], rowf[:, 2, :])):
                for b in range(2):
                    last = pe.transpose(bank[n][:, b * RR:(b + 1) * RR], row[:, b * 128:(b + 1) * 128], ident[:RR, :RR])
                last.then_inc(s_rowsT, 1)
            pe.wait_ge(s_cols, 1)
            pe.wait_ge(s_wc, 1)
            for n in range(3):
                pe.transpose(bank[0][:, n * F:(n + 1) * F], wc[:, n, :], ident[:, :])
            for l in range(LAYERS):
                pe.transpose(bank[1][:, l * F:(l + 1) * F], wn[:, 4 + l, :], ident[:, :])
                last = pe.transpose(bank[2][:, l * F:(l + 1) * F], pt[:, l, :], ident[:, :])
            last.then_inc(s_wcT, 1)
            pe.wait_ge(s_wt, 1)

            def node_phases(base, P, sources):
                def turn_x(g, s, q):
                    n = base + g
                    done(pe, Node.xn0, n)
                    freed(pe, Node.h0, n, 1)
                    turn(pe, bank[0], XN0[s], P).then_inc(Node.t0.sem, 1)

                def product_z(g, s, q):
                    n = base + g
                    done(pe, Node.h0, n)
                    z = z_bank(s, sources)
                    if base and not sources and isinstance(g, int) and g < U:
                        done(pe, Node.w, base - 1)
                        done(pe, Node.nb, GROUPS - 1)
                        done(pe, Node.mr, GROUPS - 1)
                        done(pe, Node.ntr, GROUPS - 1)
                    else:
                        freed(pe, Node.w, n, 1 if sources else U)
                    pe.matmul(z[:P, :], ones3[:, 0:P], bias3[:, 0, :], start=True, stop=False)
                    for j in range(TPG):
                        last = pe.matmul(z[:P, j * F:(j + 1) * F], H0T[s][:, j * 128:j * 128 + P], wT[:, 0, :],
                                         start=False, stop=j == TPG - 1)
                    last.then_inc(Node.z.sem, 1)

                def turn_x1(g, s, q):
                    n = base + g
                    done(pe, Node.xn1, n)
                    freed(pe, Node.h1, n, 1)
                    turn(pe, bank[1], XN1[s], P).then_inc(Node.t1.sem, 1)

                def product_x3(g, s, q):
                    n = base + g
                    done(pe, Node.h1, n)
                    freed(pe, Node.xo, n, 1)
                    pe.matmul(bank[2][:P, :], ones3[:, 0:P], bias3[:, 1, :], start=True, stop=False)
                    for j in range(TPG):
                        last = pe.matmul(bank[2][:P, j * F:(j + 1) * F], H1T[s][:, j * 128:j * 128 + P], gcn_w_s[:, :],
                                         start=False, stop=j == TPG - 1)
                    last.then_inc(Node.x3.sem, 1)

                def turn_sums(g, s, q):
                    done(pe, Node.cnt, g)
                    freed(pe, Node.nb, g, 1)
                    turn(pe, bank[3], SUM1T[s])
                    for j in range(TPG):
                        last = pe.matmul(bank[4][:, j:j + 1], CNT[s][:, j * 128:(j + 1) * 128], ident[:, 0:1], start=True, stop=True)
                    last.then_inc(Node.ts.sem, 1)

                def message(g, s, q):
                    freed(pe, Node.mr, g, 1)
                    for j in range(TPG):
                        last = pe.matmul(wide[:, GW + j * F:GW + (j + 1) * F], H1T[s][:, j * 128:(j + 1) * 128], thetaT[:, 0, :],
                                         start=True, stop=True)
                    last.then_inc(Node.msg.sem, 1)

                def attention_rows(g, s, q):
                    done(pe, Node.xn2, g)
                    freed(pe, Node.ntr, g, 1)
                    turn(pe, bank[5], XN2[s]).then_inc(Node.t2.sem, 1)
                    done(pe, Node.h2, g)
                    for j in range(TPG):
                        last = pe.matmul(bank[5][:, j * F:(j + 1) * F], H2T[s][:, j * 128:(j + 1) * 128], gat_w_s[:, :], start=True, stop=True)
                    last.then_inc(Node.nt.sem, 1)

                first = [(7, turn_x1), (3, turn_x), (7, product_x3)]
                return first + ([(5, turn_sums), (7, message), (12, attention_rows)] if sources else []) + [(3, product_z)]

            pipelined(pe, RUN_A[1], node_phases(RUN_A[0], NP, False))
            pipelined(pe, GROUPS, node_phases(RUN_S[0], 128, True))
            pipelined(pe, RUN_B[1], node_phases(RUN_B[0], NP, False))

            pe.wait_ge(s_stage, 1)

            def dest_turn_nb(g, s, q):
                reached(pe, Dest.gather[s], q * 128 + 128)
                freed(pe, Dest.sum2, g, 1)
                turn(pe, bank[0], NBG[s]).then_inc(Dest.tn.sem, 1)

            def dest_turn_x(g, s, q):
                done(pe, Dest.xn0, g)
                freed(pe, Dest.h0, g, 1)
                turn(pe, bank[1], XN0D[s]).then_inc(Dest.t0.sem, 1)

            def dest_products(g, s, q):
                done(pe, Dest.h0, g)
                done(pe, Dest.sum2, g)
                reached(pe, Dest.load[s], q * 32 + 32)
                freed(pe, Dest.zm, g, 1)
                freed(pe, Dest.zs, g, 1)
                pe.matmul(bank[2][:, :], ones3[:, :], bias3[:, 0, :], start=True, stop=False)
                for j in range(TPG):
                    at = slice(j * F, (j + 1) * F)
                    pe.matmul(bank[2][:, at], H0D[s][:, at], wT[:, 0, :], start=False, stop=j == TPG - 1)
                    pe.matmul(bank[3][:, at], S1L[s][:, at], wT[:, 1, :], start=True, stop=False)
                    last = pe.matmul(bank[3][:, at], S2T[s][:, at], wT[:, 2, :], start=False, stop=True)
                last.then_inc(Dest.z.sem, 1)

            def dest_turn_x1(g, s, q):
                done(pe, Dest.xn1, g)
                freed(pe, Dest.h1, g, 1)
                turn(pe, bank[4], XN1D[s]).then_inc(Dest.t1.sem, 1)

            def dest_messages(g, s, q):
                done(pe, Dest.h1, g)
                freed(pe, Dest.mr, g, 1)
                for j in range(TPG):
                    last = pe.matmul(wide[:, GW + j * F:GW + (j + 1) * F], H1D[s][:, j * 128:(j + 1) * 128], thetaT[:, 0, :], start=True, stop=True)
                last.then_inc(Dest.msg.sem, 1)
                freed(pe, Dest.ownr, g, 1)
                pe.matmul(bank[5][:, :], ptT[:, 0, :], H1D[s], start=True, stop=True).then_inc(Dest.own.sem, 1)

            pipelined(pe, GROUPS, [(2, dest_turn_x), (6, dest_turn_x1), (2, dest_products), (6, dest_messages), (0, dest_turn_nb)])

            for l in range(LAYERS):
                pe.wait_ge(s_stage, 2 + l)

                def conv_turn(g, s, q, l=l):
                    n = l * GROUPS + g
                    reached(pe, Conv.gather[s], (q + l * (GROUPS // U)) * 64 + 64)
                    freed(pe, Conv.scan, n, 1)
                    turn(pe, bank[0], MG[s]).then_inc(Conv.tm.sem, 1)

                def conv_messages(g, s, q, l=l):
                    n = l * GROUPS + g
                    done(pe, Conv.yn, n)
                    freed(pe, Conv.mr, n, 1)
                    for j in range(TPG):
                        last = pe.matmul(bank[1][:, j * F:(j + 1) * F], YN[s][:, j * 128:(j + 1) * 128], thetaT[:, l + 1, :], start=True, stop=True)
                    last.then_inc(Conv.msg.sem, 1)
                    freed(pe, Conv.ownr, n, 1)
                    pe.matmul(bank[2][:, :], ptT[:, l + 1, :], YN[s], start=True, stop=True).then_inc(Conv.own.sem, 1)

                def conv_turn_back(g, s, q, l=l):
                    done(pe, Conv.yn, l * GROUPS + g)
                    freed(pe, Conv.x2, g, 1)
                    turn(pe, bank[3], YN[s]).then_inc(Conv.tb.sem, 1)

                pipelined(pe, GROUPS, [(0, conv_turn), (2, conv_messages if l < LAYERS - 1 else conv_turn_back)])

            pe.wait_ge(s_stage, 2 + LAYERS)

            def gcn_turn(g, s, q):
                reached(pe, Gcn.load[s], q * 48 + 48)
                freed(pe, Gcn.u, g, 1)
                turn(pe, bank[1], GD[s]).then_inc(Gcn.td.sem, 1)
                reached(pe, Gcn.gather[s], q * 64 + 64)
                freed(pe, Gcn.gt, g, 1)
                turn(pe, bank[0], GG[s]).then_inc(Gcn.tg.sem, 1)

            def gcn_product(g, s, q):
                done(pe, Gcn.u, g)
                freed(pe, Gcn.x3, g, 1)
                for j in range(TPG):
                    at = slice(j * F, (j + 1) * F)
                    last = pe.matmul(bank[2][:, at], UG[s][:, at], gcn_w_s[:, :], start=True, stop=True)
                last.then_inc(Gcn.w.sem, 1)

            def gcn_turn_x3(g, s, q):
                done(pe, Gcn.xn, g)
                freed(pe, Gcn.h1, g, 1)
                turn(pe, bank[3], XN3[s]).then_inc(Gcn.t1.sem, 1)

            def gcn_attention_rows(g, s, q):
                done(pe, Gcn.h1, g)
                freed(pe, Gcn.ntm, g, 1)
                for j in range(TPG):
                    last = pe.matmul(bank[4][:, j * F:(j + 1) * F], H3T[s][:, j * 128:(j + 1) * 128], gat_w_s[:, :], start=True, stop=True)
                last.then_inc(Gcn.nt.sem, 1)

            pipelined(pe, GROUPS, [(5, gcn_turn_x3), (2, gcn_product), (0, gcn_turn), (5, gcn_attention_rows)])

            pe.wait_ge(s_stage, 3 + LAYERS)

            def gat_turn(g, s, q):
                reached(pe, Gat.load[s], q * 48 + 48)
                freed(pe, Gat.spread, g, 1)
                turn(pe, bank[1], NM[s]).then_inc(Gat.td.sem, 1)
                freed(pe, Gat.xscan, g, 1)
                turn(pe, bank[2], XM[s]).then_inc(Gat.tx.sem, 1)
                reached(pe, Gat.gather[s], q * 64 + 64)
                freed(pe, Gat.nts, g, 1)
                turn(pe, bank[0], NS[s]).then_inc(Gat.ts.sem, 1)

            def gat_logits(g, s, q):
                done(pe, Gat.lks, g)
                done(pe, Gat.lkd, g)
                freed(pe, Gat.lgs, g, 1)
                pe.matmul(wide[:, 0:GW], attn_m[:, 0, :], LKS[s], start=True, stop=False)
                pe.matmul(wide[:, 0:GW], attn_m[:, 1, :], LKD[s], start=False, stop=True).then_inc(Gat.lg.sem, 1)

            def gat_turn_out(g, s, q):
                freed(pe, Gat.oe, g, 1)
                turn(pe, bank[3], X3T[s]).then_inc(Gat.txb.sem, 1)
                done(pe, Gat.den, g)
                for j in range(TPG):
                    last = pe.matmul(bank[4][:, j * HEADS:(j + 1) * HEADS], DEN[s][:, j * 128:(j + 1) * 128], ident[:, ::HC],
                                     start=True, stop=True)
                last.then_inc(Gat.tden.sem, 1)
                done(pe, Gat.num, g)
                turn(pe, bank[5], NUM[s]).then_inc(Gat.tnum.sem, 1)

            pipelined(pe, GROUPS, [(0, gat_turn), (3, gat_logits), (5, gat_turn_out)])


_INS = ["x", "src", "dst", "node_vec", "L0_gnn_W_self", "L0_gnn_W_nb1", "L0_gnn_W_hp", "L0_gnn_W_nb2", "L0_gnn_bias",
        "L0_gnn_branch_logits", "L0_gnn_ln_gamma", "L0_gnn_ln_beta", "L1_gnn_theta_w", "L1_gnn_theta_b",
        "L1_gnn_phi_w", "L1_gnn_phi_b", "L2_gnn_W", "L2_gnn_b", "L3_gnn_W", "L3_gnn_b", "L3_gnn_attn_w", "L3_gnn_attn_b"]


def kernel(**inputs):
    import concourse.bacc as bacc
    from concourse.bass_utils import run_bass_kernel_spmd

    nc = bacc.Bacc("TRN2", target_bir_lowering=False, num_devices=1)
    arrays, args = {}, []
    for name in _INS:
        a = np.ascontiguousarray(inputs[name])
        arrays[f"in_{name}"] = a
        args.append(nc.dram_tensor(f"in_{name}", a.shape, mybir.dt.from_np(a.dtype), kind="ExternalInput").ap())
    out = nc.dram_tensor("out_0", (NODES, F), F32, kind="ExternalOutput").ap()
    build(nc, *args, out)
    return run_bass_kernel_spmd(nc, [arrays], core_ids=[0]).results[0]["out_0"]
```

```python
from contextlib import ExitStack

import numpy as np
import concourse.bass as bass
from concourse import mybir

F32 = mybir.dt.float32
BF16 = mybir.dt.bfloat16
I32 = mybir.dt.int32
ALU = mybir.AluOpType
ACT = mybir.ActivationFunctionType
AX = mybir.AxisListType

NODES, EDGES, F = 100000, 25000, 128
LAYERS, HEADS = 4, 8
HC = F // HEADS
TPG = 4
GW = TPG * 128
U = 5
GROUPS = -(-EDGES // GW)
GROUPS += -GROUPS % U
SLOTS = GROUPS * GW
TILES = SLOTS // 128
RW = 2 * 128
RR = SLOTS // RW
NOWHERE = 1 << 20
NP = 125
NG = NP * TPG
NODE_GROUPS = NODES // NG
PT = 40
EPS = 1e-5
SLOPE = 0.2
NEG = 3.0e38
ds = bass.ds


def pipelined(eng, count, phases):
    deepest = max(lag for lag, _ in phases)
    head = U + -(-deepest // U) * U
    turns = (count - head) // U

    def static(n):
        for lag, phase in phases:
            if 0 <= n - lag < count:
                phase(n - lag, (n - lag) % U, (n - lag) // U)

    for n in range(head):
        static(n)
    if turns > 0:
        with eng.Fori(0, turns) as i:
            for k in range(U):
                for lag, phase in phases:
                    g = head + k - lag
                    phase(i * U + g, g % U, i + g // U)
    for n in range(head + turns * U, count + deepest):
        static(n)


class Signal:

    def __init__(self, semaphore, base):
        self.sem, self.base = semaphore, base


def reached(eng, signal, value):
    eng.wait_ge(signal.sem, value + signal.base)


def done(eng, signal, n):
    reached(eng, signal, n + 1)


def freed(eng, signal, n, depth):
    if isinstance(n, int) and n < depth:
        return
    reached(eng, signal, n - depth + 1)


def build(nc, x, src, dst, node_vec, w_self, w_nb1, w_hp, w_nb2, l0_bias, logits, gamma, beta,
          theta_w, theta_b, phi_w, phi_b, gcn_w, gcn_b, gat_w, gat_b, attn_w, attn_b, out):
    with ExitStack() as ctx:
        def sb(name, shape, dt=F32):
            return ctx.enter_context(nc.sbuf_tensor(name, shape, dt))

        def sem(name):
            return ctx.enter_context(nc.semaphore(name))

        def sems(name):
            return [sem(f"{name}{k}") for k in range(U)]

        def dram(name, shape, dt=F32):
            return nc.dram_tensor(name, shape, dt, kind="Internal").ap()

        dst_padded = dram("dst_padded", (1, SLOTS + 2), I32)
        flags_d = [dram(f"flags_{n}", (1, SLOTS), BF16) for n in range(4)]
        same_prev_d, neg_prev_d, same_next_d, neg_next_d = flags_d
        slot_of_node = dram("slot_of_node", (NODES, 1), I32)
        nb1_tab = dram("nb1_tab", (SLOTS + 1, F))
        sum1T_tab = dram("sum1T_tab", (F, SLOTS))
        h1_local = dram("h1_local", (SLOTS, F))
        message_local = dram("message_local", (SLOTS, F))
        nt_local = dram("nt_local", (SLOTS, F))
        x1_tab = dram("x1_tab", (SLOTS, F))
        message_tab = [dram(f"message_tab{n}", (SLOTS + (n > 0), F)) for n in range(LAYERS)]
        ownT_tab = [dram(f"ownT_tab{n}", (F, SLOTS)) for n in range(LAYERS)]
        x2_tab = dram("x2_tab", (SLOTS, F))
        g_tab = dram("g_tab", (SLOTS, F))
        nt_tab = dram("nt_tab", (SLOTS, F))
        x3_last_tab = dram("x3_last_tab", (SLOTS, F))
        nt_last_tab = dram("nt_last_tab", (SLOTS, F))

        def rows_of(tab, g):
            return tab[ds(g * GW, GW), :].rearrange("(j p) f -> p j f", p=128)

        def cols_of(tab, g):
            return tab[:, ds(g * GW, GW)]

        def flags_of(tab, g):
            return tab[0:1, ds(g * GW, GW)].partition_broadcast(128)

        ident = sb("ident", [128, 128])
        head_mask = sb("head_mask", [128, 128])
        ones = sb("ones", [128, GW])
        zeros = sb("zeros", [128, F])
        eps = sb("eps", [128, 1])
        gamma_b = sb("gamma_b", [128, F])
        beta_b = sb("beta_b", [128, F])
        gcn_b_b = sb("gcn_b_b", [128, F])
        bias3 = sb("bias3", [3, 2, GW], BF16)
        ones3 = sb("ones3", [3, 128], BF16)
        wT = sb("wT", [128, 3, F])
        thetaT = sb("thetaT", [128, LAYERS, F])
        ptT = sb("ptT", [128, LAYERS, F])
        gcn_w_s = sb("gcn_w_s", [128, F])
        gat_w_s = sb("gat_w_s", [128, F])
        gat_b_c = sb("gat_b_c", [128, 1])
        attn_c = sb("attn_c", [128, 2])
        attn_b_c = sb("attn_b_c", [128, 1])
        attn_m = sb("attn_m", [128, 2, F])
        conv_b = sb("conv_b", [128, 2, LAYERS])
        conv_bias = sb("conv_bias", [128, LAYERS])
        scale_l = sb("scale_l", [128, 4])
        scale_s = sb("scale_s", [128, 4])
        scale_2 = sb("scale_2", [128, 6])
        small = sb("small", [128, 4])

        far_i = sb("far_i", [NP, NODES // NP], I32)
        last_i = sb("last_i", [128, TILES], I32)
        first_i = sb("first_i", [128, TILES], I32)
        dst_i = sb("dst_i", [128, TILES], I32)
        src_c = sb("src_c", [128, TILES], I32)
        slot_i = sb("slot_i", [128, TILES], I32)
        from_i = sb("from_i", [128, TILES], I32)
        is_last = sb("is_last", [128, TILES])
        deg = sb("deg", [128, U, TPG])
        rdeg = sb("rdeg", [128, TILES])
        count = sb("count", [128, TILES])
        dinv = sb("dinv", [128, TILES])
        now_i = sb("now_i", [128, PT], I32)
        now_v = sb("now_v", [128, PT], I32)
        gi = sb("gi", [128, U, 2 * TPG], I32)

        units = sb("units", [128, 75, GW])
        near = units[0:RR, 0:2, :].rearrange("p a (b w) -> p (a b) w", w=RW)
        rowf = units[0:RR, 2:6, :].rearrange("p a (b w) -> p (a b) w", w=RW)
        def lent(unit, parts, shape, dt=F32):
            size = int(np.prod(shape)) * (2 if dt == BF16 else 4) // 4
            flat = units[0:parts, unit:unit + -(-size // GW), :].rearrange("p a b -> p (a b)")[:, 0:size]
            flat = flat if dt == F32 else flat.bitcast(dt)
            names = "abc"[:len(shape)]
            return flat.rearrange(f"p ({' '.join(names)}) -> p {' '.join(names)}", **dict(zip(names, shape)))

        wn = lent(40, 128, (12, F))
        pt = lent(43, 128, (LAYERS, F))
        wc = lent(44, 128, (3, F))
        near_i = lent(45, RR, (3, RW), I32)
        pad_i = lent(47, 1, (SLOTS - EDGES + 2,), I32)
        src_i = lent(49, RR, (RW,), I32)
        bias_src = lent(50, 3, (2, F))
        bias_part = lent(51, 3, (3, 2, F))
        bias_rest = lent(53, 3, (2, F))
        bias_bf = lent(54, 3, (2, F), BF16)
        flag_row = [units[0:RR, 6 + n, 0:RW // 2].bitcast(BF16) for n in range(4)]

        def ring(n):
            return [units[:, n * U + k, :] for k in range(U)]

        mask_a = sb("mask_a", [128, U, GW], BF16)
        mask_b = sb("mask_b", [128, U, GW], BF16)
        mx = sb("mx", [128, U, GW + 1])
        junk = sb("junk", [128, GW])
        st0 = sb("st0", [128, U, TPG, 6])
        st2 = sb("st2", [128, U, TPG, 6])
        mv2 = sb("mv2", [128, U, TPG, 2])
        sd2 = sb("sd2", [128, U, TPG])
        rs2 = sb("rs2", [128, U, TPG])
        nm2 = sb("nm2", [128, U, TPG])
        st1 = sb("st1", [128, U, TPG, 6])
        mv0 = sb("mv0", [128, U, TPG, 2])
        mv1 = sb("mv1", [128, U, TPG, 2])
        sd0 = sb("sd0", [128, U, TPG])
        sd1 = sb("sd1", [128, U, TPG])
        sdz = sb("sdz", [128, U, TPG])
        nm0 = sb("nm0", [128, U, TPG])
        nm1 = sb("nm1", [128, U, TPG])
        rs0 = sb("rs0", [128, U, TPG])
        rs1 = sb("rs1", [128, U, TPG])
        rsz = sb("rsz", [128, U, TPG])
        ssq = sb("ssq", [128, U, TPG])
        rdg = sb("rdg", [128, U, TPG])
        lastg = sb("lastg", [128, U, TPG])
        rden = sb("rden", [128, U, TPG * HEADS])

        bank = [ctx.enter_context(nc.psum_tensor(f"bank{n}", [128, GW], F32)) for n in range(6)]
        wide = ctx.enter_context(nc.psum_tensor("wide", [128, 2 * GW], F32))

        def by_tile(t):
            return t.rearrange("p (j f) -> p j f", j=TPG)

        s_const, s_w, s_pad, s_padded = sem("s_const"), sem("s_w"), sem("s_pad"), sem("s_padded")
        s_near, s_setup, s_rows, s_rowsT = sem("s_near"), sem("s_setup"), sem("s_rows"), sem("s_rowsT")
        s_flags, s_cols, s_act = sem("s_flags"), sem("s_cols"), sem("s_act")
        s_wc, s_wcT, s_wt = sem("s_wc"), sem("s_wcT"), sem("s_wt")
        s_far, s_init, s_placed, s_tails = sem("s_far"), sem("s_init"), sem("s_placed"), sem("s_tails")
        s_got, s_slot, s_from = sem("s_got"), sem("s_slot"), sem("s_from")
        s_stage, s_sd, s_dinv = sem("s_stage"), sem("s_sd"), sem("s_dinv")
        s_gate = {e: sem(f"s_gate_{e}") for e in ("dve", "pool", "sp")}

        def hold(eng, name):
            eng.sem_inc(s_gate[name], 1)

        raised = {}

        def signal(name, total=GROUPS):
            handle, base = raised.get(name) or (sem(name), 0)
            raised[name] = (handle, base + total)
            return Signal(handle, base)

        def signals(names, total=GROUPS):
            return [signal(name, total) for name in names.split()]

        def by_slot(name, per_group, groups=GROUPS):
            return [signal(f"{name}{k}", per_group * groups // U) for k in range(U)]

        NODE_STEPS = GROUPS + NODE_GROUPS

        class Node:
            bn0, mv0, sd0, rs0, nm0, xn0, xb = signals("stats0 moments0 root0 scale0 shift0 normed0 x_beta", NODE_STEPS)
            t0, h0, z, ssq, sdz, rsz, w = signals("turned0 relu0 z z_squares z_root z_scale z_scaled", NODE_STEPS)
            x1, bn1, mv1, sd1, rs1, nm1, xn1 = signals("x1 stats1 moments1 root1 scale1 shift1 normed1", NODE_STEPS)
            t1, h1, x3, xo = signals("turned1 relu1 gcn_product x_out", NODE_STEPS)
            sum1, cnt, ts, nb, rdeg = signals("source_sums edge_counts sums_turned means node_vec_inverse")
            idx = signal("indices", 2 * GROUPS)
            bn2, mv2, sd2, rs2, nm2, xn2, t2, h2 = signals("stats2 moments2 root2 scale2 shift2 normed2 turned2 relu2")
            msg, mr, nt, ntr = signals("message message_rows nt nt_rows")
            load, store = by_slot("load", 16, NODE_GROUPS), by_slot("store", 16, NODE_GROUPS)
            gather, mask, sum_store = by_slot("gathered", 128), by_slot("flags", 16), by_slot("sums_stored", 32)
            h1_store, msg_store, nt_store = by_slot("h1_stored", 16), by_slot("message_stored", 16), by_slot("nt_stored", 16)

        X, XB, XN0, H0T, X1, XN1, H1T, XO = [ring(n) for n in range(8)]
        SUM1T, CNT, NBR, XN2, H2T, NTR, MR = [ring(n) for n in range(8, 15)]

        def node_rows(tab, n):
            return tab[ds(n * NG, NG), :].rearrange("(p j) f -> p j f", j=TPG)

        class Dest:
            load, gather, idx = by_slot("load", 32), by_slot("gathered", 128), signal("indices", 2 * GROUPS)
            x1_store, store = by_slot("h1_stored", 16), by_slot("store", 32)
            bn0, mv0, sd0, rs0, nm0, xn0, xb = signals("stats0 moments0 root0 scale0 shift0 normed0 x_beta")
            tn, sum2, t0, h0, z, zs, zm = signals("turned2 scanned turned0 relu0 z z_mean z_whole")
            ssq, sdz, rsz, w = signals("z_squares z_root z_scale z_scaled")
            x1, bn1, mv1, sd1, rs1, nm1, xn1, t1, h1 = signals("x1 stats1 moments1 root1 scale1 shift1 normed1 turned1 relu1")
            msg, mr, own, ownr = signals("message message_rows own own_kept")

        NBG, XD, S1L, XBD, XN0D, H0D, S2T, ZS, ZM, X1D, XN1D, H1D, MD, OD = [ring(n) for n in range(14)]

        class Conv:
            fill, load, x1_load = by_slot("flags", 16), by_slot("load", 32, LAYERS * GROUPS), by_slot("flags", 16)
            gather, store, idx = by_slot("gathered", 64, LAYERS * GROUPS), by_slot("store", 32, LAYERS * GROUPS), signal("indices", LAYERS * GROUPS)
            tm, scan, add, yn = signals("turned0 scanned with_own relu1", LAYERS * GROUPS)
            msg, mr, own, ownr = signals("message message_rows own own_kept", (LAYERS - 1) * GROUPS)
            tb, x2, bn, mv, sd, rs, rd, nm, g = signals("turned1 x_out stats0 moments0 root0 scale0 scale1 shift0 normed0")

        MG, OL, SC, AD, YN, MRN, OWN, X1L, X2, G2 = [ring(n) for n in range(10)]

        class Gcn:
            fill, load, gather, store = by_slot("flags", 16), by_slot("load", 48), by_slot("gathered", 64), by_slot("store", 32)
            x3_store = by_slot("h1_stored", 16)
            idx, tg, gt, scan, u, w, xb, x3, td = signals("indices turned0 relu0 scanned with_own gcn_product x_beta x_out own_turned")
            last, bn, mv, sd, rs, nm, xn, t1, h1 = signals("last_kept stats1 moments1 root1 scale1 shift1 normed1 turned1 relu1")
            x3m, nt, ntr, ntm = signals("x3_last nt nt_rows nt_last")

        GG, GD, X2L, GTs, SG, UG, XB2, X3, X3M, XN3, H3T, NT3, NTM = [ring(n) for n in range(13)]

        class Gat:
            fill, load, neg_load = by_slot("flags", 16), by_slot("load", 48), by_slot("sums_stored", 16)
            gather, scatter, idx, out_idx = by_slot("gathered", 64), by_slot("scattered", 64), signal("indices"), signal("out_indices")
            ts, nts, lks, td, spread, ntd, lkd = signals("turned0 nt_rows leaky_source turned1 nt_spread nt_dest leaky_dest")
            lg, lgs, tx, xscan, txb = signals("logits_sum logits turned2 x3_spread x3_rows")
            mscan, diff, drop, sub, ec, ep = signals("scanned max_diff max_drop exponent decay weight")
            den, pn, num, tden, tnum = signals("denominator weighted numerator denominator_turned numerator_turned")
            rden, ratio, oe = signals("scale0 attended x_out")

        NS, NM, XM, NTS, LKS, NDT, NTD, LKD, X3T, LGS, CE, PE_, DEN, NUM, OE = [ring(n) for n in range(15)]
        MX = [mx[:, k, :] for k in range(U)]

        def stats(dve, source, st, s_bn, P=128):
            for j in range(TPG):
                last = dve.bn_stats(st[:P, j, :], source[:P, j * F:(j + 1) * F])
            last.then_inc(s_bn.sem, 1)

        def moments(dve, mv, st, s_bn, s_mv, n, P=128):
            done(dve, s_bn, n)
            hold(dve, "dve")
            for j in range(TPG):
                last = dve.bn_aggr(mv[:P, j, :], st[:P, j, :])
            last.then_inc(s_mv.sem, 1)

        def inverse(dve, rs, sd, s_sd_, s_rs, n, P=128):
            done(dve, s_sd_, n)
            dve.reciprocal(rs[:P, :], sd[:P, :]).then_inc(s_rs.sem, 1)

        def shift(dve, nm, mv, rs, s_rs, s_nm, n, P=128):
            done(dve, s_rs, n)
            dve.scalar_tensor_tensor(nm[:P, :], mv[:P, :, 0], -1.0, rs[:P, :], ALU.mult, ALU.mult).then_inc(s_nm.sem, 1)

        def norm_rows(act, result, source, rs, nm, s_nm, s_xn, n, P=128):
            done(act, s_nm, n)
            for j in range(TPG):
                last = act.activation(result[:P, j * F:(j + 1) * F], source[:P, j * F:(j + 1) * F], ACT.Identity,
                                      bias=nm[:P, j:j + 1], scale=rs[:P, j:j + 1])
            last.then_inc(s_xn.sem, 1)

        def z_bank(s, sources):
            return wide[:, 0:GW] if sources or s == 0 else wide[:, GW:] if s == 1 else bank[s + 1][:, :]

        def turn(pe, result, source, P=128):
            for j in range(TPG):
                last = pe.transpose(result[:, j * 128:j * 128 + P], source[:P, j * 128:(j + 1) * 128], ident[:P, :P])
            return last

        block = ctx.enter_context(nc.Block())

        @block.sync
        def _(sp):
            sp.wait_ge(s_pad, 2)
            sp.dma_start(dst_padded[0:1, 0:1], pad_i[0:1, 0:1]).then_inc(s_padded, 16)
            sp.dma_start(dst_padded[0:1, 1 + EDGES:], pad_i[0:1, 1:]).then_inc(s_padded, 16)
            sp.dma_start(dst_padded[0:1, 1:1 + EDGES], dst.unsqueeze(0)).then_inc(s_padded, 16)
            full = EDGES // RW
            sp.dma_start(src_i[0:full, :], src[0:full * RW].rearrange("(p w) -> p w", w=RW)).then_inc(s_near, 16)
            sp.dma_start(src_i[full:full + 1, 0:EDGES - full * RW], src[full * RW:EDGES].unsqueeze(0)).then_inc(s_near, 16)
            sp.wait_ge(s_padded, 48)
            for n in range(3):
                sp.dma_start(near_i[:, n, :], dst_padded[0, n:n + SLOTS].rearrange("(p w) -> p w", w=RW)).then_inc(s_near, 16)
            for n, w in enumerate((w_self, w_nb1, w_hp, w_nb2)):
                sp.dma_start(wn[:, n, :], w).then_inc(s_w, 16)
            sp.dma_start(wn[:, 4:8, :], theta_w.rearrange("l o i -> o l i")).then_inc(s_w, 16)
            sp.dma_start(wn[:, 8:12, :], phi_w.rearrange("l o i -> o l i")).then_inc(s_w, 16)
            sp.dma_start(gcn_w_s[:, :], gcn_w).then_inc(s_w, 16)
            sp.dma_start(gat_w_s[:, :], gat_w).then_inc(s_w, 16)
            sp.dma_start(gamma_b[:, :], gamma.unsqueeze(0).partition_broadcast(128)).then_inc(s_w, 16)
            sp.dma_start(beta_b[:, :], beta.unsqueeze(0).partition_broadcast(128)).then_inc(s_w, 16)
            sp.dma_start(gcn_b_b[:, :], gcn_b.unsqueeze(0).partition_broadcast(128)).then_inc(s_w, 16)
            sp.dma_start(bias_src[:, 0, :], l0_bias.unsqueeze(0).partition_broadcast(3)).then_inc(s_w, 16)
            sp.dma_start(bias_src[:, 1, :], gcn_b.unsqueeze(0).partition_broadcast(3)).then_inc(s_w, 16)
            sp.dma_start(scale_l[:, :], logits.unsqueeze(0).partition_broadcast(128)).then_inc(s_w, 16)
            sp.dma_start(attn_b_c[:, :], attn_b.unsqueeze(0).partition_broadcast(128)).then_inc(s_w, 16)
            sp.dma_start(gat_b_c[:, :], gat_b.unsqueeze(1)).then_inc(s_w, 16)
            for l in range(LAYERS):
                sp.dma_start(conv_b[:, 0, l:l + 1], theta_b[l, :].unsqueeze(1)).then_inc(s_w, 16)
                sp.dma_start(conv_b[:, 1, l:l + 1], phi_b[l, :].unsqueeze(1)).then_inc(s_w, 16)
            for h in range(HEADS):
                for n in range(2):
                    sp.dma_start(attn_c[h * HC:(h + 1) * HC, n:n + 1], attn_w[n * HC:(n + 1) * HC, :]).then_inc(s_w, 16)
            sp.wait_ge(s_const, 6)
            for tab in (nb1_tab, message_tab[1], message_tab[2], message_tab[3]):
                sp.dma_start(tab[SLOTS:SLOTS + 1, :], zeros[0:1, :]).then_inc(s_tails, 16)
            sp.wait_ge(s_far, 1)
            sp.dma_start(slot_of_node.rearrange("(p a) o -> p (a o)", p=NP), far_i[:, :]).then_inc(s_init, 16)
            sp.wait_ge(s_rows, 1)
            for tab, row in zip(flags_d, flag_row):
                sp.dma_start(tab[0, :].rearrange("(p w) -> p w", w=RW), row).then_inc(s_flags, 16)
            sp.wait_ge(s_flags, 64)
            sp.wait_ge(s_cols, 1)

            def node_load(g, s, q):
                freed(sp, Node.xn0, GROUPS + g, U)
                freed(sp, Node.xb, GROUPS + g, U)
                hold(sp, "sp")
                sp.dma_start(by_tile(X[s])[:NP], node_rows(x, g)).then_inc(Node.load[s].sem, 16)

            def node_store(g, s, q):
                done(sp, Node.xo, GROUPS + g)
                hold(sp, "sp")
                sp.dma_start(node_rows(out, g), by_tile(XO[s])[:NP]).then_inc(Node.store[s].sem, 16)

            def source_flags(g, s, q):
                freed(sp, Node.cnt, g, U)
                hold(sp, "sp")
                sp.dma_start(mask_a[:, s, :], flags_of(same_prev_d, g)).then_inc(Node.mask[s].sem, 16)

            def source_store(g, s, q):
                done(sp, Node.sum1, g)
                hold(sp, "sp")
                sp.dma_start(cols_of(sum1T_tab, g), SUM1T[s]).then_inc(Node.sum_store[s].sem, 16)
                done(sp, Node.xn1, g)
                hold(sp, "sp")
                sp.dma_start(rows_of(h1_local, g), by_tile(XN1[s])).then_inc(Node.h1_store[s].sem, 16)
                done(sp, Node.nb, g)
                hold(sp, "sp")
                sp.dma_start(rows_of(nb1_tab, g), by_tile(NBR[s])).then_inc(Node.sum_store[s].sem, 16)

            def message_store(g, s, q):
                done(sp, Node.mr, g)
                hold(sp, "sp")
                sp.dma_start(rows_of(message_local, g), by_tile(MR[s])).then_inc(Node.msg_store[s].sem, 16)

            def nt_store(g, s, q):
                done(sp, Node.ntr, g)
                hold(sp, "sp")
                sp.dma_start(rows_of(nt_local, g), by_tile(NTR[s])).then_inc(Node.nt_store[s].sem, 16)

            pipelined(sp, GROUPS, [(0, source_flags), (7, source_store), (9, message_store), (14, nt_store)])
            pipelined(sp, NODE_GROUPS, [(0, node_load), (11, node_store)])
            for k in range(U):
                reached(sp, Node.store[k], 16 * (NODE_GROUPS // U))
                reached(sp, Node.msg_store[k], 16 * (GROUPS // U))
                reached(sp, Node.nt_store[k], 16 * (GROUPS // U))
                reached(sp, Node.sum_store[k], 32 * (GROUPS // U))
                reached(sp, Node.h1_store[k], 16 * (GROUPS // U))
            sp.wait_ge(s_tails, 64)
            sp.wait_ge(s_dinv, 1)
            sp.sem_inc(s_stage, 1)

            def dest_load(g, s, q):
                freed(sp, Dest.sum2, g, U)
                hold(sp, "sp")
                sp.dma_start(mask_a[:, s, :], flags_of(same_prev_d, g)).then_inc(Dest.load[s].sem, 16)
                freed(sp, Dest.z, g, U)
                hold(sp, "sp")
                sp.dma_start(S1L[s], cols_of(sum1T_tab, g)).then_inc(Dest.load[s].sem, 16)

            def dest_store(g, s, q):
                done(sp, Dest.x1, g)
                hold(sp, "sp")
                sp.dma_start(rows_of(x1_tab, g), by_tile(X1D[s])).then_inc(Dest.x1_store[s].sem, 16)

            def dest_table_store(g, s, q):
                done(sp, Dest.mr, g)
                hold(sp, "sp")
                sp.dma_start(rows_of(message_tab[0], g), by_tile(MD[s])).then_inc(Dest.store[s].sem, 16)
                done(sp, Dest.ownr, g)
                hold(sp, "sp")
                sp.dma_start(cols_of(ownT_tab[0], g), OD[s]).then_inc(Dest.store[s].sem, 16)

            pipelined(sp, GROUPS, [(0, dest_load), (8, dest_store), (12, dest_table_store)])
            for k in range(U):
                reached(sp, Dest.x1_store[k], 16 * (GROUPS // U))
                reached(sp, Dest.store[k], 32 * (GROUPS // U))
            sp.sem_inc(s_stage, 1)

            for l in range(LAYERS):
                def conv_load(g, s, q, l=l):
                    n = l * GROUPS + g
                    if l == 0:
                        freed(sp, Conv.tm, n, U)
                        hold(sp, "sp")
                        sp.dma_start(by_tile(MG[s]), rows_of(message_local, g)).then_inc(Conv.fill[s].sem, 16)
                    freed(sp, Conv.scan, n, U)
                    hold(sp, "sp")
                    sp.dma_start(mask_a[:, s, :], flags_of(neg_prev_d, g)).then_inc(Conv.load[s].sem, 16)
                    freed(sp, Conv.add, n, U)
                    hold(sp, "sp")
                    sp.dma_start(OL[s], cols_of(ownT_tab[l], g)).then_inc(Conv.load[s].sem, 16)
                    if l == LAYERS - 1:
                        freed(sp, Conv.x2, g, U)
                        hold(sp, "sp")
                        sp.dma_start(by_tile(X1L[s]), rows_of(x1_tab, g)).then_inc(Conv.x1_load[s].sem, 16)

                def conv_store(g, s, q, l=l):
                    n = l * GROUPS + g
                    if l < LAYERS - 1:
                        done(sp, Conv.mr, n)
                        hold(sp, "sp")
                        sp.dma_start(rows_of(message_tab[l + 1], g), by_tile(MRN[s])).then_inc(Conv.store[s].sem, 16)
                        done(sp, Conv.ownr, n)
                        hold(sp, "sp")
                        sp.dma_start(cols_of(ownT_tab[l + 1], g), OWN[s]).then_inc(Conv.store[s].sem, 16)
                    else:
                        done(sp, Conv.x2, g)
                        hold(sp, "sp")
                        sp.dma_start(rows_of(x2_tab, g), by_tile(X2[s])).then_inc(Conv.store[s].sem, 16)
                        done(sp, Conv.g, g)
                        hold(sp, "sp")
                        sp.dma_start(rows_of(g_tab, g), by_tile(G2[s])).then_inc(Conv.store[s].sem, 16)

                pipelined(sp, GROUPS, [(0, conv_load), (7, conv_store)])
                for k in range(U):
                    reached(sp, Conv.store[k], 32 * (l + 1) * (GROUPS // U))
                sp.sem_inc(s_stage, 1)

            def gcn_load(g, s, q):
                freed(sp, Gcn.tg, g, U)
                hold(sp, "sp")
                sp.dma_start(by_tile(GG[s]), rows_of(h1_local, g)).then_inc(Gcn.fill[s].sem, 16)
                freed(sp, Gcn.td, g, U)
                hold(sp, "sp")
                sp.dma_start(by_tile(GD[s]), rows_of(g_tab, g)).then_inc(Gcn.load[s].sem, 16)
                freed(sp, Gcn.scan, g, U)
                hold(sp, "sp")
                sp.dma_start(mask_a[:, s, :], flags_of(same_prev_d, g)).then_inc(Gcn.load[s].sem, 16)
                freed(sp, Gcn.xb, g, U)
                hold(sp, "sp")
                sp.dma_start(by_tile(X2L[s]), rows_of(x2_tab, g)).then_inc(Gcn.load[s].sem, 16)

            def gcn_x3_store(g, s, q):
                done(sp, Gcn.x3m, g)
                hold(sp, "sp")
                sp.dma_start(rows_of(x3_last_tab, g), by_tile(X3M[s])).then_inc(Gcn.x3_store[s].sem, 16)

            def gcn_store(g, s, q):
                done(sp, Gcn.ntr, g)
                hold(sp, "sp")
                sp.dma_start(rows_of(nt_tab, g), by_tile(NT3[s])).then_inc(Gcn.store[s].sem, 16)
                done(sp, Gcn.ntm, g)
                hold(sp, "sp")
                sp.dma_start(rows_of(nt_last_tab, g), by_tile(NTM[s])).then_inc(Gcn.store[s].sem, 16)

            pipelined(sp, GROUPS, [(0, gcn_load), (6, gcn_x3_store), (10, gcn_store)])
            for k in range(U):
                reached(sp, Gcn.x3_store[k], 16 * (GROUPS // U))
                reached(sp, Gcn.store[k], 32 * (GROUPS // U))
            sp.sem_inc(s_stage, 1)

            def gat_load(g, s, q):
                G = GROUPS - 1 - g
                freed(sp, Gat.ts, g, U)
                hold(sp, "sp")
                sp.dma_start(by_tile(NS[s]), rows_of(nt_local, G)).then_inc(Gat.fill[s].sem, 16)
                freed(sp, Gat.td, g, U)
                hold(sp, "sp")
                sp.dma_start(by_tile(NM[s]), rows_of(nt_last_tab, G)).then_inc(Gat.load[s].sem, 16)
                freed(sp, Gat.spread, g, U)
                freed(sp, Gat.xscan, g, U)
                hold(sp, "sp")
                sp.dma_start(mask_a[:, s, :], flags_of(same_next_d, G)).then_inc(Gat.load[s].sem, 16)
                freed(sp, Gat.tx, g, U)
                hold(sp, "sp")
                sp.dma_start(by_tile(XM[s]), rows_of(x3_last_tab, G)).then_inc(Gat.load[s].sem, 16)
                freed(sp, Gat.drop, g, U)
                hold(sp, "sp")
                sp.dma_start(mask_b[:, s, :], flags_of(neg_next_d, G)).then_inc(Gat.neg_load[s].sem, 16)

            pipelined(sp, GROUPS, [(0, gat_load)])

        @block.gpsimd
        def _(pool):
            pool.memset(ident[:, :], 0.0).then_inc(s_const, 1)
            pool.memset(head_mask[:, :], 1.0).then_inc(s_const, 1)
            pool.memset(zeros[:, :], 0.0).then_inc(s_const, 1)
            pool.memset(ones[:, :], 1.0).then_inc(s_const, 1)
            pool.memset(eps[:, :], EPS).then_inc(s_const, 1)
            pool.memset(ones3[:, :], 1.0).then_inc(s_const, 1)
            pool.wait_ge(s_const, 6)
            pool.affine_select(out=ident[:, :], in_=ident[:, :], compare_op=ALU.not_equal, fill=1.0,
                               base=0, pattern=[[-1, 128]], channel_multiplier=1).then_inc(s_const, 1)
            pool.affine_select(out=head_mask[:, :], in_=head_mask[:, :], compare_op=ALU.is_ge, fill=0.0,
                               base=0, pattern=[[-HC, HEADS], [0, HC]], channel_multiplier=1).then_inc(s_const, 1)
            pool.wait_ge(s_const, 8)
            pool.affine_select(out=head_mask[:, :], in_=head_mask[:, :], compare_op=ALU.is_ge, fill=0.0,
                               base=HC - 1, pattern=[[HC, HEADS], [0, HC]], channel_multiplier=-1).then_inc(s_const, 1)
            pool.iota(slot_i[:, :], pattern=[[128, TILES]], base=0, channel_multiplier=1).then_inc(s_const, 1)
            pool.wait_ge(s_cols, 1)

            def gather4(s, rows, table, gathered, limit=None, at=0):
                for j in range(TPG):
                    kw = {} if limit is None else {"bounds_check": limit, "oob_is_err": False}
                    pool.indirect_dma_start(out=rows[s][:, j * F:(j + 1) * F], out_offset=None, in_=table,
                                            in_offset=bass.IndirectOffsetOnAxis(ap=gi[:, s, at + j:at + j + 1], axis=0),
                                            **kw).then_inc(gathered[s].sem, 16)

            def source_gather(g, s, q):
                freed(pool, Node.xn0, g, U)
                freed(pool, Node.xb, g, U)
                hold(pool, "pool")
                pool.tensor_copy(gi[:, s, 0:TPG], src_c[:, ds(g * TPG, TPG)]).then_inc(Node.idx.sem, 1)
                pool.tensor_copy(gi[:, s, TPG:], dst_i[:, ds(g * TPG, TPG)]).then_inc(Node.idx.sem, 1)
                reached(pool, Node.idx, g * 2 + 2)
                hold(pool, "pool")
                gather4(s, X, x, Node.gather)
                for j in range(TPG):
                    pool.indirect_dma_start(out=deg[:, s, j:j + 1], out_offset=None, in_=node_vec.unsqueeze(1),
                                            in_offset=bass.IndirectOffsetOnAxis(ap=gi[:, s, TPG + j:TPG + j + 1], axis=0)
                                            ).then_inc(Node.gather[s].sem, 16)

            pipelined(pool, GROUPS, [(0, source_gather)])

            pool.wait_ge(s_init, 16)
            with pool.Fori(0, TILES // PT) as i:
                pool.tensor_copy(now_i[:, :], last_i[:, ds(i * PT, PT)]).then_inc(s_slot, 1)
                pool.tensor_copy(now_v[:, :], slot_i[:, ds(i * PT, PT)]).then_inc(s_slot, 1)
                pool.wait_ge(s_slot, i * 2 + 2)
                hold(pool, "pool")
                for k in range(PT):
                    pool.indirect_dma_start(out=slot_of_node, out_offset=bass.IndirectOffsetOnAxis(ap=now_i[:, k:k + 1], axis=0),
                                            in_=now_v[:, k:k + 1], in_offset=None,
                                            bounds_check=NODES - 1, oob_is_err=False).then_inc(s_placed, 16)
                pool.wait_ge(s_placed, (i + 1) * (16 * PT))
                hold(pool, "pool")
            with pool.Fori(0, TILES // PT) as i:
                pool.tensor_copy(now_i[:, :], src_c[:, ds(i * PT, PT)]).then_inc(s_from, 1)
                pool.wait_ge(s_from, i * 2 + 1)
                hold(pool, "pool")
                for k in range(PT):
                    pool.indirect_dma_start(out=now_v[:, k:k + 1], out_offset=None, in_=slot_of_node,
                                            in_offset=bass.IndirectOffsetOnAxis(ap=now_i[:, k:k + 1], axis=0)
                                            ).then_inc(s_got, 16)
                pool.wait_ge(s_got, (i + 1) * (16 * PT))
                hold(pool, "pool")
                pool.tensor_copy(from_i[:, ds(i * PT, PT)], now_v[:, :]).then_inc(s_from, 1)
                pool.wait_ge(s_from, i * 2 + 2)
                hold(pool, "pool")

            pool.wait_ge(s_stage, 1)

            def dest_gather(g, s, q):
                freed(pool, Dest.tn, g, U)
                freed(pool, Dest.xn0, g, U)
                freed(pool, Dest.xb, g, U)
                hold(pool, "pool")
                pool.tensor_copy(gi[:, s, 0:TPG], from_i[:, ds(g * TPG, TPG)]).then_inc(Dest.idx.sem, 1)
                pool.tensor_copy(gi[:, s, TPG:], dst_i[:, ds(g * TPG, TPG)]).then_inc(Dest.idx.sem, 1)
                reached(pool, Dest.idx, g * 2 + 2)
                hold(pool, "pool")
                gather4(s, NBG, nb1_tab, Dest.gather)
                gather4(s, XD, x, Dest.gather, at=TPG)

            pipelined(pool, GROUPS, [(0, dest_gather)])

            for l in range(LAYERS):
                pool.wait_ge(s_stage, 2 + l)

                def conv_gather(g, s, q, l=l):
                    n = l * GROUPS + g
                    freed(pool, Conv.tm, n, U)
                    if l == 0:
                        reached(pool, Conv.fill[s], q * 16 + 16)
                    hold(pool, "pool")
                    pool.tensor_copy(gi[:, s, 0:TPG], from_i[:, ds(g * TPG, TPG)]).then_inc(Conv.idx.sem, 1)
                    done(pool, Conv.idx, n)
                    hold(pool, "pool")
                    gather4(s, MG, message_tab[l], Conv.gather, limit=SLOTS - 1 if l == 0 else None)

                pipelined(pool, GROUPS, [(0, conv_gather)])

            pool.wait_ge(s_stage, 2 + LAYERS)

            def gcn_gather(g, s, q):
                reached(pool, Gcn.fill[s], q * 16 + 16)
                hold(pool, "pool")
                pool.tensor_copy(gi[:, s, 0:TPG], from_i[:, ds(g * TPG, TPG)]).then_inc(Gcn.idx.sem, 1)
                done(pool, Gcn.idx, g)
                hold(pool, "pool")
                gather4(s, GG, g_tab, Gcn.gather, limit=SLOTS - 1)

            pipelined(pool, GROUPS, [(0, gcn_gather)])

            pool.wait_ge(s_stage, 3 + LAYERS)

            def gat_gather(g, s, q):
                reached(pool, Gat.fill[s], q * 16 + 16)
                hold(pool, "pool")
                pool.tensor_copy(gi[:, s, 0:TPG], from_i[:, ds((GROUPS - 1 - g) * TPG, TPG)]).then_inc(Gat.idx.sem, 1)
                done(pool, Gat.idx, g)
                hold(pool, "pool")
                gather4(s, NS, nt_tab, Gat.gather, limit=SLOTS - 1)

            def gat_scatter(g, s, q):
                if not isinstance(g, int) or g >= U:
                    reached(pool, Gat.scatter[s], q * 64)
                    hold(pool, "pool")
                pool.tensor_copy(gi[:, s, TPG:], first_i[:, ds((GROUPS - 1 - g) * TPG, TPG)]).then_inc(Gat.out_idx.sem, 1)
                done(pool, Gat.out_idx, g)
                done(pool, Gat.oe, g)
                hold(pool, "pool")
                for j in range(TPG):
                    pool.indirect_dma_start(out=out, out_offset=bass.IndirectOffsetOnAxis(ap=gi[:, s, TPG + j:TPG + j + 1], axis=0),
                                            in_=OE[s][:, j * F:(j + 1) * F], in_offset=None,
                                            bounds_check=NODES - 1, oob_is_err=False).then_inc(Gat.scatter[s].sem, 16)

            pipelined(pool, GROUPS, [(0, gat_gather), (8, gat_scatter)])
            for k in range(U):
                reached(pool, Gat.scatter[k], 64 * (GROUPS // U))

        @block.vector
        def _(dve):
            link_count = [0]

            def link(ins):
                link_count[0] += 1
                ins.then_inc(s_setup, 1)
                dve.wait_ge(s_setup, link_count[0])

            link(dve.memset(pad_i[0:1, :], NOWHERE))
            link(dve.memset(pad_i[0:1, 0:1], -1))
            dve.memset(src_i[:, :], 0).then_inc(s_pad, 1)
            dve.memset(near_i[:, :, :], 0).then_inc(s_pad, 1)
            dve.memset(far_i[:, :], SLOTS).then_inc(s_far, 1)
            dve.wait_ge(s_near, 80)
            for n in range(3):
                dve.tensor_copy(near[:, n, :], near_i[:, n, :])
            link(dve.tensor_copy(near[:, 3, :], src_i[:, :]))
            before, itself, behind = near[:, 0, :], near[:, 1, :], near[:, 2, :]
            dve.tensor_tensor(rowf[:, 0, :], itself, before, ALU.is_equal)
            link(dve.tensor_tensor(rowf[:, 1, :], itself, behind, ALU.is_equal))
            dve.tensor_scalar(rowf[:, 2, :], rowf[:, 1, :], -1.0, 1.0, ALU.mult, ALU.add)
            dve.tensor_scalar(rowf[:, 3, :], rowf[:, 0, :], -1.0, 1.0, ALU.mult, ALU.add)
            dve.tensor_copy(flag_row[0], rowf[:, 0, :])
            dve.tensor_scalar(flag_row[1], rowf[:, 0, :], -1.0, NEG, ALU.add, ALU.mult)
            dve.tensor_copy(flag_row[2], rowf[:, 1, :])
            link(dve.tensor_scalar(flag_row[3], rowf[:, 1, :], -1.0, NEG, ALU.add, ALU.mult))
            dve.scalar_tensor_tensor(rowf[:, 4, :], itself, -float(NOWHERE), rowf[:, 2, :], ALU.add, ALU.mult)
            dve.scalar_tensor_tensor(rowf[:, 5, :], itself, -float(NOWHERE), rowf[:, 3, :], ALU.add, ALU.mult)
            link(dve.tensor_scalar(rowf[:, 6, :], itself, float(NODES - 1), None, ALU.min))
            dve.tensor_scalar(rowf[:, 4, :], rowf[:, 4, :], float(NOWHERE), None, ALU.add)
            dve.tensor_scalar(rowf[:, 5, :], rowf[:, 5, :], float(NOWHERE), None, ALU.add).then_inc(s_rows, 1)
            for n, dest in enumerate((last_i, first_i, dst_i, src_c, is_last)):
                dve.wait_ge(s_rowsT, n + 1)
                last = dve.tensor_copy(dest[:, :].rearrange("p (a b) -> p b a", b=2),
                                       bank[n][:, 0:2 * RR].rearrange("p (b a) -> p b a", b=2))
            last.then_inc(s_cols, 1)
            dve.wait_ge(s_act, 1)
            dve.wait_ge(s_w, 16 * (16 + 2 * LAYERS + 2 * HEADS))
            link(dve.tensor_scalar(scale_2[:, 0:4], scale_s[:, :], 2.0, None, ALU.mult))
            link(dve.tensor_scalar(scale_2[:, 4:5], scale_2[:, 2:3], -1.0, None, ALU.mult))
            dve.tensor_scalar(wc[:, 0, :], wn[:, 2, :], scale_2[:, 2:3], None, ALU.mult)
            dve.tensor_scalar(wc[:, 1, :], wn[:, 2, :], scale_2[:, 4:5], None, ALU.mult)
            link(dve.tensor_scalar(wc[:, 2, :], wn[:, 3, :], scale_2[:, 3:4], None, ALU.mult))
            dve.scalar_tensor_tensor(wc[:, 0, :], wn[:, 0, :], scale_2[:, 0:1], wc[:, 0, :], ALU.mult, ALU.add)
            dve.scalar_tensor_tensor(wc[:, 1, :], wn[:, 1, :], scale_2[:, 1:2], wc[:, 1, :], ALU.mult, ALU.add)
            dve.tensor_tensor(pt[:, :, :], wn[:, 8:12, :], wn[:, 4:8, :], ALU.subtract).then_inc(s_wc, 1)
            dve.wait_ge(s_wcT, 1)
            for n in range(3):
                last = dve.reduce_sum(small[:, n:n + 1], bank[0][:, n * F:(n + 1) * F], axis=AX.X)
            link(last)
            link(dve.reduce_sum(small[0:3, 3:4], bias_src[:, 0, :], axis=AX.X))
            link(dve.tensor_scalar(small[:, 0:3], small[:, 0:3], 1.0 / F, None, ALU.mult))
            link(dve.tensor_scalar(small[0:3, 3:4], small[0:3, 3:4], 1.0 / F, None, ALU.mult))
            for n in range(3):
                dve.tensor_scalar(wT[:, n, :], bank[0][:, n * F:(n + 1) * F], small[:, n:n + 1], None, ALU.subtract)
            link(dve.tensor_scalar(bias_src[:, 0, :], bias_src[:, 0, :], small[0:3, 3:4], None, ALU.subtract))
            link(dve.tensor_copy(bias_bf[:, :, :], bias_src[:, :, :]))
            link(dve.tensor_copy(bias_part[:, 0, :, :], bias_bf[:, :, :]))
            link(dve.tensor_tensor(bias_rest[:, :, :], bias_src[:, :, :], bias_part[:, 0, :, :], ALU.subtract))
            link(dve.tensor_copy(bias_bf[:, :, :], bias_rest[:, :, :]))
            link(dve.tensor_copy(bias_part[:, 1, :, :], bias_bf[:, :, :]))
            link(dve.tensor_tensor(bias_part[:, 2, :, :], bias_rest[:, :, :], bias_part[:, 1, :, :], ALU.subtract))
            dve.wait_ge(s_const, 9)
            link(dve.tensor_scalar(bias_rest[:, :, :], bias_part[:, 0, :, :], ident[0:3, 0:1], None, ALU.mult))
            for k in (1, 2):
                link(dve.scalar_tensor_tensor(bias_rest[:, :, :], bias_part[:, k, :, :], ident[0:3, k:k + 1], bias_rest[:, :, :],
                                              ALU.mult, ALU.add))
            for j in range(TPG):
                dve.tensor_copy(bias3[:, :, j * F:(j + 1) * F], bias_rest[:, :, :])
            for n in range(2):
                dve.tensor_scalar(attn_m[:, n, :], head_mask[:, :], attn_c[:, n:n + 1], None, ALU.mult)
            dve.tensor_tensor(conv_bias[:, :], conv_b[:, 0, :], conv_b[:, 1, :], ALU.add)
            dve.tensor_copy(thetaT[:, :, :], bank[1][:, :].rearrange("p (l f) -> p l f", l=LAYERS))
            dve.tensor_copy(ptT[:, :, :], bank[2][:, :].rearrange("p (l f) -> p l f", l=LAYERS)).then_inc(s_wt, 1)

            dve.wait_ge(s_flags, 64)

            def node_phases(base, P, sources):
                def finish(g, s, q):
                    n = base + g
                    done(dve, Node.x3, n)
                    if not sources:
                        if not isinstance(g, int) or g >= U:
                            reached(dve, Node.store[s], q * 16)
                        else:
                            done(dve, Node.xn2, GROUPS - 1)
                    dve.tensor_tensor(XO[s][:P], X1[s][:P], bank[2][:P, :], ALU.add).then_inc(Node.xo.sem, 1)

                def stats_x(g, s, q):
                    if sources:
                        reached(dve, Node.gather[s], q * 128 + 128)
                    else:
                        reached(dve, Node.load[s], q * 16 + 16)
                    stats(dve, X[s], st0[:, s], Node.bn0, P)

                def beta_x(g, s, q):
                    if sources:
                        hold(dve, "dve")
                        dve.reciprocal(rdeg[:, ds(g * TPG, TPG)], deg[:, s, :]).then_inc(Node.rdeg.sem, 1)
                    dve.tensor_tensor(by_tile(XB[s])[:P], by_tile(X[s])[:P], beta_b[:P, :].unsqueeze(1).broadcast_to((P, TPG, F)), ALU.add).then_inc(Node.xb.sem, 1)

                def moments_x(g, s, q):
                    moments(dve, mv0[:, s], st0[:, s], Node.bn0, Node.mv0, base + g, P)

                def inverse_x(g, s, q):
                    inverse(dve, rs0[:, s], sd0[:, s], Node.sd0, Node.rs0, base + g, P)

                def shift_x(g, s, q):
                    shift(dve, nm0[:, s], mv0[:, s], rs0[:, s], Node.rs0, Node.nm0, base + g, P)

                def inverse_z(g, s, q):
                    inverse(dve, rsz[:, s], sdz[:, s], Node.sdz, Node.rsz, base + g, P)

                def scale_z(g, s, q):
                    done(dve, Node.rsz, base + g)
                    for j in range(TPG):
                        last = dve.scalar_tensor_tensor(X1[s][:P, j * F:(j + 1) * F], z_bank(s, sources)[:P, j * F:(j + 1) * F], rsz[:P, s, j:j + 1],
                                                        gamma_b[:P, :], ALU.mult, ALU.mult)
                    last.then_inc(Node.w.sem, 1)

                def add_x1(g, s, q):
                    done(dve, Node.w, base + g)
                    dve.tensor_tensor(X1[s][:P], X1[s][:P], XB[s][:P], ALU.add).then_inc(Node.x1.sem, 1)

                def stats_x1(g, s, q):
                    done(dve, Node.x1, base + g)
                    stats(dve, X1[s], st1[:, s], Node.bn1, P)

                def moments_x1(g, s, q):
                    moments(dve, mv1[:, s], st1[:, s], Node.bn1, Node.mv1, base + g, P)

                def inverse_x1(g, s, q):
                    inverse(dve, rs1[:, s], sd1[:, s], Node.sd1, Node.rs1, base + g, P)

                def shift_x1(g, s, q):
                    shift(dve, nm1[:, s], mv1[:, s], rs1[:, s], Node.rs1, Node.nm1, base + g, P)

                def scan_sources(g, s, q):
                    n = base + g
                    done(dve, Node.h0, n)
                    reached(dve, Node.mask[s], q * 16 + 16)
                    first = isinstance(g, int) and g == 0
                    if not first:
                        reached(dve, Node.sum1, g)
                        reached(dve, Node.cnt, g)
                    if not (isinstance(g, int) and g < U):
                        reached(dve, Node.sum_store[s], q * 32)
                    before_ = (s - 1) % U
                    dve.tensor_tensor_scan(SUM1T[s], mask_a[:, s, :], H0T[s], 0.0 if first else SUM1T[before_][:, GW - 1:GW],
                                           ALU.mult, ALU.add).then_inc(Node.sum1.sem, 1)
                    dve.tensor_tensor_scan(CNT[s], mask_a[:, s, :], ones[:, :], 0.0 if first else CNT[before_][:, GW - 1:GW],
                                           ALU.mult, ALU.add).then_inc(Node.cnt.sem, 1)

                def mean_sources(g, s, q):
                    done(dve, Node.rdeg, g)
                    done(dve, Node.ts, g)
                    if not (isinstance(g, int) and g < U):
                        reached(dve, Node.sum_store[s], q * 32)
                    hold(dve, "dve")
                    for j in range(TPG):
                        dve.tensor_scalar(NBR[s][:, j * F:(j + 1) * F], bank[3][:, j * F:(j + 1) * F], rdeg[:, ds(g * TPG + j, 1)], None, ALU.mult)
                    dve.tensor_copy(count[:, ds(g * TPG, TPG)], bank[4][:, 0:TPG]).then_inc(Node.nb.sem, 1)

                def stats_x3(g, s, q):
                    done(dve, Node.xo, g)
                    stats(dve, XO[s], st2[:, s], Node.bn2, P)

                def moments_x3(g, s, q):
                    moments(dve, mv2[:, s], st2[:, s], Node.bn2, Node.mv2, g, P)

                def inverse_x3(g, s, q):
                    inverse(dve, rs2[:, s], sd2[:, s], Node.sd2, Node.rs2, g, P)

                def shift_x3(g, s, q):
                    shift(dve, nm2[:, s], mv2[:, s], rs2[:, s], Node.rs2, Node.nm2, g, P)

                if sources:
                    return [(8, finish), (6, mean_sources), (4, inverse_z), (0, stats_x), (4, scale_z), (9, stats_x3), (4, add_x1), (0, beta_x),
                            (0, moments_x), (4, stats_x1), (9, moments_x3), (1, inverse_x), (5, inverse_x1), (4, moments_x1), (1, shift_x),
                            (10, inverse_x3), (5, shift_x1), (4, scan_sources), (10, shift_x3)]
                return [(8, finish), (0, stats_x), (4, inverse_z), (0, beta_x), (4, scale_z), (0, moments_x), (4, add_x1), (1, inverse_x),
                        (5, inverse_x1), (4, stats_x1), (1, shift_x), (5, shift_x1), (4, moments_x1)]

            pipelined(dve, GROUPS, node_phases(0, 128, True))
            pipelined(dve, NODE_GROUPS, node_phases(GROUPS, NP, False))
            done(dve, Node.nb, GROUPS - 1)
            link(dve.tensor_scalar(count[:, :], count[:, :], 1.0, None, ALU.add))
            dve.sem_inc(s_sd, 1)
            dve.wait_ge(s_sd, 2)
            dve.reciprocal(dinv[:, :], dinv[:, :]).then_inc(s_dinv, 1)

            dve.wait_ge(s_stage, 1)

            def dest_stats(g, s, q):
                reached(dve, Dest.gather[s], q * 128 + 128)
                stats(dve, XD[s], st0[:, s], Dest.bn0)

            def dest_beta(g, s, q):
                hold(dve, "dve")
                dve.tensor_copy(rdg[:, s, :], rdeg[:, ds(g * TPG, TPG)])
                dve.tensor_tensor(by_tile(XBD[s]), by_tile(XD[s]), beta_b[:, :].unsqueeze(1).broadcast_to((128, TPG, F)), ALU.add).then_inc(Dest.xb.sem, 1)

            def dest_moments(g, s, q):
                moments(dve, mv0[:, s], st0[:, s], Dest.bn0, Dest.mv0, g)

            def dest_scan(g, s, q):
                done(dve, Dest.tn, g)
                reached(dve, Dest.load[s], q * 32 + 32)
                first = isinstance(g, int) and g == 0
                if not first:
                    reached(dve, Dest.sum2, g)
                dve.tensor_tensor_scan(S2T[s], mask_a[:, s, :], bank[0][:, :], 0.0 if first else S2T[(s - 1) % U][:, GW - 1:GW],
                                       ALU.mult, ALU.add).then_inc(Dest.sum2.sem, 1)

            def dest_inverse(g, s, q):
                inverse(dve, rs0[:, s], sd0[:, s], Dest.sd0, Dest.rs0, g)

            def dest_shift(g, s, q):
                shift(dve, nm0[:, s], mv0[:, s], rs0[:, s], Dest.rs0, Dest.nm0, g)

            def dest_z(g, s, q):
                done(dve, Dest.zs, g)
                dve.tensor_tensor(ZM[s], ZS[s], bank[2][:, :], ALU.add).then_inc(Dest.zm.sem, 1)

            def dest_inverse_z(g, s, q):
                inverse(dve, rsz[:, s], sdz[:, s], Dest.sdz, Dest.rsz, g)

            def dest_scale_z(g, s, q):
                done(dve, Dest.rsz, g)
                for j in range(TPG):
                    last = dve.scalar_tensor_tensor(ZM[s][:, j * F:(j + 1) * F], ZM[s][:, j * F:(j + 1) * F], rsz[:, s, j:j + 1],
                                                    gamma_b[:, :], ALU.mult, ALU.mult)
                last.then_inc(Dest.w.sem, 1)

            def dest_x1(g, s, q):
                done(dve, Dest.w, g)
                if not (isinstance(g, int) and g < U):
                    reached(dve, Dest.x1_store[s], q * 16)
                dve.tensor_tensor(X1D[s], ZM[s], XBD[s], ALU.add).then_inc(Dest.x1.sem, 1)

            def dest_stats1(g, s, q):
                done(dve, Dest.x1, g)
                stats(dve, X1D[s], st1[:, s], Dest.bn1)

            def dest_moments1(g, s, q):
                moments(dve, mv1[:, s], st1[:, s], Dest.bn1, Dest.mv1, g)

            def dest_inverse1(g, s, q):
                inverse(dve, rs1[:, s], sd1[:, s], Dest.sd1, Dest.rs1, g)

            def dest_shift1(g, s, q):
                shift(dve, nm1[:, s], mv1[:, s], rs1[:, s], Dest.rs1, Dest.nm1, g)

            pipelined(dve, GROUPS, [(5, dest_inverse_z), (4, dest_z), (5, dest_scale_z), (1, dest_scan), (5, dest_x1), (0, dest_stats),
                                    (5, dest_stats1), (0, dest_beta), (0, dest_moments), (5, dest_moments1), (1, dest_inverse),
                                    (6, dest_inverse1), (1, dest_shift), (6, dest_shift1)])

            for l in range(LAYERS):
                dve.wait_ge(s_stage, 2 + l)

                def conv_scan(g, s, q, l=l):
                    n = l * GROUPS + g
                    done(dve, Conv.tm, n)
                    reached(dve, Conv.load[s], (q + l * (GROUPS // U)) * 32 + 32)
                    first = isinstance(g, int) and g == 0
                    if not first:
                        reached(dve, Conv.scan, n)
                    dve.tensor_tensor_scan(SC[s], mask_a[:, s, :], bank[0][:, :], -NEG if first else SC[(s - 1) % U][:, GW - 1:GW],
                                           ALU.add, ALU.max).then_inc(Conv.scan.sem, 1)
                    done(dve, Conv.scan, n)
                    freed(dve, Conv.yn, n, U)
                    dve.tensor_tensor(AD[s], SC[s], OL[s], ALU.add).then_inc(Conv.add.sem, 1)

                def conv_x2(g, s, q, l=l):
                    done(dve, Conv.tb, g)
                    reached(dve, Conv.x1_load[s], q * 16 + 16)
                    if not (isinstance(g, int) and g < U):
                        reached(dve, Conv.store[s], (q + l * (GROUPS // U)) * 32)
                    dve.tensor_tensor(X2[s], X1L[s], bank[3][:, :], ALU.add).then_inc(Conv.x2.sem, 1)
                    done(dve, Conv.x2, g)
                    stats(dve, X2[s], st0[:, s], Conv.bn)
                    moments(dve, mv0[:, s], st0[:, s], Conv.bn, Conv.mv, g)

                def conv_scale(g, s, q):
                    done(dve, Conv.sd, g)
                    dve.reciprocal(rs0[:, s], sd0[:, s]).then_inc(Conv.rs.sem, 1)
                    done(dve, Conv.rs, g)
                    hold(dve, "dve")
                    dve.tensor_tensor(rs1[:, s], rs0[:, s], dinv[:, ds(g * TPG, TPG)], ALU.mult).then_inc(Conv.rd.sem, 1)
                    done(dve, Conv.rd, g)
                    dve.scalar_tensor_tensor(nm0[:, s], mv0[:, s, :, 0], -1.0, rs1[:, s], ALU.mult, ALU.mult).then_inc(Conv.nm.sem, 1)

                pipelined(dve, GROUPS, [(0, conv_scan)] + ([(3, conv_x2), (4, conv_scale)] if l == LAYERS - 1 else []))

            dve.wait_ge(s_stage, 2 + LAYERS)

            def gcn_scan(g, s, q):
                done(dve, Gcn.gt, g)
                reached(dve, Gcn.load[s], q * 48 + 48)
                first = isinstance(g, int) and g == 0
                if not first:
                    reached(dve, Gcn.scan, g)
                dve.tensor_tensor_scan(SG[s], mask_a[:, s, :], GTs[s], 0.0 if first else SG[(s - 1) % U][:, GW - 1:GW],
                                       ALU.mult, ALU.add).then_inc(Gcn.scan.sem, 1)

            def gcn_own(g, s, q):
                done(dve, Gcn.scan, g)
                done(dve, Gcn.td, g)
                dve.tensor_tensor(UG[s], SG[s], bank[1][:, :], ALU.add).then_inc(Gcn.u.sem, 1)
                dve.tensor_tensor(by_tile(XB2[s]), by_tile(X2L[s]), gcn_b_b[:, :].unsqueeze(1).broadcast_to((128, TPG, F)), ALU.add).then_inc(Gcn.xb.sem, 1)

            def gcn_x3(g, s, q):
                done(dve, Gcn.w, g)
                done(dve, Gcn.xb, g)
                if not (isinstance(g, int) and g < U):
                    reached(dve, Gcn.xn, g - U + 1)
                    reached(dve, Gcn.ntm, g - U + 1)
                hold(dve, "dve")
                for j in range(TPG):
                    last = dve.scalar_tensor_tensor(X3[s][:, j * F:(j + 1) * F], bank[2][:, j * F:(j + 1) * F], dinv[:, ds(g * TPG + j, 1)],
                                                    XB2[s][:, j * F:(j + 1) * F], ALU.mult, ALU.add)
                last.then_inc(Gcn.x3.sem, 1)
                dve.tensor_copy(lastg[:, s], is_last[:, ds(g * TPG, TPG)]).then_inc(Gcn.last.sem, 1)
                done(dve, Gcn.x3, g)
                stats(dve, X3[s], st1[:, s], Gcn.bn)
                moments(dve, mv1[:, s], st1[:, s], Gcn.bn, Gcn.mv, g)
                if not (isinstance(g, int) and g < U):
                    reached(dve, Gcn.x3_store[s], q * 16)
                done(dve, Gcn.last, g)
                for j in range(TPG):
                    last = dve.tensor_scalar(X3M[s][:, j * F:(j + 1) * F], X3[s][:, j * F:(j + 1) * F], lastg[:, s, j:j + 1], None, ALU.mult)
                last.then_inc(Gcn.x3m.sem, 1)

            def gcn_inverse(g, s, q):
                inverse(dve, rs1[:, s], sd1[:, s], Gcn.sd, Gcn.rs, g)

            def gcn_shift(g, s, q):
                shift(dve, nm1[:, s], mv1[:, s], rs1[:, s], Gcn.rs, Gcn.nm, g)

            pipelined(dve, GROUPS, [(3, gcn_x3), (1, gcn_scan), (4, gcn_inverse), (1, gcn_own), (4, gcn_shift)])

            dve.wait_ge(s_stage, 3 + LAYERS)

            def back(t):
                return t[:, ::-1]

            def gat_leaky(g, s, q):
                done(dve, Gat.nts, g)
                freed(dve, Gat.lg, g, U)
                dve.scalar_tensor_tensor(LKS[s], NTS[s], SLOPE, NTS[s], ALU.mult, ALU.max).then_inc(Gat.lks.sem, 1)

            def gat_leaky_d(g, s, q):
                done(dve, Gat.ntd, g)
                freed(dve, Gat.lg, g, U)
                dve.scalar_tensor_tensor(LKD[s], NTD[s], SLOPE, NTD[s], ALU.mult, ALU.max).then_inc(Gat.lkd.sem, 1)

            def spread(signal_, result, rows, g, s):
                first = isinstance(g, int) and g == 0
                if not first:
                    reached(dve, signal_, g)
                dve.tensor_tensor_scan(back(result[s]), back(mask_a[:, s, :]), back(rows),
                                       0.0 if first else result[(s - 1) % U][:, 0:1], ALU.mult, ALU.add).then_inc(signal_.sem, 1)

            def gat_spread(g, s, q):
                done(dve, Gat.td, g)
                reached(dve, Gat.load[s], q * 48 + 48)
                freed(dve, Gat.ntd, g, U)
                spread(Gat.spread, NDT, bank[1][:, :], g, s)

            def gat_spread_x(g, s, q):
                done(dve, Gat.tx, g)
                freed(dve, Gat.txb, g, U)
                spread(Gat.xscan, X3T, bank[2][:, :], g, s)

            def gat_max(g, s, q):
                done(dve, Gat.lgs, g)
                reached(dve, Gat.neg_load[s], q * 16 + 16)
                first = isinstance(g, int) and g == 0
                if not first:
                    reached(dve, Gat.mscan, g)
                    dve.tensor_copy(MX[s][:, GW:GW + 1], MX[(s - 1) % U][:, 0:1])
                else:
                    dve.memset(MX[s][:, GW:GW + 1], 0.0)
                dve.tensor_tensor_scan(back(MX[s][:, 0:GW]), back(mask_b[:, s, :]), back(LGS[s]),
                                       -NEG if first else MX[(s - 1) % U][:, 0:1], ALU.add, ALU.max).then_inc(Gat.mscan.sem, 1)

            def gat_exponents(g, s, q):
                done(dve, Gat.mscan, g)
                dve.tensor_tensor(CE[s], MX[s][:, 1:GW + 1], MX[s][:, 0:GW], ALU.subtract).then_inc(Gat.diff.sem, 1)
                dve.tensor_tensor(PE_[s], LGS[s], MX[s][:, 0:GW], ALU.subtract).then_inc(Gat.sub.sem, 1)
                done(dve, Gat.diff, g)
                dve.scalar_tensor_tensor(CE[s], CE[s], 0.0, mask_b[:, s, :], ALU.min, ALU.add).then_inc(Gat.drop.sem, 1)

            def gat_sum(g, s, q):
                done(dve, Gat.ec, g)
                done(dve, Gat.ep, g)
                dve.tensor_tensor(NTS[s], PE_[s], NTS[s], ALU.mult).then_inc(Gat.pn.sem, 1)
                first = isinstance(g, int) and g == 0
                if not first:
                    reached(dve, Gat.den, g)
                dve.tensor_tensor_scan(back(DEN[s]), back(CE[s]), back(PE_[s]), 0.0 if first else DEN[(s - 1) % U][:, 0:1],
                                       ALU.mult, ALU.add).then_inc(Gat.den.sem, 1)
                if not first:
                    reached(dve, Gat.num, g)
                done(dve, Gat.pn, g)
                dve.tensor_tensor_scan(back(NUM[s]), back(CE[s]), back(NTS[s]), 0.0 if first else NUM[(s - 1) % U][:, 0:1],
                                       ALU.mult, ALU.add).then_inc(Gat.num.sem, 1)

            def gat_inverse(g, s, q):
                done(dve, Gat.tden, g)
                dve.reciprocal(rden[:, s], bank[4][:, 0:TPG * HEADS]).then_inc(Gat.rden.sem, 1)

            def gat_ratio(g, s, q):
                done(dve, Gat.rden, g)
                done(dve, Gat.tnum, g)
                if not (isinstance(g, int) and g < U):
                    reached(dve, Gat.scatter[s], q * 64)
                dve.tensor_tensor(OE[s].rearrange("p (h c) -> p h c", c=HC), bank[5][:, :].rearrange("p (h c) -> p h c", c=HC),
                                  rden[:, s].unsqueeze(2).broadcast_to((128, TPG * HEADS, HC)), ALU.mult).then_inc(Gat.ratio.sem, 1)

            def gat_out(g, s, q):
                done(dve, Gat.ratio, g)
                done(dve, Gat.txb, g)
                dve.tensor_tensor(OE[s], OE[s], bank[3][:, :], ALU.add).then_inc(Gat.oe.sem, 1)

            pipelined(dve, GROUPS, [(6, gat_inverse), (1, gat_spread), (6, gat_ratio), (1, gat_spread_x), (6, gat_out), (5, gat_sum),
                                    (4, gat_max), (1, gat_leaky), (4, gat_exponents), (2, gat_leaky_d)])

        @block.scalar
        def _(act):
            act.wait_ge(s_w, 16 * (16 + 2 * LAYERS + 2 * HEADS))
            act.activation(scale_s[:, :], scale_l[:, :], ACT.Sigmoid).then_inc(s_act, 1)

            def root(sd, mv, s_sd_, s_mv, n, P=128):
                done(act, s_mv, n)
                act.activation(sd[:P, :], mv[:P, :, 1], ACT.Sqrt, bias=eps[:P, :]).then_inc(s_sd_.sem, 1)

            def node_phases(base, P, sources):
                def root_x(g, s, q):
                    root(sd0[:, s], mv0[:, s], Node.sd0, Node.mv0, base + g, P)

                def turned_x(g, s, q):
                    done(act, Node.t0, base + g)
                    if sources and not (isinstance(g, int) and g < U):
                        reached(act, Node.sum1, g - U + 1)
                    act.activation(by_tile(H0T[s])[:, :, 0:P], by_tile(bank[0][:, :])[:, :, 0:P], ACT.Relu).then_inc(Node.h0.sem, 1)

                def square_z(g, s, q):
                    n = base + g
                    done(act, Node.z, n)
                    for j in range(TPG):
                        last = act.activation(junk[:P, j * F:(j + 1) * F], z_bank(s, sources)[:P, j * F:(j + 1) * F], ACT.Square, accum_out=ssq[:P, s, j:j + 1])
                    last.then_inc(Node.ssq.sem, 1)
                    done(act, Node.ssq, n)
                    act.activation(sdz[:P, s, :], ssq[:P, s, :], ACT.Sqrt, bias=eps[:P, :], scale=1.0 / F).then_inc(Node.sdz.sem, 1)

                def root_x1(g, s, q):
                    root(sd1[:, s], mv1[:, s], Node.sd1, Node.mv1, base + g, P)

                def turned_x1(g, s, q):
                    done(act, Node.t1, base + g)
                    act.activation(by_tile(H1T[s])[:, :, 0:P], by_tile(bank[1][:, :])[:, :, 0:P], ACT.Relu).then_inc(Node.h1.sem, 1)

                def norm_x(g, s, q):
                    norm_rows(act, XN0[s], X[s], rs0[:, s], nm0[:, s], Node.nm0, Node.xn0, base + g, P)

                def norm_x1(g, s, q):
                    if not (isinstance(g, int) and g < U):
                        if sources:
                            reached(act, Node.h1_store[s], q * 16)
                    elif not sources:
                        reached(act, Node.h1_store[s], 16 * (GROUPS // U))
                    norm_rows(act, XN1[s], X1[s], rs1[:, s], nm1[:, s], Node.nm1, Node.xn1, base + g, P)

                def message_rows(g, s, q):
                    done(act, Node.msg, g)
                    if not (isinstance(g, int) and g < U):
                        reached(act, Node.msg_store[s], q * 16)
                    act.activation(MR[s], wide[:, GW:], ACT.Copy).then_inc(Node.mr.sem, 1)

                def root_x3(g, s, q):
                    root(sd2[:, s], mv2[:, s], Node.sd2, Node.mv2, g)

                def norm_x3(g, s, q):
                    norm_rows(act, XN2[s], XO[s], rs2[:, s], nm2[:, s], Node.nm2, Node.xn2, g)

                def turned_x3(g, s, q):
                    done(act, Node.t2, g)
                    act.activation(H2T[s], bank[5][:, :], ACT.Relu).then_inc(Node.h2.sem, 1)

                def nt_rows(g, s, q):
                    done(act, Node.nt, g)
                    if not (isinstance(g, int) and g < U):
                        reached(act, Node.nt_store[s], q * 16)
                    act.activation(NTR[s], bank[5][:, :], ACT.Copy).then_inc(Node.ntr.sem, 1)

                if sources:
                    return [(13, nt_rows), (1, root_x), (5, root_x1), (10, root_x3), (7, turned_x1), (3, turned_x), (12, turned_x3),
                            (8, message_rows), (2, norm_x), (6, norm_x1), (3, square_z), (11, norm_x3)]
                return [(4, square_z), (1, root_x), (5, root_x1), (7, turned_x1), (3, turned_x), (2, norm_x), (6, norm_x1)]

            pipelined(act, GROUPS, node_phases(0, 128, True))
            pipelined(act, NODE_GROUPS, node_phases(GROUPS, NP, False))
            act.wait_ge(s_sd, 1)
            act.activation(dinv[:, :], count[:, :], ACT.Sqrt).then_inc(s_sd, 1)

            act.wait_ge(s_stage, 1)

            def dest_root(g, s, q):
                root(sd0[:, s], mv0[:, s], Dest.sd0, Dest.mv0, g)

            def dest_turned(g, s, q):
                done(act, Dest.t0, g)
                act.activation(H0D[s], bank[1][:, :], ACT.Relu).then_inc(Dest.h0.sem, 1)

            def dest_mean(g, s, q):
                done(act, Dest.z, g)
                done(act, Dest.xb, g)
                for j in range(TPG):
                    last = act.activation(ZS[s][:, j * F:(j + 1) * F], bank[3][:, j * F:(j + 1) * F], ACT.Identity, scale=rdg[:, s, j:j + 1])
                last.then_inc(Dest.zs.sem, 1)

            def dest_square(g, s, q):
                done(act, Dest.zm, g)
                for j in range(TPG):
                    last = act.activation(junk[:, j * F:(j + 1) * F], ZM[s][:, j * F:(j + 1) * F], ACT.Square, accum_out=ssq[:, s, j:j + 1])
                last.then_inc(Dest.ssq.sem, 1)
                done(act, Dest.ssq, g)
                act.activation(sdz[:, s, :], ssq[:, s, :], ACT.Sqrt, bias=eps[:, :], scale=1.0 / F).then_inc(Dest.sdz.sem, 1)

            def dest_root1(g, s, q):
                root(sd1[:, s], mv1[:, s], Dest.sd1, Dest.mv1, g)

            def dest_turned1(g, s, q):
                done(act, Dest.t1, g)
                act.activation(H1D[s], bank[4][:, :], ACT.Relu).then_inc(Dest.h1.sem, 1)

            def dest_messages(g, s, q):
                done(act, Dest.msg, g)
                if not (isinstance(g, int) and g < U):
                    reached(act, Dest.store[s], q * 32)
                act.activation(MD[s], wide[:, GW:], ACT.Copy).then_inc(Dest.mr.sem, 1)
                done(act, Dest.own, g)
                act.activation(OD[s], bank[5][:, :], ACT.Identity, bias=conv_bias[:, 0:1]).then_inc(Dest.ownr.sem, 1)

            def dest_norm(g, s, q):
                norm_rows(act, XN0D[s], XD[s], rs0[:, s], nm0[:, s], Dest.nm0, Dest.xn0, g)

            def dest_norm1(g, s, q):
                norm_rows(act, XN1D[s], X1D[s], rs1[:, s], nm1[:, s], Dest.nm1, Dest.xn1, g)

            pipelined(act, GROUPS, [(4, dest_mean), (1, dest_root), (6, dest_root1), (9, dest_messages), (8, dest_turned1), (3, dest_turned),
                                    (2, dest_norm), (7, dest_norm1), (4, dest_square)])

            for l in range(LAYERS):
                act.wait_ge(s_stage, 2 + l)

                def conv_relu(g, s, q, l=l):
                    done(act, Conv.add, l * GROUPS + g)
                    act.activation(YN[s], AD[s], ACT.Relu).then_inc(Conv.yn.sem, 1)

                def conv_tables(g, s, q, l=l):
                    n = l * GROUPS + g
                    done(act, Conv.msg, n)
                    if not (isinstance(g, int) and g < U):
                        reached(act, Conv.store[s], (q + l * (GROUPS // U)) * 32)
                    act.activation(MRN[s], bank[1][:, :], ACT.Copy).then_inc(Conv.mr.sem, 1)
                    done(act, Conv.own, n)
                    act.activation(OWN[s], bank[2][:, :], ACT.Identity, bias=conv_bias[:, l + 1:l + 2]).then_inc(Conv.ownr.sem, 1)

                def conv_root(g, s, q):
                    root(sd0[:, s], mv0[:, s], Conv.sd, Conv.mv, g)

                def conv_g(g, s, q):
                    done(act, Conv.nm, g)
                    if not (isinstance(g, int) and g < U):
                        reached(act, Conv.store[s], (q + (LAYERS - 1) * (GROUPS // U)) * 32)
                    for j in range(TPG):
                        last = act.activation(G2[s][:, j * F:(j + 1) * F], X2[s][:, j * F:(j + 1) * F], ACT.Relu,
                                              bias=nm0[:, s, j:j + 1], scale=rs1[:, s, j:j + 1])
                    last.then_inc(Conv.g.sem, 1)

                if l < LAYERS - 1:
                    pipelined(act, GROUPS, [(3, conv_tables), (1, conv_relu)])
                else:
                    pipelined(act, GROUPS, [(4, conv_g), (3, conv_root), (1, conv_relu)])

            act.wait_ge(s_stage, 2 + LAYERS)

            def gcn_turned(g, s, q):
                done(act, Gcn.tg, g)
                freed(act, Gcn.scan, g, U)
                act.activation(GTs[s], bank[0][:, :], ACT.Relu).then_inc(Gcn.gt.sem, 1)

            def gcn_root(g, s, q):
                root(sd1[:, s], mv1[:, s], Gcn.sd, Gcn.mv, g)

            def gcn_norm(g, s, q):
                norm_rows(act, XN3[s], X3[s], rs1[:, s], nm1[:, s], Gcn.nm, Gcn.xn, g)

            def gcn_turned1(g, s, q):
                done(act, Gcn.t1, g)
                act.activation(H3T[s], bank[3][:, :], ACT.Relu).then_inc(Gcn.h1.sem, 1)

            def gcn_nt(g, s, q):
                done(act, Gcn.nt, g)
                if not (isinstance(g, int) and g < U):
                    reached(act, Gcn.store[s], q * 32)
                act.activation(NT3[s], bank[4][:, :], ACT.Copy).then_inc(Gcn.ntr.sem, 1)
                for j in range(TPG):
                    last = act.activation(NTM[s][:, j * F:(j + 1) * F], bank[4][:, j * F:(j + 1) * F], ACT.Identity, scale=lastg[:, s, j:j + 1])
                last.then_inc(Gcn.ntm.sem, 1)

            pipelined(act, GROUPS, [(4, gcn_root), (7, gcn_nt), (6, gcn_turned1), (5, gcn_norm), (0, gcn_turned)])

            act.wait_ge(s_stage, 3 + LAYERS)

            def gat_source(g, s, q):
                done(act, Gat.ts, g)
                freed(act, Gat.num, g, U)
                act.activation(NTS[s], bank[0][:, :], ACT.Identity, bias=gat_b_c[:, :]).then_inc(Gat.nts.sem, 1)

            def gat_dest(g, s, q):
                done(act, Gat.spread, g)
                freed(act, Gat.lkd, g, U)
                act.activation(NTD[s], NDT[s], ACT.Identity, bias=gat_b_c[:, :]).then_inc(Gat.ntd.sem, 1)

            def gat_logits(g, s, q):
                done(act, Gat.lg, g)
                freed(act, Gat.sub, g, U)
                act.activation(LGS[s], wide[:, 0:GW], ACT.Identity, bias=attn_b_c[:, :]).then_inc(Gat.lgs.sem, 1)

            def gat_exp(g, s, q):
                done(act, Gat.sub, g)
                act.activation(PE_[s], PE_[s], ACT.Exp).then_inc(Gat.ep.sem, 1)
                done(act, Gat.drop, g)
                act.activation(CE[s], CE[s], ACT.Exp).then_inc(Gat.ec.sem, 1)

            pipelined(act, GROUPS, [(1, gat_dest), (3, gat_logits), (0, gat_source), (4, gat_exp)])

        @block.tensor
        def _(pe):
            pe.wait_ge(s_const, 8)
            pe.wait_ge(s_rows, 1)
            for n, row in enumerate((rowf[:, 4, :], rowf[:, 5, :], rowf[:, 6, :], near[:, 3, :], rowf[:, 2, :])):
                for b in range(2):
                    last = pe.transpose(bank[n][:, b * RR:(b + 1) * RR], row[:, b * 128:(b + 1) * 128], ident[:RR, :RR])
                last.then_inc(s_rowsT, 1)
            pe.wait_ge(s_cols, 1)
            pe.wait_ge(s_wc, 1)
            for n in range(3):
                pe.transpose(bank[0][:, n * F:(n + 1) * F], wc[:, n, :], ident[:, :])
            for l in range(LAYERS):
                pe.transpose(bank[1][:, l * F:(l + 1) * F], wn[:, 4 + l, :], ident[:, :])
                last = pe.transpose(bank[2][:, l * F:(l + 1) * F], pt[:, l, :], ident[:, :])
            last.then_inc(s_wcT, 1)
            pe.wait_ge(s_wt, 1)

            def node_phases(base, P, sources):
                def turn_x(g, s, q):
                    n = base + g
                    done(pe, Node.xn0, n)
                    freed(pe, Node.h0, n, 1)
                    turn(pe, bank[0], XN0[s], P).then_inc(Node.t0.sem, 1)

                def product_z(g, s, q):
                    n = base + g
                    done(pe, Node.h0, n)
                    z = z_bank(s, sources)
                    if not sources and isinstance(g, int) and g < U:
                        done(pe, Node.w, base - 1)
                        done(pe, Node.nb, GROUPS - 1)
                        done(pe, Node.mr, GROUPS - 1)
                        done(pe, Node.ntr, GROUPS - 1)
                    else:
                        freed(pe, Node.w, n, 1 if sources else U)
                    pe.matmul(z[:P, :], ones3[:, 0:P], bias3[:, 0, :], start=True, stop=False)
                    for j in range(TPG):
                        last = pe.matmul(z[:P, j * F:(j + 1) * F], H0T[s][:, j * 128:j * 128 + P], wT[:, 0, :],
                                         start=False, stop=j == TPG - 1)
                    last.then_inc(Node.z.sem, 1)

                def turn_x1(g, s, q):
                    n = base + g
                    done(pe, Node.xn1, n)
                    freed(pe, Node.h1, n, 1)
                    turn(pe, bank[1], XN1[s], P).then_inc(Node.t1.sem, 1)

                def product_x3(g, s, q):
                    n = base + g
                    done(pe, Node.h1, n)
                    freed(pe, Node.xo, n, 1)
                    pe.matmul(bank[2][:P, :], ones3[:, 0:P], bias3[:, 1, :], start=True, stop=False)
                    for j in range(TPG):
                        last = pe.matmul(bank[2][:P, j * F:(j + 1) * F], H1T[s][:, j * 128:j * 128 + P], gcn_w_s[:, :],
                                         start=False, stop=j == TPG - 1)
                    last.then_inc(Node.x3.sem, 1)

                def turn_sums(g, s, q):
                    done(pe, Node.cnt, g)
                    freed(pe, Node.nb, g, 1)
                    turn(pe, bank[3], SUM1T[s])
                    for j in range(TPG):
                        last = pe.matmul(bank[4][:, j:j + 1], CNT[s][:, j * 128:(j + 1) * 128], ident[:, 0:1], start=True, stop=True)
                    last.then_inc(Node.ts.sem, 1)

                def message(g, s, q):
                    freed(pe, Node.mr, g, 1)
                    for j in range(TPG):
                        last = pe.matmul(wide[:, GW + j * F:GW + (j + 1) * F], H1T[s][:, j * 128:(j + 1) * 128], thetaT[:, 0, :],
                                         start=True, stop=True)
                    last.then_inc(Node.msg.sem, 1)

                def turn_x3(g, s, q):
                    done(pe, Node.xn2, g)
                    freed(pe, Node.ntr, g, 1)
                    turn(pe, bank[5], XN2[s]).then_inc(Node.t2.sem, 1)

                def attention_rows(g, s, q):
                    done(pe, Node.h2, g)
                    for j in range(TPG):
                        last = pe.matmul(bank[5][:, j * F:(j + 1) * F], H2T[s][:, j * 128:(j + 1) * 128], gat_w_s[:, :], start=True, stop=True)
                    last.then_inc(Node.nt.sem, 1)

                if sources:
                    return [(7, turn_x1), (3, turn_x), (12, turn_x3), (7, product_x3), (5, turn_sums), (7, message), (3, product_z),
                            (12, attention_rows)]
                return [(7, turn_x1), (3, turn_x), (7, product_x3), (3, product_z)]

            pipelined(pe, GROUPS, node_phases(0, 128, True))
            pipelined(pe, NODE_GROUPS, node_phases(GROUPS, NP, False))

            pe.wait_ge(s_stage, 1)

            def dest_turn_nb(g, s, q):
                reached(pe, Dest.gather[s], q * 128 + 128)
                freed(pe, Dest.sum2, g, 1)
                turn(pe, bank[0], NBG[s]).then_inc(Dest.tn.sem, 1)

            def dest_turn_x(g, s, q):
                done(pe, Dest.xn0, g)
                freed(pe, Dest.h0, g, 1)
                turn(pe, bank[1], XN0D[s]).then_inc(Dest.t0.sem, 1)

            def dest_products(g, s, q):
                done(pe, Dest.h0, g)
                done(pe, Dest.sum2, g)
                reached(pe, Dest.load[s], q * 32 + 32)
                freed(pe, Dest.zm, g, 1)
                freed(pe, Dest.zs, g, 1)
                pe.matmul(bank[2][:, :], ones3[:, :], bias3[:, 0, :], start=True, stop=False)
                for j in range(TPG):
                    at = slice(j * F, (j + 1) * F)
                    pe.matmul(bank[2][:, at], H0D[s][:, at], wT[:, 0, :], start=False, stop=j == TPG - 1)
                    pe.matmul(bank[3][:, at], S1L[s][:, at], wT[:, 1, :], start=True, stop=False)
                    last = pe.matmul(bank[3][:, at], S2T[s][:, at], wT[:, 2, :], start=False, stop=True)
                last.then_inc(Dest.z.sem, 1)

            def dest_turn_x1(g, s, q):
                done(pe, Dest.xn1, g)
                freed(pe, Dest.h1, g, 1)
                turn(pe, bank[4], XN1D[s]).then_inc(Dest.t1.sem, 1)

            def dest_messages(g, s, q):
                done(pe, Dest.h1, g)
                freed(pe, Dest.mr, g, 1)
                for j in range(TPG):
                    last = pe.matmul(wide[:, GW + j * F:GW + (j + 1) * F], H1D[s][:, j * 128:(j + 1) * 128], thetaT[:, 0, :], start=True, stop=True)
                last.then_inc(Dest.msg.sem, 1)
                freed(pe, Dest.ownr, g, 1)
                pe.matmul(bank[5][:, :], ptT[:, 0, :], H1D[s], start=True, stop=True).then_inc(Dest.own.sem, 1)

            pipelined(pe, GROUPS, [(8, dest_turn_x1), (3, dest_turn_x), (8, dest_messages), (3, dest_products), (0, dest_turn_nb)])

            for l in range(LAYERS):
                pe.wait_ge(s_stage, 2 + l)

                def conv_turn(g, s, q, l=l):
                    n = l * GROUPS + g
                    reached(pe, Conv.gather[s], (q + l * (GROUPS // U)) * 64 + 64)
                    freed(pe, Conv.scan, n, 1)
                    turn(pe, bank[0], MG[s]).then_inc(Conv.tm.sem, 1)

                def conv_messages(g, s, q, l=l):
                    n = l * GROUPS + g
                    done(pe, Conv.yn, n)
                    freed(pe, Conv.mr, n, 1)
                    for j in range(TPG):
                        last = pe.matmul(bank[1][:, j * F:(j + 1) * F], YN[s][:, j * 128:(j + 1) * 128], thetaT[:, l + 1, :], start=True, stop=True)
                    last.then_inc(Conv.msg.sem, 1)
                    freed(pe, Conv.ownr, n, 1)
                    pe.matmul(bank[2][:, :], ptT[:, l + 1, :], YN[s], start=True, stop=True).then_inc(Conv.own.sem, 1)

                def conv_turn_back(g, s, q, l=l):
                    done(pe, Conv.yn, l * GROUPS + g)
                    freed(pe, Conv.x2, g, 1)
                    turn(pe, bank[3], YN[s]).then_inc(Conv.tb.sem, 1)

                pipelined(pe, GROUPS, [(0, conv_turn), (2, conv_messages if l < LAYERS - 1 else conv_turn_back)])

            pe.wait_ge(s_stage, 2 + LAYERS)

            def gcn_turn(g, s, q):
                reached(pe, Gcn.gather[s], q * 64 + 64)
                freed(pe, Gcn.gt, g, 1)
                turn(pe, bank[0], GG[s]).then_inc(Gcn.tg.sem, 1)
                reached(pe, Gcn.load[s], q * 48 + 48)
                freed(pe, Gcn.u, g, 1)
                turn(pe, bank[1], GD[s]).then_inc(Gcn.td.sem, 1)

            def gcn_product(g, s, q):
                done(pe, Gcn.u, g)
                freed(pe, Gcn.x3, g, 1)
                for j in range(TPG):
                    at = slice(j * F, (j + 1) * F)
                    last = pe.matmul(bank[2][:, at], UG[s][:, at], gcn_w_s[:, :], start=True, stop=True)
                last.then_inc(Gcn.w.sem, 1)

            def gcn_turn_x3(g, s, q):
                done(pe, Gcn.xn, g)
                freed(pe, Gcn.h1, g, 1)
                turn(pe, bank[3], XN3[s]).then_inc(Gcn.t1.sem, 1)

            def gcn_attention_rows(g, s, q):
                done(pe, Gcn.h1, g)
                freed(pe, Gcn.ntm, g, 1)
                for j in range(TPG):
                    last = pe.matmul(bank[4][:, j * F:(j + 1) * F], H3T[s][:, j * 128:(j + 1) * 128], gat_w_s[:, :], start=True, stop=True)
                last.then_inc(Gcn.nt.sem, 1)

            pipelined(pe, GROUPS, [(6, gcn_turn_x3), (2, gcn_product), (6, gcn_attention_rows), (0, gcn_turn)])

            pe.wait_ge(s_stage, 3 + LAYERS)

            def gat_turn(g, s, q):
                reached(pe, Gat.load[s], q * 48 + 48)
                freed(pe, Gat.spread, g, 1)
                turn(pe, bank[1], NM[s]).then_inc(Gat.td.sem, 1)
                freed(pe, Gat.xscan, g, 1)
                turn(pe, bank[2], XM[s]).then_inc(Gat.tx.sem, 1)
                reached(pe, Gat.gather[s], q * 64 + 64)
                freed(pe, Gat.nts, g, 1)
                turn(pe, bank[0], NS[s]).then_inc(Gat.ts.sem, 1)

            def gat_logits(g, s, q):
                done(pe, Gat.lks, g)
                done(pe, Gat.lkd, g)
                freed(pe, Gat.lgs, g, 1)
                pe.matmul(wide[:, 0:GW], attn_m[:, 0, :], LKS[s], start=True, stop=False)
                pe.matmul(wide[:, 0:GW], attn_m[:, 1, :], LKD[s], start=False, stop=True).then_inc(Gat.lg.sem, 1)

            def gat_turn_out(g, s, q):
                freed(pe, Gat.oe, g, 1)
                turn(pe, bank[3], X3T[s]).then_inc(Gat.txb.sem, 1)
                done(pe, Gat.den, g)
                for j in range(TPG):
                    last = pe.matmul(bank[4][:, j * HEADS:(j + 1) * HEADS], DEN[s][:, j * 128:(j + 1) * 128], ident[:, ::HC],
                                     start=True, stop=True)
                last.then_inc(Gat.tden.sem, 1)
                done(pe, Gat.num, g)
                turn(pe, bank[5], NUM[s]).then_inc(Gat.tnum.sem, 1)

            pipelined(pe, GROUPS, [(0, gat_turn), (3, gat_logits), (5, gat_turn_out)])


_INS = ["x", "src", "dst", "node_vec", "L0_gnn_W_self", "L0_gnn_W_nb1", "L0_gnn_W_hp", "L0_gnn_W_nb2", "L0_gnn_bias",
        "L0_gnn_branch_logits", "L0_gnn_ln_gamma", "L0_gnn_ln_beta", "L1_gnn_theta_w", "L1_gnn_theta_b",
        "L1_gnn_phi_w", "L1_gnn_phi_b", "L2_gnn_W", "L2_gnn_b", "L3_gnn_W", "L3_gnn_b", "L3_gnn_attn_w", "L3_gnn_attn_b"]


def kernel(**inputs):
    import concourse.bacc as bacc
    from concourse.bass_utils import run_bass_kernel_spmd

    nc = bacc.Bacc("TRN2", target_bir_lowering=False, num_devices=1)
    arrays, args = {}, []
    for name in _INS:
        a = np.ascontiguousarray(inputs[name])
        arrays[f"in_{name}"] = a
        args.append(nc.dram_tensor(f"in_{name}", a.shape, mybir.dt.from_np(a.dtype), kind="ExternalInput").ap())
    out = nc.dram_tensor("out_0", (NODES, F), F32, kind="ExternalOutput").ap()
    build(nc, *args, out)
    return run_bass_kernel_spmd(nc, [arrays], core_ids=[0]).results[0]["out_0"]
```
